# Optimizing a Trainium2 kernel written in Bass

```python
import numpy as np
import jax
import jax.numpy as jnp

def _softmax(x, axis=-1):
    return jax.nn.softmax(x, axis=axis)

def _gelu(x):
    return jax.nn.gelu(x, approximate=True)

def _silu(x):
    return jax.nn.silu(x)

def _sigmoid(x):
    return jax.nn.sigmoid(x)

def _layernorm(x, axis=-1, eps=1e-05):
    m = jnp.mean(x, axis=axis, keepdims=True)
    v = jnp.var(x, axis=axis, keepdims=True)
    return (x - m) / jnp.sqrt(v + eps)

def _scatter_add(tgt, idx, src, axis=0):
    return tgt.at[idx].add(src)

def _segment_sum(src, seg, n):
    return jax.ops.segment_sum(src, seg, n)
kernel_name = 'mk_gnn_resnorm_d4_gnn_r32_04f1ca'

def setup_inputs(seed: int=0):
    np.random.seed(seed)
    _w = jnp.asarray

    def _rec_inputs():
        import jax
        import jax.numpy as jnp
        _gk = jax.random.key(seed)
        x = -0.000202 + 1 * jax.random.normal(jax.random.fold_in(_gk, 1), (3125, 128), jnp.float32)
        _s = jax.random.randint(jax.random.fold_in(_gk, 2), (25000,), 0, 3125, jnp.int32)
        _d = jax.random.randint(jax.random.fold_in(_gk, 3), (25000,), 0, 3125, jnp.int32)
        _loop = jnp.arange(3125, dtype=jnp.int32)
        src = jnp.concatenate([_s, _d, _loop])
        dst = jnp.concatenate([_d, _s, _loop])
        _o = jnp.argsort(dst, stable=True)
        src = src[_o]
        dst = dst[_o]
        edge_attr_3 = -0.000451519 + 1.00018 * jax.random.normal(jax.random.fold_in(_gk, 12), (53125, 3), jnp.float32)
        edge_weight = jax.random.uniform(jax.random.fold_in(_gk, 15), (53125,), jnp.float32, 0.0, 0.999998)
        return (x, src, dst, edge_attr_3, edge_weight)
    x, src, dst, edge_attr_3, edge_weight = _rec_inputs()

    def _L0_gnn_setup():
        import jax, jax.numpy as jnp
        import numpy as np
        N_NODES = 50000
        N_EDGES = 50000
        IN_FEATS = 128
        OUT_FEATS = 128
        key = jax.random.key(seed)
        k_h, k_w, k_b, k_s, k_d = jax.random.split(key, 5)
        h = jax.random.normal(k_h, (N_NODES, IN_FEATS), dtype=jnp.float32)
        W = jax.random.normal(k_w, (OUT_FEATS, 2 * IN_FEATS), dtype=jnp.float32) * 0.05
        b = jax.random.normal(k_b, (OUT_FEATS,), dtype=jnp.float32) * 0.05
        src = jax.random.randint(k_s, (N_EDGES,), 0, N_NODES, dtype=jnp.int32)
        dst = jax.random.randint(k_d, (N_EDGES,), 0, N_NODES, dtype=jnp.int32)
        return {'h': h, 'W': W, 'b': b, 'src': src, 'dst': dst}
    _L0_gnn_all = _L0_gnn_setup()
    _L0_gnn_in = {k: v for k, v in _L0_gnn_all.items() if k in ('W', 'b')}
    del _L0_gnn_all

    def _L1_gnn_setup():
        import jax, jax.numpy as jnp
        import numpy as np
        N = 50000
        E = 25000
        MUL = 32
        NB = 8
        R_MAX = 1.0
        AVG = 16.0
        SQ3 = 3.0 ** 0.5

        def _radial_embedding(r):
            x = jnp.clip(r / R_MAX, 0.0, 1.0)
            centers = jnp.arange(NB, dtype=jnp.float32) / (NB - 1)
            sigma = 1.0 / (NB - 1)
            emb = jnp.exp(-0.5 * ((x[:, None] - centers[None, :]) / sigma) ** 2)
            emb = emb * NB ** 0.5 * (r <= R_MAX).astype(jnp.float32)[:, None]
            return emb
        key = jax.random.key(seed)
        k = jax.random.split(key, 12)
        inp = {'node_feats': jax.random.normal(k[0], (N, 4 * MUL), dtype=jnp.float32), 'edge_vec': jax.random.normal(k[1], (E, 3), dtype=jnp.float32), 'edge_length': jax.random.uniform(k[2], (E,), dtype=jnp.float32), 'senders': jax.random.randint(k[3], (E,), 0, N, dtype=jnp.int32), 'receivers': jax.random.randint(k[4], (E,), 0, N, dtype=jnp.int32), 'num_nodes': N, 'W_up0': jax.random.normal(k[5], (MUL, MUL), dtype=jnp.float32), 'W_up1': jax.random.normal(k[6], (MUL, MUL), dtype=jnp.float32), 'mlp_w0': jax.random.normal(k[7], (NB, 64), dtype=jnp.float32) / NB ** 0.5, 'mlp_b0': jnp.zeros((64,), dtype=jnp.float32), 'mlp_w1': jax.random.normal(k[8], (64, 64), dtype=jnp.float32) / 8.0, 'mlp_b1': jnp.zeros((64,), dtype=jnp.float32), 'mlp_w2': jax.random.normal(k[9], (64, 4 * MUL), dtype=jnp.float32) / 8.0, 'mlp_b2': jnp.zeros((4 * MUL,), dtype=jnp.float32), 'W_out0': jax.random.normal(k[10], (2 * MUL, MUL), dtype=jnp.float32), 'W_out1': jax.random.normal(k[11], (2 * MUL, MUL), dtype=jnp.float32)}
        return inp
    _L1_gnn_all = _L1_gnn_setup()
    _L1_gnn_in = {k: v for k, v in _L1_gnn_all.items() if k in ('W_up0', 'W_up1', 'mlp_w0', 'mlp_b0', 'mlp_w1', 'mlp_b1', 'mlp_w2', 'mlp_b2', 'W_out0', 'W_out1')}
    del _L1_gnn_all

    def _L2_gnn_setup():
        import jax, jax.numpy as jnp
        import numpy as np
        N = 50000
        E = 25000
        IN_C = 128
        HID = 64
        HEADS = 4
        OUT_C = 128
        NEG_SLOPE = 0.2
        EPS = 1e-05

        def _gat(x, W, asrc, adst, b, src, dst):
            n = x.shape[0]
            h = (x @ W).reshape(n, HEADS, HID)
            es = jnp.sum(h * asrc, axis=-1)
            ed = jnp.sum(h * adst, axis=-1)
            e = jax.nn.leaky_relu(es[src] + ed[dst], NEG_SLOPE)
            emax = jax.ops.segment_max(e, dst, num_segments=n)
            ex = jnp.exp(e - emax[dst])
            den = jax.ops.segment_sum(ex, dst, num_segments=n)
            alpha = ex / den[dst]
            msg = h[src] * alpha[:, :, None]
            out = jax.ops.segment_sum(msg, dst, num_segments=n)
            return out.mean(axis=1) + b

        def _ln(x, g, b):
            m = x.mean(-1, keepdims=True)
            v = x.var(-1, keepdims=True)
            return (x - m) / jnp.sqrt(v + EPS) * g + b
        key = jax.random.key(seed)
        ks = jax.random.split(key, 12)
        p = lambda k, shape: jax.random.normal(k, shape, dtype=jnp.float32) * 0.1
        inp = {'x': jax.random.normal(ks[0], (N, IN_C), dtype=jnp.float32), 'edge_index': jax.random.randint(ks[1], (2, E), 0, N, dtype=jnp.int32), 'W1': p(ks[2], (IN_C, HEADS * HID)), 'asrc1': p(ks[3], (HEADS, HID)), 'adst1': p(ks[4], (HEADS, HID)), 'b1': jnp.zeros((HID,), jnp.float32), 'g1': jnp.ones((HID,), jnp.float32), 'be1': jnp.zeros((HID,), jnp.float32), 'W2': p(ks[5], (HID, HEADS * HID)), 'asrc2': p(ks[6], (HEADS, HID)), 'adst2': p(ks[7], (HEADS, HID)), 'b2': jnp.zeros((HID,), jnp.float32), 'g2': jnp.ones((HID,), jnp.float32), 'be2': jnp.zeros((HID,), jnp.float32), 'Wo': p(ks[8], (HID, OUT_C)), 'bo': jnp.zeros((OUT_C,), jnp.float32)}
        return inp
    _L2_gnn_all = _L2_gnn_setup()
    _L2_gnn_in = {k: v for k, v in _L2_gnn_all.items() if k in ('W1', 'asrc1', 'adst1', 'b1', 'g1', 'be1', 'W2', 'asrc2', 'adst2', 'b2', 'g2', 'be2', 'Wo', 'bo')}
    del _L2_gnn_all

    def _L3_gnn_setup():
        import jax, jax.numpy as jnp
        import numpy as np
        N_NODES = 10000
        N_EDGES = 20000
        FEAT_DIM = 128
        AGG_STRENGTH = 0.3
        EPS = 1e-08
        key = jax.random.key(seed)
        k1, k2, k3, k4 = jax.random.split(key, 4)
        features = jax.random.normal(k1, (N_NODES, FEAT_DIM), dtype=jnp.float32)
        edge_weights = jax.random.uniform(k2, (N_EDGES,), dtype=jnp.float32)
        src = jax.random.randint(k3, (N_EDGES,), 0, N_NODES, dtype=jnp.int32)
        tgt = jax.random.randint(k4, (N_EDGES,), 0, N_NODES, dtype=jnp.int32)
        edges = jnp.stack([src, tgt], axis=1)
        return {'features': features, 'edge_weights': edge_weights, 'edges': edges}
    _L3_gnn_all = _L3_gnn_setup()
    _L3_gnn_in = {k: v for k, v in _L3_gnn_all.items() if k in ()}
    del _L3_gnn_all
    return {'x': x, 'src': src, 'dst': dst, 'edge_attr_3': edge_attr_3, 'edge_weight': edge_weight, 'L0_gnn_W': _L0_gnn_in['W'], 'L0_gnn_b': _L0_gnn_in['b'], 'L1_gnn_W_up0': _L1_gnn_in['W_up0'], 'L1_gnn_W_up1': _L1_gnn_in['W_up1'], 'L1_gnn_mlp_w0': _L1_gnn_in['mlp_w0'], 'L1_gnn_mlp_b0': _L1_gnn_in['mlp_b0'], 'L1_gnn_mlp_w1': _L1_gnn_in['mlp_w1'], 'L1_gnn_mlp_b1': _L1_gnn_in['mlp_b1'], 'L1_gnn_mlp_w2': _L1_gnn_in['mlp_w2'], 'L1_gnn_mlp_b2': _L1_gnn_in['mlp_b2'], 'L1_gnn_W_out0': _L1_gnn_in['W_out0'], 'L1_gnn_W_out1': _L1_gnn_in['W_out1'], 'L2_gnn_W1': _L2_gnn_in['W1'], 'L2_gnn_asrc1': _L2_gnn_in['asrc1'], 'L2_gnn_adst1': _L2_gnn_in['adst1'], 'L2_gnn_b1': _L2_gnn_in['b1'], 'L2_gnn_g1': _L2_gnn_in['g1'], 'L2_gnn_be1': _L2_gnn_in['be1'], 'L2_gnn_W2': _L2_gnn_in['W2'], 'L2_gnn_asrc2': _L2_gnn_in['asrc2'], 'L2_gnn_adst2': _L2_gnn_in['adst2'], 'L2_gnn_b2': _L2_gnn_in['b2'], 'L2_gnn_g2': _L2_gnn_in['g2'], 'L2_gnn_be2': _L2_gnn_in['be2'], 'L2_gnn_Wo': _L2_gnn_in['Wo'], 'L2_gnn_bo': _L2_gnn_in['bo']}

def reference(x, src, dst, edge_attr_3, edge_weight, L0_gnn_W, L0_gnn_b, L1_gnn_W_up0, L1_gnn_W_up1, L1_gnn_mlp_w0, L1_gnn_mlp_b0, L1_gnn_mlp_w1, L1_gnn_mlp_b1, L1_gnn_mlp_w2, L1_gnn_mlp_b2, L1_gnn_W_out0, L1_gnn_W_out1, L2_gnn_W1, L2_gnn_asrc1, L2_gnn_adst1, L2_gnn_b1, L2_gnn_g1, L2_gnn_be1, L2_gnn_W2, L2_gnn_asrc2, L2_gnn_adst2, L2_gnn_b2, L2_gnn_g2, L2_gnn_be2, L2_gnn_Wo, L2_gnn_bo):
    import jax
    import jax.numpy as jnp

    def _L0_gnn_ref(h, W, b, src, dst):
        import jax, jax.numpy as jnp
        import numpy as np
        N_NODES = 50000
        N_EDGES = 50000
        IN_FEATS = 128
        OUT_FEATS = 128
        m = jax.ops.segment_sum(h[src], dst, num_segments=h.shape[0])
        hm = jnp.concatenate([h, m], axis=1)
        out = jax.nn.relu(hm @ W.T + b)
        return out

    def _L1_gnn_ref(node_feats, edge_vec, edge_length, senders, receivers, num_nodes, W_up0, W_up1, mlp_w0, mlp_b0, mlp_w1, mlp_b1, mlp_w2, mlp_b2, W_out0, W_out1):
        import jax, jax.numpy as jnp
        import numpy as np
        N = 50000
        E = 25000
        MUL = 32
        NB = 8
        R_MAX = 1.0
        AVG = 16.0
        SQ3 = 3.0 ** 0.5

        def _radial_embedding(r):
            x = jnp.clip(r / R_MAX, 0.0, 1.0)
            centers = jnp.arange(NB, dtype=jnp.float32) / (NB - 1)
            sigma = 1.0 / (NB - 1)
            emb = jnp.exp(-0.5 * ((x[:, None] - centers[None, :]) / sigma) ** 2)
            emb = emb * NB ** 0.5 * (r <= R_MAX).astype(jnp.float32)[:, None]
            return emb
        f32 = jnp.float32
        rhat = edge_vec / (jnp.linalg.norm(edge_vec, axis=-1, keepdims=True) + 1e-12)
        Y1 = SQ3 * rhat
        emb = _radial_embedding(edge_length)
        h = jax.nn.silu(emb @ mlp_w0 + mlp_b0)
        h = jax.nn.silu(h @ mlp_w1 + mlp_b1)
        w = (h @ mlp_w2 + mlp_b2).reshape(-1, 4, MUL)
        s = node_feats[:, :MUL]
        v = node_feats[:, MUL:].reshape(-1, MUL, 3)
        xs = s @ W_up0 / f32(MUL) ** 0.5
        xv = jnp.einsum('nmc,mk->nkc', v, W_up1) / f32(MUL) ** 0.5
        ss = xs[senders]
        vv = xv[senders]
        m0 = w[:, 0] * ss
        m1 = w[:, 1][:, :, None] * ss[:, :, None] * Y1[:, None, :]
        m2 = w[:, 2][:, :, None] * vv
        m3 = w[:, 3] * (jnp.einsum('emc,ec->em', vv, Y1) / SQ3)
        mid_s = jnp.concatenate([m0, m3], axis=1)
        mid_v = jnp.concatenate([m1, m2], axis=1)
        msg_s = jax.ops.segment_sum(mid_s, receivers, num_segments=num_nodes)
        msg_v = jax.ops.segment_sum(mid_v, receivers, num_segments=num_nodes)
        out_s = msg_s @ W_out0 / f32(2 * MUL) ** 0.5
        out_v = jnp.einsum('nmc,mk->nkc', msg_v, W_out1) / f32(2 * MUL) ** 0.5
        out = jnp.concatenate([out_s, out_v.reshape(-1, 3 * MUL)], axis=1)
        return out / max(AVG, 1e-08)

    def _L2_gnn_ref(x, edge_index, W1, asrc1, adst1, b1, g1, be1, W2, asrc2, adst2, b2, g2, be2, Wo, bo):
        import jax, jax.numpy as jnp
        import numpy as np
        N = 50000
        E = 25000
        IN_C = 128
        HID = 64
        HEADS = 4
        OUT_C = 128
        NEG_SLOPE = 0.2
        EPS = 1e-05

        def _gat(x, W, asrc, adst, b, src, dst):
            n = x.shape[0]
            h = (x @ W).reshape(n, HEADS, HID)
            es = jnp.sum(h * asrc, axis=-1)
            ed = jnp.sum(h * adst, axis=-1)
            e = jax.nn.leaky_relu(es[src] + ed[dst], NEG_SLOPE)
            emax = jax.ops.segment_max(e, dst, num_segments=n)
            ex = jnp.exp(e - emax[dst])
            den = jax.ops.segment_sum(ex, dst, num_segments=n)
            alpha = ex / den[dst]
            msg = h[src] * alpha[:, :, None]
            out = jax.ops.segment_sum(msg, dst, num_segments=n)
            return out.mean(axis=1) + b

        def _ln(x, g, b):
            m = x.mean(-1, keepdims=True)
            v = x.var(-1, keepdims=True)
            return (x - m) / jnp.sqrt(v + EPS) * g + b
        n = x.shape[0]
        loop = jnp.arange(n, dtype=edge_index.dtype)
        src = jnp.concatenate([edge_index[0], loop])
        dst = jnp.concatenate([edge_index[1], loop])
        h = jax.nn.relu(_ln(_gat(x, W1, asrc1, adst1, b1, src, dst), g1, be1))
        h = jax.nn.relu(_ln(_gat(h, W2, asrc2, adst2, b2, src, dst), g2, be2))
        return h @ Wo + bo

    def _L3_gnn_ref(features, edge_weights, edges):
        import jax, jax.numpy as jnp
        import numpy as np
        N_NODES = 10000
        N_EDGES = 20000
        FEAT_DIM = 128
        AGG_STRENGTH = 0.3
        EPS = 1e-08
        n_nodes = features.shape[0]
        src = edges[:, 0]
        tgt = edges[:, 1]
        msgs = features[src] * edge_weights[:, None]
        enhanced = jax.ops.segment_sum(msgs, tgt, num_segments=n_nodes)
        counts = jax.ops.segment_sum(edge_weights, tgt, num_segments=n_nodes)
        counts = jnp.maximum(counts, EPS)
        enhanced = enhanced / counts[:, None]
        mask = (counts > EPS).astype(features.dtype)[:, None]
        a = AGG_STRENGTH
        return features * (1.0 - a * mask) + enhanced * (a * mask)
    edge_index = jnp.stack([src, dst])
    edge_index_t = jnp.stack([src, dst], axis=1)
    x = _layernorm(x + _L0_gnn_ref(x, L0_gnn_W, L0_gnn_b, src, dst), axis=-1)
    x = _layernorm(x + _L1_gnn_ref(x, edge_attr_3, edge_weight, src, dst, 3125, L1_gnn_W_up0, L1_gnn_W_up1, L1_gnn_mlp_w0, L1_gnn_mlp_b0, L1_gnn_mlp_w1, L1_gnn_mlp_b1, L1_gnn_mlp_w2, L1_gnn_mlp_b2, L1_gnn_W_out0, L1_gnn_W_out1), axis=-1)
    x = _layernorm(x + _L2_gnn_ref(x, edge_index, L2_gnn_W1, L2_gnn_asrc1, L2_gnn_adst1, L2_gnn_b1, L2_gnn_g1, L2_gnn_be1, L2_gnn_W2, L2_gnn_asrc2, L2_gnn_adst2, L2_gnn_b2, L2_gnn_g2, L2_gnn_be2, L2_gnn_Wo, L2_gnn_bo), axis=-1)
    x = _layernorm(x + _L3_gnn_ref(x, edge_weight, edge_index_t), axis=-1)
    return x

_drawn_inputs = setup_inputs


def setup_inputs(seed=0):
    import zlib

    import numpy as np

    out = dict(_drawn_inputs(seed))
    spreads = {'L1_gnn_mlp_b0': (0.0, 0.8),
     'L1_gnn_mlp_b1': (0.0, 0.558),
     'L1_gnn_mlp_b2': (0.0, 0.363),
     'L2_gnn_b1': (0.0, 0.1),
     'L2_gnn_g1': (1.0, 0.2),
     'L2_gnn_be1': (0.0, 0.1),
     'L2_gnn_b2': (0.0, 0.1),
     'L2_gnn_g2': (1.0, 0.2),
     'L2_gnn_be2': (0.0, 0.1),
     'L2_gnn_bo': (0.0, 0.1)}
    factors = {'L2_gnn_adst2': 3.941}
    for name, (base, spread) in spreads.items():
        noise = np.random.default_rng([zlib.crc32(name.encode()), seed]).standard_normal(out[name].shape)
        drawn = base * np.exp(spread * noise) if base else spread * noise
        out[name] = jnp.asarray(drawn.astype(out[name].dtype))
    for name, factor in factors.items():
        out[name] = (out[name] * factor).astype(out[name].dtype)
    return out
```

```python
import concourse.bass as bass
from concourse import mybir
from contextlib import ExitStack

F32 = mybir.dt.float32
I32 = mybir.dt.int32
ALU = mybir.AluOpType
ACT = mybir.ActivationFunctionType
AX = mybir.AxisListType

N = 3125
E = 53125
D = 128
P = 128
CH = 4
GE = CH * P
NG = -(-E // GE)
LAST = E - (NG - 1) * GE
W = 64
ROUNDS = -(-N // W)
NP = N + W + (-(N + W)) % P
NB = 125
JB = 5
NS = JB * NB
NT = N // NS
HEADS = 4
HID = 64
MUL = 32
NBAS = 8
BIG = 1e30
NOWHERE = float(1 << 20)
LN_EPS = 1e-5
MIN_NORM2 = 1.3e-35
HEAD_OF = [0, 2, 1, 3]


def wait(eng, sem, value):
    if not isinstance(value, int) or value > 0:
        eng.wait_ge(sem, value)


def pipeline(eng, unroll, stages):
    def at(turn, s):
        for lag, step in stages:
            slot, t = (s - lag) % unroll, turn + (s - lag) // unroll
            k = t * unroll + slot
            if not isinstance(k, int) or 0 <= k < NG:
                step(k, slot, t)

    for s in range(unroll):
        at(0, s)
    with eng.Fori(1, NG // unroll) as turn:
        for s in range(unroll):
            at(turn, s)
    for s in range(max(lag for lag, _ in stages)):
        at(NG // unroll, s)


def each(eng, step):
    step(0)
    with eng.Fori(1, NT) as t:
        step(t)


class Chain:

    def __init__(self, eng, sem, start=0):
        self.eng, self.sem, self.start, self.n = eng, sem, start, 0

    def __call__(self, ins):
        self.n += 1
        ins.then_inc(self.sem, 1)
        self.eng.wait_ge(self.sem, self.start + self.n)


class Program:
    def __init__(self, nc, ins, out):
        self.nc, self.i, self.out = nc, ins, out
        self.ctx = ExitStack()

    def sb(self, name, shape, dt=F32, ctx=None):
        return (ctx or self.ctx).enter_context(self.nc.sbuf_tensor(name, shape, dt))

    def ps(self, name, shape, ctx, dt=F32):
        return ctx.enter_context(self.nc.psum_tensor(name, shape, dt))

    def sem(self, name, ctx=None):
        return (ctx or self.ctx).enter_context(self.nc.semaphore(name))

    def dram(self, name, shape, dt=F32):
        return self.nc.dram_tensor(name, shape, dt, kind="Internal").ap()

    def allocate(self):
        sb = self.sb
        self.ident = sb("ident", [P, P])
        self.ones = sb("ones", [P, P])
        self.pick = sb("pick", [HEADS, 2, P])
        self.iota = sb("iota", [P, W])
        self.node_of_row = sb("node_of_row", [P, 1])
        self.iota_now = sb("iota_now", [P, W])
        self.node_now = sb("node_now", [P, 1])
        self.base_first = sb("base_first", [1, NG], I32)
        self.base_now = sb("base_now", [1, NG], I32)
        self.shift = sb("shift", [P, 1])
        self.general = sb("general", [1, 1], I32)
        self.src_t = sb("src_t", [P, NG, CH], I32)
        self.dst_t = sb("dst_t", [P, NG, CH])
        self.w_t = sb("w_t", [P, NG, CH])
        self.dir_t = sb("dir_t", [P, NG, CH, 3])
        self.l0_w = sb("l0_w", [P, 2, D])
        self.l0_b = sb("l0_b", [1, D])
        self.up = sb("up", [P, P])
        self.outw = sb("outw", [P, 2, P])
        self.m_w0 = sb("m_w0", [NBAS, 64])
        self.m_b0 = sb("m_b0", [64, 1])
        self.m_w1 = sb("m_w1", [64, P])
        self.m_b1 = sb("m_b1", [64, 1])
        self.m_w2 = sb("m_w2", [65, 4 * MUL])
        self.g_w = [sb("g_w1", [D, HEADS * HID]), sb("g_w2", [HID, HEADS * HID])]
        self.g_a = [sb("g_a1", [D, 8]), sb("g_a2", [HID, 8])]
        self.g_row = [sb(f"g_row{n}", [P, 3, HID]) for n in (1, 2)]
        self.wo = sb("wo", [HID, D])
        self.bo = sb("bo", [1, D])
        self.acc = sb("acc", [P, HEADS * NP])
        self.den = sb("den", [HEADS, NP])
        self.top = sb("top", [2, 2, NP])
        self.landed = [self.sem(f"rows_landed{n}") for n in range(8)]
        dram = self.dram
        self.dst_d = dram("dst_rows", [NG, GE])
        self.emb_d = dram("emb_rows", [NG, NBAS, GE])
        self.x1_d = dram("x1_rows", [N, D])
        self.up_d = dram("up_rows", [N, D])
        self.t1_d = dram("gat1_rows", [N, D + HEADS])
        self.t2_d = dram("gat2_rows", [N, HID + HEADS])
        self.ed_d = [dram("ed1_rows", [NP, HEADS]), dram("ed2_rows", [NP, HEADS])]
        self.x3_d = dram("x3_rows", [N, D])

    def setup(self):
        nc, i, sb, ps, sem = self.nc, self.i, self.sb, self.ps, self.sem
        with ExitStack() as ctx:
            src_i = sb("src_i", [NG, GE], I32, ctx)
            dst_i = sb("dst_i", [NG, GE], I32, ctx)
            w_r = sb("w_r", [NG, GE], F32, ctx)
            vec_r = sb("vec_r", [NG, GE * 3], F32, ctx)
            src_f = sb("src_f", [NG, GE], F32, ctx)
            dst_f = sb("dst_f", [NG, GE], F32, ctx)
            dst_l = sb("dst_l", [NG, GE], F32, ctx)
            fl_i = sb("fl_i", [1, 2, NG], I32, ctx)
            fl = sb("fl", [1, 2, NG], F32, ctx)
            bad = sb("bad", [NG, GE], F32, ctx)
            bad_n = sb("bad_n", [NG, 1], F32, ctx)
            bad_r = sb("bad_r", [1, 3, NG], F32, ctx)
            bad_s = sb("bad_s", [1, 4], F32, ctx)
            row = sb("row", [1, NG + 1], F32, ctx)
            fcol = sb("fcol", [NG, 1], F32, ctx)
            row_b = sb("row_b", [P, NG + 1], F32, ctx)
            l0_n = sb("l0_n", [P, 2 * D], F32, ctx)
            a_m = sb("a_m", [P, 2, 2, 8], F32, ctx)
            wt = sb("wt", [P, 2, 2, P], F32, ctx)
            m0r = sb("m0r", [NBAS, 64], F32, ctx)
            upr = sb("upr", [P, P], F32, ctx)
            outr = sb("outr", [P, 2, P], F32, ctx)
            zero = sb("zero", [P, HEADS], F32, ctx)
            cleared = sem("cleared", ctx)
            consts = sem("consts", ctx)
            loaded = sem("loaded", ctx)
            with nc.Block() as block:
                @block.vector
                def _(v):
                    v.memset(src_i[:, :], 0).then_inc(cleared, 1)
                    v.memset(dst_i[:, :], int(NOWHERE)).then_inc(cleared, 1)
                    v.memset(w_r[:, :], 0.0).then_inc(cleared, 1)
                    v.memset(vec_r[:, :], 0.0).then_inc(cleared, 1)
                    v.memset(upr[:, :], 0.0).then_inc(cleared, 1)
                    v.memset(outr[:, :, :], 0.0).then_inc(cleared, 1)
                    v.memset(a_m[:, :, :, :], 0.0).then_inc(cleared, 1)
                    v.memset(zero[:, :], 0.0).then_inc(cleared, 1)
                    v.memset(self.ones[:, :], 1.0)
                    v.memset(self.top[:, :, N:], -BIG)
                    v.memset(self.m_w1[:, 64:P], 0.0)

                @block.gpsimd
                def _(g):
                    g.memset(self.ident[:, :], 0.0).then_inc(consts, 1)
                    g.iota(self.iota[:, :], [[1, W]], base=0, channel_multiplier=0,
                           allow_small_or_imprecise_dtypes=True).then_inc(consts, 1)
                    for q in range(P // W):
                        g.wait_ge(consts, 2 + q)
                        g.iota(self.node_of_row[q * W:(q + 1) * W, :], [[0, 1]], base=0, channel_multiplier=1,
                               allow_small_or_imprecise_dtypes=True).then_inc(consts, 1)
                    g.wait_ge(consts, 2 + P // W)
                    g.affine_select(out=self.ident[:, :], in_=self.ident[:, :], compare_op=ALU.not_equal,
                                    fill=1.0, base=0, pattern=[[-1, P]], channel_multiplier=1).then_inc(consts, 1)
                    g.wait_ge(consts, 3 + P // W)
                    g.memset(self.pick[:, :, :], 0.0).then_inc(consts, 1)
                    g.wait_ge(consts, 4 + P // W)
                    g.affine_select(out=self.pick[:, :, :].rearrange("o b (h n) -> o b h n", h=2),
                                    in_=self.pick[:, :, :].rearrange("o b (h n) -> o b h n", h=2),
                                    compare_op=ALU.not_equal, fill=1.0, base=0,
                                    pattern=[[-1, 2], [-2, 2], [0, W]], channel_multiplier=1).then_inc(consts, 1)
                    g.wait_ge(consts, 5 + P // W)

                @block.sync
                def _(s):
                    n = 0

                    def load(dst, src):
                        nonlocal n
                        n += 16
                        with nc.allow_non_contiguous_dma(reason="columns of small weights"):
                            s.dma_start(dst, src).then_inc(loaded, 16)
                    s.wait_ge(cleared, 8)
                    full = (NG - 1) * GE
                    for tile, name, k in ((src_i, "src", 1), (dst_i, "dst", 1), (w_r, "edge_weight", 1)):
                        load(tile[0:NG - 1, :], i[name][0:full].rearrange("(g e) -> g e", e=GE))
                        load(tile[NG - 1:NG, 0:LAST], i[name][full:E].rearrange("(g e) -> g e", g=1))
                    load(vec_r[0:NG - 1, :], i["edge_attr_3"][0:full, :].rearrange("(g e) c -> g (e c)", e=GE))
                    load(vec_r[NG - 1:NG, 0:3 * LAST], i["edge_attr_3"][full:E, :].rearrange("(g e) c -> g (e c)", g=1))
                    firsts = i["dst"][0:full].rearrange("(g e) -> e g", e=GE)
                    load(fl_i[:, 0, 0:NG - 1], firsts[0:1, :])
                    load(fl_i[:, 1, 0:NG - 1], firsts[GE - 1:GE, :])
                    load(fl_i[:, 0, NG - 1:NG], i["dst"][full:full + 1].rearrange("(g e) -> g e", g=1))
                    load(fl_i[:, 1, NG - 1:NG], i["dst"][E - 1:E].rearrange("(g e) -> g e", g=1))
                    load(l0_n[:, :], i["L0_gnn_W"])
                    load(self.l0_b[:, :], i["L0_gnn_b"].rearrange("(a n) -> a n", a=1))
                    load(upr[0:MUL, 0:MUL], i["L1_gnn_W_up0"])
                    for c in range(3):
                        load(upr[MUL + c:P:3, MUL * (1 + c):MUL * (2 + c)], i["L1_gnn_W_up1"])
                    load(outr[0:2 * MUL, 0, 0:MUL], i["L1_gnn_W_out0"])
                    for c, (r, h) in enumerate(((64, 0), (0, 1), (64, 1))):
                        load(outr[r:r + 2 * MUL, h, MUL + c:P:3], i["L1_gnn_W_out1"])
                    load(m0r[:, :], i["L1_gnn_mlp_w0"])
                    load(self.m_b0[:, :], i["L1_gnn_mlp_b0"].rearrange("(n a) -> n a", a=1))
                    load(self.m_w1[:, 0:64], i["L1_gnn_mlp_w1"])
                    load(self.m_b1[:, :], i["L1_gnn_mlp_b1"].rearrange("(n a) -> n a", a=1))
                    load(self.m_w2[0:64, :], i["L1_gnn_mlp_w2"])
                    load(self.m_w2[64:65, :], i["L1_gnn_mlp_b2"].rearrange("(a n) -> a n", a=1))
                    for l, n_ in ((0, "1"), (1, "2")):
                        load(self.g_w[l][:, :], i["L2_gnn_W" + n_])
                        for o, h in enumerate(HEAD_OF):
                            r = HID * (h % 2)
                            for k, name in ((0, "asrc"), (HEADS, "adst")):
                                load(a_m[r:r + HID, l, h // 2, k + o:k + o + 1],
                                     i[f"L2_gnn_{name}{n_}"][h, :].rearrange("(n a) -> n a", a=1))
                        for k, name in enumerate(("b", "g", "be")):
                            load(self.g_row[l][:, k, :],
                                 i[f"L2_gnn_{name}{n_}"].rearrange("(a n) -> a n", a=1).to_broadcast([P, HID]))
                        load(self.ed_d[l][N:NP, :], zero[0:NP - N, :])
                    load(self.wo[:, :], i["L2_gnn_Wo"])
                    load(self.bo[:, :], i["L2_gnn_bo"].rearrange("(a n) -> a n", a=1))
                    s.wait_ge(loaded, n)

            step = sem("setup_step", ctx)
            counted = sem("counted", ctx)
            rowed = sem("rowed", ctx)
            spread = sem("spread", ctx)
            stored = sem("dst_stored", ctx)
            with ExitStack() as pctx:
                p_n = ps("p_n", [1, 1], pctx)
                p_row = ps("p_row", [P, NG + 1], pctx)
                p_col = ps("p_col", [NG, 1], pctx)
                with nc.Block() as block:
                    @block.vector
                    def _(v):
                        then = Chain(v, step)
                        v.tensor_copy(src_f[:, :], src_i[:, :])
                        v.tensor_copy(fl[:, :, :], fl_i[:, :, :]).then_inc(spread, 1)
                        then(v.tensor_copy(dst_f[:, :], dst_i[:, :]))
                        then(v.tensor_tensor(bad[:, 0:GE - 1], dst_f[:, 0:GE - 1], dst_f[:, 1:GE], ALU.is_gt))
                        then(v.tensor_reduce(bad_n[:, :], bad[:, 0:GE - 1], AX.X, ALU.add))
                        then(v.memset(bad_r[:, :, :], 0.0))
                        v.wait_ge(spread, 1)
                        first, last = fl[:, 0, :], fl[:, 1, :]
                        then(v.tensor_tensor(bad_r[:, 0, :], last, first, ALU.subtract))
                        then(v.tensor_scalar(bad_r[:, 0, :], bad_r[:, 0, :], float(W - 1), None, ALU.is_gt))
                        v.tensor_tensor(bad_r[:, 1, 0:NG - 1], last[:, 0:NG - 1], first[:, 1:NG], ALU.is_gt)
                        then(v.tensor_tensor(bad_r[:, 2, 0:NG - 2], last[:, 0:NG - 2], first[:, 2:NG], ALU.is_ge))
                        then(v.tensor_reduce(bad_s[:, 0:1], bad_r[:, :, :], AX.XY, ALU.add))
                        v.wait_ge(counted, 1)
                        then(v.tensor_tensor(bad_s[:, 1:2], bad_s[:, 0:1], p_n[:, :], ALU.add))
                        then(v.tensor_scalar(row[:, NG:NG + 1], bad_s[:, 1:2], 0.0, None, ALU.is_gt))
                        then(v.tensor_copy(self.general[:, :], row[:, NG:NG + 1]))
                        then(v.tensor_scalar(bad_s[:, 2:3], row[:, NG:NG + 1], -1.0, 1.0, ALU.mult, ALU.add))
                        then(v.tensor_scalar(row[:, 0:NG], first, bad_s[:, 2:3], None, ALU.mult))
                        v.tensor_copy(self.base_first[:, :], row[:, 0:NG]).then_inc(rowed, 1)
                        v.wait_ge(counted, 3)
                        v.tensor_copy(row_b[:, :], p_row[:, :])
                        then(v.tensor_copy(fcol[:, :], p_col[:, :]))
                        then(v.tensor_scalar(self.shift[:, :], row_b[:, NG:NG + 1], float(W), None, ALU.mult))
                        v.tensor_scalar(dst_l[:, :], dst_f[:, :], fcol[:, 0:1], None, ALU.subtract).then_inc(spread, 1)

                    @block.tensor
                    def _(t):
                        t.wait_ge(step, 3)
                        nc.tensor.matmul(p_n[:, :], bad_n[:, :], self.ones[0:NG, 0:1], start=True, stop=True).then_inc(counted, 1)
                        t.wait_ge(rowed, 1)
                        nc.tensor.matmul(p_row[:, :], self.ones[0:1, :], row[:, :], start=True, stop=True).then_inc(counted, 1)
                        nc.tensor.matmul(p_col[:, :], row[:, 0:NG], self.ones[0:1, 0:1], start=True, stop=True).then_inc(counted, 1)

                    @block.sync
                    def _(s):
                        s.wait_ge(spread, 2)
                        s.dma_start(self.dst_d, dst_l[:, :]).then_inc(stored, 16)
                        s.wait_ge(stored, 16)

            turned = sem("turned", ctx)
            taken = sem("taken", ctx)
            vstep = sem("dir_step", ctx)
            rooted = sem("rooted", ctx)
            with ExitStack() as pctx:
                p_t = [ps(f"p_t{n}", [P, CH, P], pctx) for n in range(4)]
                nrm = sb("nrm", [P, NG, CH], F32, pctx)
                sqv = sb("sqv", [P, NG, CH, 3], F32, pctx)
                vec_t = sb("vec_t", [P, NG, CH, 3], F32, pctx)
                vec_v = vec_r[:, :].rearrange("g (e c) -> g c e", c=3)
                jobs = [("src", lambda q: src_f[:, q * P:(q + 1) * P]), ("dst", lambda q: dst_f[:, q * P:(q + 1) * P]),
                        ("w", lambda q: w_r[:, q * P:(q + 1) * P])]
                jobs += [(c, lambda q, c=c: vec_v[:, c, q * P:(q + 1) * P]) for c in range(3)]
                with nc.Block() as block:
                    @block.tensor
                    def _(t):
                        for n, (_, part) in enumerate(jobs):
                            wait(t, taken, n - 3)
                            for q in range(CH):
                                last = nc.tensor.transpose(p_t[n % 4][:, q, 0:NG], part(q), self.ident[0:NG, 0:NG])
                            last.then_inc(turned, 1)
                        t.wait_ge(taken, 3)
                        for h in range(2):
                            last = nc.tensor.transpose(p_t[2][:, h, :], l0_n[:, h * P:(h + 1) * P], self.ident[:, :])
                        last.then_inc(turned, 1)
                        t.wait_ge(taken, 4)
                        for h in range(2):
                            nc.tensor.transpose(p_t[3][:, h, :], self.g_w[0][:, h * P:(h + 1) * P], self.ident[:, :])
                            last = nc.tensor.transpose(p_t[3][:, 2 + h, 0:HID], self.g_w[1][:, h * P:(h + 1) * P],
                                                       self.ident[0:HID, 0:HID])
                        last.then_inc(turned, 1)
                        t.wait_ge(taken, 9)
                        for l, k in ((0, D), (1, HID)):
                            for h in range(2):
                                last = nc.tensor.matmul(p_t[l][0:k, 0, 0:8], wt[:, l, h, 0:k], a_m[:, l, h, :],
                                                        start=(h == 0), stop=(h == 1))
                        last.then_inc(turned, 1)

                    @block.vector
                    def _(v):
                        view = [p[:, :, 0:NG].rearrange("p q g -> p g q") for p in p_t]
                        v.wait_ge(turned, 1)
                        v.tensor_copy(self.src_t[:, :, :], view[0]).then_inc(taken, 1)
                        v.wait_ge(turned, 2)
                        v.tensor_tensor(self.dst_t[:, :, :], view[1],
                                        row_b[:, 0:NG].unsqueeze(2).to_broadcast([P, NG, CH]), ALU.subtract).then_inc(taken, 1)
                        v.wait_ge(turned, 3)
                        v.tensor_copy(self.w_t[:, :, :], view[2]).then_inc(taken, 1)
                        for c in range(3):
                            v.wait_ge(turned, 4 + c)
                            v.tensor_copy(vec_t[:, :, :, c], view[(3 + c) % 4]).then_inc(taken, 1)
                        v.wait_ge(turned, 7)
                        v.tensor_copy(self.l0_w[:, :, :], p_t[2][:, 0:2, :]).then_inc(taken, 1)
                        v.wait_ge(turned, 8)
                        v.tensor_copy(wt[:, 0, :, :], p_t[3][:, 0:2, :]).then_inc(taken, 1)
                        v.tensor_copy(wt[:, 1, :, 0:HID], p_t[3][:, 2:4, 0:HID]).then_inc(taken, 1)
                        then = Chain(v, vstep)
                        v.wait_ge(taken, 9)
                        then(v.tensor_tensor(sqv[:, :, :, :], vec_t[:, :, :, :], vec_t[:, :, :, :], ALU.mult))
                        then(v.tensor_reduce(nrm[:, :, :], sqv[:, :, :, :], AX.X, ALU.add))
                        then(v.tensor_scalar(nrm[:, :, :], nrm[:, :, :], MIN_NORM2, None, ALU.max))
                        v.wait_ge(rooted, 1)
                        then(v.tensor_scalar(nrm[:, :, :], nrm[:, :, :], 1e-12, None, ALU.add))
                        then(v.reciprocal(nrm[:, :, :], nrm[:, :, :]))
                        v.tensor_tensor(self.dir_t[:, :, :, :], vec_t[:, :, :, :],
                                        nrm[:, :, :].unsqueeze(3).to_broadcast([P, NG, CH, 3]), ALU.mult)
                        v.wait_ge(turned, 9)
                        v.tensor_copy(self.g_a[0][:, :], p_t[0][:, 0, 0:8])
                        v.tensor_copy(self.g_a[1][:, :], p_t[1][0:HID, 0, 0:8])
                        v.tensor_scalar(self.m_w0[:, :], m0r[:, :], float(NBAS) ** 0.5, None, ALU.mult)
                        v.tensor_scalar(self.up[:, :], upr[:, :], float(MUL) ** -0.5, None, ALU.mult)
                        out_scale = float(2 * MUL) ** -0.5 / 16.0
                        v.tensor_scalar(self.outw[:, :, :], outr[:, :, :], out_scale, None, ALU.mult)

                    @block.scalar
                    def _(a):
                        a.wait_ge(vstep, 3)
                        nc.scalar.activation(nrm[:, :, :], nrm[:, :, :], ACT.Sqrt).then_inc(rooted, 1)

            clipped = sem("clipped", ctx)
            squared = sem("squared", ctx)
            bumped = sem("bumped", ctx)
            masked = sem("masked", ctx)
            emb_out = sem("emb_out", ctx)
            with ExitStack() as pctx:
                w_c = sb("w_c", [NG, GE], F32, pctx)
                centre = sb("centre", [NG, NBAS], F32, pctx)
                emb = sb("emb", [NG, NBAS, GE], F32, pctx)
                with nc.Block() as block:
                    @block.vector
                    def _(v):
                        for k in range(NBAS):
                            v.memset(centre[:, k:k + 1], -float(k))
                        v.tensor_scalar(w_c[:, :], w_r[:, :], 0.0, 1.0, ALU.max, ALU.min).then_inc(clipped, 1)
                        for lo, h in ((64, 0), (0, 1), (64, 1)):
                            v.tensor_scalar(self.outw[lo:lo + MUL, h, :], self.outw[lo:lo + MUL, h, :],
                                            3.0 ** 0.5, None, ALU.mult)
                        for k in range(NBAS):
                            v.wait_ge(bumped, k + 1)
                            v.scalar_tensor_tensor(emb[:, k, :], w_r[:, :], 1.0, emb[:, k, :],
                                                   ALU.is_le, ALU.mult).then_inc(masked, 1)

                    @block.scalar
                    def _(a):
                        a.wait_ge(clipped, 1)
                        for k in range(NBAS):
                            nc.scalar.activation(emb[:, k, :], w_c[:, :], ACT.Square, scale=float(NBAS - 1),
                                                 bias=centre[:, k:k + 1]).then_inc(squared, 1)
                        for k in range(NBAS):
                            a.wait_ge(squared, k + 1)
                            nc.scalar.activation(emb[:, k, :], emb[:, k, :], ACT.Exp, scale=-0.5).then_inc(bumped, 1)

                    @block.sync
                    def _(s):
                        s.wait_ge(masked, NBAS)
                        s.dma_start(self.emb_d, emb[:, :, :]).then_inc(emb_out, 16)
                        s.wait_ge(emb_out, 16)
            self.zero([cleared, consts, loaded, step, counted, rowed, spread, stored, turned, taken, vstep, rooted,
                       clipped, squared, bumped, masked, emb_out])

    def clear(self, name, cells):
        nc = self.nc
        with nc.Block() as block:
            @block.vector
            def _(v):
                v.tensor_copy(self.iota_now[:, :], self.iota[:, :])
                v.tensor_copy(self.node_now[:, :], self.node_of_row[:, :])
                v.tensor_copy(self.base_now[:, :], self.base_first[:, :])
                for ap, value in cells:
                    v.memset(ap, value)

    def advance(self, v, done, n):
        v.wait_ge(done, n)
        v.tensor_scalar(self.iota_now[:, :], self.iota_now[:, :], self.shift[:, 0:1], None, ALU.add)
        v.tensor_scalar(self.node_now[:, :], self.node_now[:, :], self.shift[:, 0:1], None, ALU.add)
        v.tensor_scalar(self.base_now[:, :], self.base_now[:, :], self.shift[0:1, 0:1], None, ALU.add)

    def zero(self, sems):
        nc = self.nc
        ids = sorted(s.num for s in sems)
        while ids:
            n = 1
            while n < len(ids) and ids[n] == ids[0] + n:
                n += 1
            nc.gpsimd.sem_clear(range(ids[0], ids[0] + n))
            ids = ids[n:]
        nc.all_engine_barrier()

    def rounds(self, sems, body):
        with self.nc.Fori(0, self.is_general * (ROUNDS - 1) + 1):
            body()
            self.nc.gpsimd.dma_reset(range(self.landed[0].num, self.landed[-1].num + 1))
            self.zero(sems + self.landed)

    def gather(self, g, slots, table, width, rows, idx, s):
        def step(k, slot, turn):
            wait(g, s["used"], k - slots + 1)
            g.tensor_copy(idx[:, slot, :], self.src_t[:, bass.ds(k, 1), :].rearrange("p a q -> p (a q)")).then_inc(s["idx"], 1)
            g.wait_ge(s["idx"], k + 1)
            g.sem_inc(s["turn"], 1)
            for q in range(CH):
                g.indirect_dma_start(rows[:, slot, q, 0:width], None, table,
                                     bass.IndirectOffsetOnAxis(ap=idx[:, slot, q:q + 1], axis=0)).then_inc(s["rows"][slot], 16)
        return step

    def window(self, v, k):
        return v.value_load(self.base_now[0:1, bass.ds(k, 1)], min_val=0, max_val=NP - W)

    def onehot(self, k):
        a = self.iota_now[:, :].unsqueeze(1).to_broadcast([P, CH, W])
        b = self.dst_t[:, bass.ds(k, 1), :].rearrange("p a q -> p (a q)").unsqueeze(2).to_broadcast([P, CH, W])
        return a, b

    def sum_edges(self, name, table, weighted):
        nc = self.nc
        U = 4
        with ExitStack() as ctx:
            rows = self.sb(name + "rows", [P, U, CH, D], F32, ctx)
            idx = self.sb(name + "idx", [P, U, CH], I32, ctx)
            sel = self.sb(name + "sel", [P, U, CH, W], F32, ctx)
            p_s = [self.ps(f"{name}p{n}", [P, 512], ctx) for n in range(2)]
            s = {k: self.sem(name + k, ctx) for k in ("idx", "turn", "sel0", "sel", "used", "added")}
            landed = self.landed[0:U]
            s["rows"] = landed
            acc = self.acc[:, 0:NP]
            cells = [(acc, 0.0)] + ([(self.den[0:1, :], 0.0)] if weighted else [])
            self.clear(name, cells)

            def body():
                with nc.Block() as block:
                    @block.gpsimd
                    def _(g):
                        pipeline(g, U, [(0, self.gather(g, U, table, D, rows, idx, s))])

                    @block.tensor
                    def _(t):
                        def step(k, slot, turn):
                            t.wait_ge(s["sel"], k + 1)
                            wait(t, s["added"], k - 1)
                            t.wait_ge(landed[slot], (turn + 1) * 16 * CH)
                            p = p_s[slot % 2]
                            for q in range(CH):
                                last = nc.tensor.matmul(p[:, 0:W], rows[:, slot, q, :], sel[:, slot, q, :],
                                                        start=(q == 0), stop=(q == CH - 1))
                            if weighted:
                                for q in range(CH):
                                    last = nc.tensor.matmul(p[0:1, W:2 * W], self.ones[:, 0:1], sel[:, slot, q, :],
                                                            start=(q == 0), stop=(q == CH - 1))
                            last.then_inc(s["used"], 1)
                        pipeline(t, U, [(0, step)])

                    @block.vector
                    def _(v):
                        def select(k, slot, turn):
                            wait(v, s["used"], k - U + 1)
                            a, b = self.onehot(k)
                            if not weighted:
                                v.tensor_tensor(sel[:, slot, :, :], a, b, ALU.is_equal).then_inc(s["sel"], 1)
                                return
                            v.tensor_tensor(sel[:, slot, :, :], a, b, ALU.is_equal).then_inc(s["sel0"], 1)
                            v.wait_ge(s["sel0"], k + 1)
                            w = self.w_t[:, bass.ds(k, 1), :].rearrange("p a q -> p (a q)").unsqueeze(2).to_broadcast([P, CH, W])
                            v.tensor_tensor(sel[:, slot, :, :], sel[:, slot, :, :], w, ALU.mult).then_inc(s["sel"], 1)

                        def add(k, slot, turn):
                            base = self.window(v, k)
                            v.wait_ge(s["used"], k + 1)
                            wait(v, s["added"], k)
                            at = bass.ds(base, W)
                            if weighted:
                                v.tensor_tensor(self.den[0:1, at], self.den[0:1, at], p_s[slot % 2][0:1, W:2 * W], ALU.add)
                            v.tensor_tensor(acc[:, at], acc[:, at], p_s[slot % 2][:, 0:W], ALU.add).then_inc(s["added"], 1)
                        pipeline(v, U, [(0, select), (1, add)])
                        self.advance(v, s["added"], NG)
            self.rounds([x for k, x in s.items() if k != "rows"], body)

    def product_edges(self):
        nc = self.nc
        U = 8
        with ExitStack() as ctx:
            sb, ps, sem = self.sb, self.ps, self.sem
            rows = sb("tp_rows", [P, U, CH, D], F32, ctx)
            idx = sb("tp_idx", [P, U, CH], I32, ctx)
            sel = sb("tp_sel", [P, U, CH, W], F32, ctx)
            emb = sb("tp_emb", [NBAS, U, GE], F32, ctx)
            h0 = sb("tp_h0", [64, 2, GE], F32, ctx)
            h1 = sb("tp_h1", [65, 2, GE], F32, ctx)
            msg = sb("tp_msg", [P, 2, CH, 2 * P], F32, ctx)
            u = sb("tp_u", [P, 2, CH, MUL], F32, ctx)
            vy = sb("tp_vy", [P, 2, CH, 3, MUL], F32, ctx)
            dot = sb("tp_dot", [P, 2, CH, MUL], F32, ctx)
            p_h0 = ps("tp_p0", [64, GE], ctx)
            p_h1 = ps("tp_p1", [P, GE], ctx)
            p_w = [ps(f"tp_pw{n}", [P, CH, 4 * MUL], ctx) for n in range(2)]
            p_s = [ps(f"tp_ps{n}", [P, 512], ctx) for n in range(2)]
            names = ("idx", "turn", "hid0", "hid1", "act0", "act1", "coef", "sel", "parts", "msgs", "used", "added", "summed")
            s = {k: sem("tp_" + k, ctx) for k in names}
            landed = self.landed[0:U]
            emb_in = [sem(f"tp_emb{n}", ctx) for n in range(U)]
            s["rows"] = landed
            acc = self.acc[:, 0:2 * NP].rearrange("p (h n) -> p h n", h=2)
            self.clear("tp", [(acc, 0.0), (h1[64:65, :, :], 1.0)])

            def body():
                with nc.Block() as block:
                    @block.gpsimd
                    def _(g):
                        g_s = dict(s, used=s["msgs"])
                        pipeline(g, U, [(0, self.gather(g, U, self.up_d, D, rows, idx, g_s))])

                    @block.sync
                    def _(e):
                        def load(k, slot, turn):
                            wait(e, s["hid0"], k - U + 1)
                            e.dma_start(emb[:, slot, :], self.emb_d[bass.ds(k, 1), :, :].rearrange("a b e -> (a b) e"))\
                                .then_inc(emb_in[slot], 16)
                        pipeline(e, U, [(0, load)])

                    @block.tensor
                    def _(t):
                        def hidden0(k, slot, turn):
                            t.wait_ge(emb_in[slot], (turn + 1) * 16)
                            wait(t, s["act0"], k)
                            nc.tensor.matmul(p_h0[:, :], self.m_w0[:, :], emb[:, slot, :], start=True, stop=True).then_inc(s["hid0"], 1)

                        def hidden1(k, slot, turn):
                            t.wait_ge(s["act0"], k + 1)
                            wait(t, s["act1"], k)
                            nc.tensor.matmul(p_h1[:, :], self.m_w1[:, :], h0[:, slot % 2, :], start=True, stop=True).then_inc(s["hid1"], 1)

                        def coefs(k, slot, turn):
                            t.wait_ge(s["act1"], k + 1)
                            wait(t, s["msgs"], k - 1)
                            for q in range(CH):
                                last = nc.tensor.matmul(p_w[slot % 2][:, q, :], h1[:, slot % 2, q * P:(q + 1) * P],
                                                        self.m_w2[:, :], start=True, stop=True)
                            last.then_inc(s["coef"], 1)

                        def total(k, slot, turn):
                            t.wait_ge(s["msgs"], k + 1)
                            wait(t, s["added"], k - 1)
                            for h in range(2):
                                for q in range(CH):
                                    last = nc.tensor.matmul(p_s[slot % 2][:, h * W:(h + 1) * W],
                                                            msg[:, slot % 2, q, h * P:(h + 1) * P], sel[:, slot, q, :],
                                                            start=(q == 0), stop=(q == CH - 1))
                            last.then_inc(s["summed"], 1)
                        pipeline(t, U, [(0, hidden0), (1, hidden1), (2, coefs), (3, total)])

                    @block.scalar
                    def _(a):
                        def silu0(k, slot, turn):
                            a.wait_ge(s["hid0"], k + 1)
                            wait(a, s["hid1"], k - 1)
                            nc.scalar.activation(h0[:, slot % 2, :], p_h0[:, :], ACT.Silu, bias=self.m_b0[:, 0:1]).then_inc(s["act0"], 1)

                        def silu1(k, slot, turn):
                            a.wait_ge(s["hid1"], k + 1)
                            wait(a, s["coef"], k - 1)
                            nc.scalar.activation(h1[0:64, slot % 2, :], p_h1[0:64, :], ACT.Silu, bias=self.m_b1[:, 0:1]).then_inc(s["act1"], 1)
                        pipeline(a, U, [(0, silu0), (1, silu1)])

                    @block.vector
                    def _(v):
                        def select(k, slot, turn):
                            wait(v, s["summed"], k - U + 1)
                            a, b = self.onehot(k)
                            v.tensor_tensor(sel[:, slot, :, :], a, b, ALU.is_equal).then_inc(s["sel"], 1)

                        def messages(k, slot, turn):
                            h = slot % 2
                            v.wait_ge(landed[slot], (turn + 1) * 16 * CH)
                            v.wait_ge(s["coef"], k + 1)
                            wait(v, s["summed"], k - 1)
                            v.wait_ge(s["sel"], k + 1)
                            p = p_w[h]
                            ss, vv = rows[:, slot, :, 0:MUL], rows[:, slot, :, MUL:].rearrange("p q (c m) -> p q c m", c=3)
                            y = self.dir_t[:, bass.ds(k, 1), :, :].rearrange("p a q c -> p (a q) c").unsqueeze(3)\
                                .to_broadcast([P, CH, 3, MUL])
                            v.tensor_tensor(msg[:, h, :, 0:MUL], p[:, :, 0:MUL], ss, ALU.mult)
                            v.tensor_tensor(u[:, h, :, :], p[:, :, MUL:2 * MUL], ss, ALU.mult).then_inc(s["parts"], 1)
                            v.tensor_tensor(vy[:, h, :, :, :], vv, y, ALU.mult).then_inc(s["parts"], 1)
                            cols = {0: 3 * MUL, 1: 5 * MUL, 2: 7 * MUL}
                            for c in range(3):
                                v.tensor_tensor(msg[:, h, :, cols[c]:cols[c] + MUL], p[:, :, 2 * MUL:3 * MUL],
                                                vv[:, :, c, :], ALU.mult)
                            v.wait_ge(s["parts"], 4 * k + 2)
                            v.tensor_tensor(dot[:, h, :, :], vy[:, h, :, 0, :], vy[:, h, :, 1, :], ALU.add).then_inc(s["parts"], 1)
                            for c in range(3):
                                v.tensor_tensor(msg[:, h, :, cols[c] - MUL:cols[c]], u[:, h, :, :], y[:, :, c, :], ALU.mult)
                            v.wait_ge(s["parts"], 4 * k + 3)
                            v.tensor_tensor(dot[:, h, :, :], dot[:, h, :, :], vy[:, h, :, 2, :], ALU.add).then_inc(s["parts"], 1)
                            v.wait_ge(s["parts"], 4 * k + 4)
                            v.tensor_tensor(msg[:, h, :, MUL:2 * MUL], p[:, :, 3 * MUL:4 * MUL], dot[:, h, :, :], ALU.mult).then_inc(s["msgs"], 1)

                        def add(k, slot, turn):
                            base = self.window(v, k)
                            v.wait_ge(s["summed"], k + 1)
                            wait(v, s["added"], k)
                            at = bass.ds(base, W)
                            v.tensor_tensor(acc[:, :, at], acc[:, :, at],
                                            p_s[slot % 2][:, 0:2 * W].rearrange("p (h n) -> p h n", h=2), ALU.add).then_inc(s["added"], 1)
                        pipeline(v, U, [(0, select), (0, messages), (1, add)])
                        self.advance(v, s["added"], NG)
            self.rounds([x for k, x in s.items() if k != "rows"] + emb_in, body)

    def attend_edges(self, l, table, dim):
        nc = self.nc
        U = 8
        width = dim + HEADS
        with ExitStack() as ctx:
            sb, ps, sem = self.sb, self.ps, self.sem
            n = f"at{l}_"
            rows = sb(n + "rows", [P, U, CH, width], F32, ctx)
            idx = sb(n + "idx", [P, U, CH], I32, ctx)
            dst_b = sb(n + "dst_b", [P, 4, GE], F32, ctx)
            ed_w = sb(n + "ed_w", [W, 4, HEADS], F32, ctx)
            hot_t = sb(n + "hot_t", [P, U, GE], F32, ctx)
            mask = sb(n + "mask", [P, 2, GE], F32, ctx)
            cand = sb(n + "cand", [P, 2, GE], F32, ctx)
            best = sb(n + "best", [P, 2, 2], F32, ctx)
            top_w = sb(n + "top_w", [2, 2, 2, W], F32, ctx)
            node_w = sb(n + "node_w", [W, 2, 8], F32, ctx)
            look = sb(n + "look", [P, 2, CH, 8], F32, ctx)
            zz = sb(n + "zz", [P, 2, 2, CH, HEADS], F32, ctx)
            zl = sb(n + "zl", [P, 2, 2, CH, HEADS], F32, ctx)
            dz = sb(n + "dz", [P, 2, CH, HEADS], F32, ctx)
            prob = sb(n + "prob", [P, 2, CH, HEADS], F32, ctx)
            sel = sb(n + "sel", [P, 2, CH, W], F32, ctx)
            psel = sb(n + "psel", [P, 2, CH, HEADS, W], F32, ctx)
            p_b = [ps(f"{n}pb{b}", [P, GE], ctx) for b in range(2)]
            p_e = ps(n + "pe", [HEADS, GE], ctx)
            esr = sb(n + "esr", [HEADS, 2, GE], F32, ctx)
            p_m = ps(n + "pm", [2, P], ctx)
            p_l = ps(n + "pl", [P, CH, 8], ctx)
            p_s = [ps(f"{n}ps{a}", [P, 512], ctx) for a in range(2)]
            turned_best = p_m[:, :]
            p_w = ps(n + "pw", [W, 4], ctx)
            names = ("idx", "turn", "spread", "hot", "mask", "cand", "best", "bestt", "merged", "topw", "topt",
                     "nodew", "looked", "look", "z", "dz", "prob", "sel", "psel_v", "psel_a", "used", "added", "est", "esr", "go_v", "go_t")
            s = {k: sem(n + k, ctx) for k in names}
            landed = self.landed[0:U]
            dst_in = [sem(f"{n}dst{a}", ctx) for a in range(4)]
            ed_in = [sem(f"{n}ed{a}", ctx) for a in range(4)]
            s["rows"] = landed
            acc = self.acc[:, :].rearrange("p (h n) -> p h n", h=HEADS)
            VQ = 2

            def body():
                with nc.Block() as block:
                    @block.gpsimd
                    def _(g):
                        pipeline(g, U, [(0, self.gather(g, U, table, width, rows, idx, s))])

                    @block.sync
                    def _(e):
                        def load(k, slot, turn):
                            b = slot % 4
                            wait(e, s["hot"], k - 3)
                            wait(e, s["nodew"], k - 3)
                            e.dma_start(dst_b[:, b, :], self.dst_d[bass.ds(k, 1), :].to_broadcast([P, GE])).then_inc(dst_in[b], 16)
                            base = e.value_load(self.base_now[0:1, bass.ds(k, 1)], min_val=0, max_val=NP - W)
                            e.dma_start(ed_w[:, b, :], self.ed_d[l][bass.ds(base, W), :]).then_inc(ed_in[b], 16)
                        pipeline(e, U, [(0, load)])

                    @block.tensor
                    def _(t):
                        def turn_es(k, slot, turn):
                            t.wait_ge(landed[slot], (turn + 1) * 16 * CH)
                            wait(t, s["esr"], k)
                            for q in range(CH):
                                last = nc.tensor.transpose(p_e[:, q * P:(q + 1) * P], rows[:, slot, q, dim:dim + HEADS], self.ident[:, :])
                            last.then_inc(s["est"], 1)

                        def spread(k, slot, turn):
                            t.wait_ge(s["esr"], k + 1)
                            wait(t, s["best"], k)
                            for b in range(2):
                                last = nc.tensor.matmul(p_b[b][:, :], self.pick[:, b, :], esr[:, slot % 2, :], start=True, stop=True)
                            last.then_inc(s["spread"], 1)

                        def turn_best(k, slot, turn):
                            t.wait_ge(s["best"], k + 1)
                            wait(t, s["merged"], k)
                            nc.tensor.transpose(turned_best, best[:, slot % 2, :], self.ident[:, :]).then_inc(s["bestt"], 1)

                        def turn_top(k, slot, turn):
                            t.wait_ge(s["topw"], k + 1)
                            wait(t, s["nodew"], k)
                            t.sem_inc(s["go_t"], 1)
                            for h in range(2):
                                last = nc.tensor.transpose(p_w[:, 2 * h:2 * h + 2], top_w[:, slot % 2, h, :], self.ident[0:2, 0:2])
                            last.then_inc(s["topt"], 1)

                        def lookup(k, slot, turn):
                            t.wait_ge(s["nodew"], k + 1)
                            wait(t, s["look"], k)
                            for q in range(CH):
                                last = nc.tensor.matmul(p_l[:, q, :], hot_t[0:W, slot, q * P:(q + 1) * P],
                                                        node_w[:, slot % 2, :], start=True, stop=True)
                            last.then_inc(s["looked"], 1)

                        def total(k, slot, turn):
                            t.wait_ge(s["psel_v"], k + 1)
                            t.wait_ge(s["psel_a"], k + 1)
                            wait(t, s["added"], k - 1)
                            p = p_s[slot % 2]
                            for q in range(CH):
                                nc.tensor.matmul(p[0:dim, 0:HEADS * W], rows[:, slot, q, 0:dim],
                                                 psel[:, slot % 2, q, :, :].rearrange("p h n -> p (h n)"),
                                                 start=(q == 0), stop=(q == CH - 1))
                            for q in range(CH):
                                last = nc.tensor.matmul(p[0:HEADS, HEADS * W:(HEADS + 1) * W], prob[:, slot % 2, q, :],
                                                        sel[:, slot % 2, q, :], start=(q == 0), stop=(q == CH - 1))
                            last.then_inc(s["used"], 1)
                        pipeline(t, U, [(0, turn_es), (1, spread), (2, turn_best), (3, turn_top), (4, lookup), (5, total)])

                    @block.scalar
                    def _(a):
                        def es_rows(k, slot, turn):
                            a.wait_ge(s["est"], k + 1)
                            wait(a, s["spread"], k - 1)
                            nc.scalar.activation(esr[:, slot % 2, :], p_e[:, :], ACT.Copy).then_inc(s["esr"], 1)

                        def masks(k, slot, turn):
                            a.wait_ge(s["hot"], k + 1)
                            wait(a, s["best"], k - 1)
                            nc.scalar.activation(mask[:, slot % 2, :], hot_t[:, slot, :], ACT.Copy,
                                                 scale=BIG, bias=-BIG).then_inc(s["mask"], 1)

                        def node_window(k, slot, turn):
                            b = slot % 4
                            a.wait_ge(ed_in[b], (2 * turn + slot // 4 + 1) * 16)
                            wait(a, s["looked"], k - 1)
                            nc.scalar.activation(node_w[:, slot % 2, 4:8], ed_w[:, b, :], ACT.Copy)
                            a.wait_ge(s["topt"], k + 1)
                            nc.scalar.activation(node_w[:, slot % 2, 0:4], p_w[:, :], ACT.Copy).then_inc(s["nodew"], 1)

                        def per_edge(k, slot, turn):
                            a.wait_ge(s["looked"], k + 1)
                            wait(a, s["dz"], k - 1)
                            nc.scalar.activation(look[:, slot % 2, :, :], p_l[:, :, :], ACT.Copy).then_inc(s["look"], 1)

                        def weigh(k, slot, turn):
                            a.wait_ge(s["dz"], k + 1)
                            wait(a, s["used"], k - 1)
                            nc.scalar.activation(prob[:, slot % 2, :, :], dz[:, slot % 2, :, :], ACT.Exp).then_inc(s["prob"], 1)
                            a.wait_ge(s["prob"], k + 1)
                            a.wait_ge(s["sel"], k + 1)
                            for q in range(VQ, CH):
                                for o in range(HEADS):
                                    last = nc.scalar.activation(psel[:, slot % 2, q, o, :], sel[:, slot % 2, q, :], ACT.Copy,
                                                                scale=prob[:, slot % 2, q, o:o + 1])
                            last.then_inc(s["psel_a"], 1)
                        pipeline(a, U, [(0, es_rows), (0, masks), (3, node_window), (4, per_edge), (4, weigh)])

                    @block.vector
                    def _(v):
                        def hot(k, slot, turn):
                            b = slot % 4
                            v.wait_ge(dst_in[b], (2 * turn + slot // 4 + 1) * 16)
                            wait(v, s["looked"], k - U + 1)
                            wait(v, s["mask"], k - U + 1)
                            v.tensor_scalar(hot_t[:, slot, :], dst_b[:, b, :], self.node_now[:, 0:1], None, ALU.is_equal).then_inc(s["hot"], 1)

                        def largest(k, slot, turn):
                            v.wait_ge(s["mask"], k + 1)
                            v.wait_ge(s["spread"], k + 1)
                            wait(v, s["bestt"], k - 1)
                            wait(v, s["cand"], 2 * k)
                            v.sem_inc(s["go_v"], 1)
                            for b in range(2):
                                ins = v.tensor_tensor_reduce(out=cand[:, b, :], in0=p_b[b][:, :], in1=mask[:, slot % 2, :],
                                                             scale=1.0, scalar=-BIG, op0=ALU.add, op1=ALU.max,
                                                             accum_out=best[:, slot % 2, b:b + 1])
                                ins.then_inc(s["cand"], 1)
                            v.wait_ge(s["cand"], 2 * k + 2)
                            v.sem_inc(s["best"], 1)

                        def merge(k, slot, turn):
                            base = self.window(v, k)
                            v.wait_ge(s["bestt"], k + 1)
                            wait(v, s["merged"], k)
                            at = bass.ds(base, W)
                            v.tensor_tensor(self.top[:, :, at], self.top[:, :, at],
                                            turned_best.rearrange("b (h n) -> b h n", h=2), ALU.max).then_inc(s["merged"], 1)

                        def take_top(k, slot, turn):
                            base = self.window(v, k)
                            if isinstance(k, int) and k == NG - 1:
                                v.wait_ge(s["merged"], NG)
                            else:
                                v.wait_ge(s["merged"], k + 2)
                            wait(v, s["topt"], k - 1)
                            v.tensor_copy(top_w[:, slot % 2, :, :], self.top[:, :, bass.ds(base, W)]).then_inc(s["topw"], 1)

                        def scores(k, slot, turn):
                            h = slot % 2
                            v.wait_ge(s["look"], k + 1)
                            wait(v, s["dz"], k)
                            ed = look[:, h, :, 4:8]
                            v.tensor_tensor(zz[:, h, 0, :, :], ed, rows[:, slot, :, dim:dim + HEADS], ALU.add)
                            v.tensor_tensor(zz[:, h, 1, :, :], ed, look[:, h, :, 0:4], ALU.add).then_inc(s["z"], 1)
                            v.wait_ge(s["z"], 3 * k + 1)
                            v.scalar_tensor_tensor(zl[:, h, :, :, :].rearrange("p a q o -> p (a q o)"),
                                                   zz[:, h, :, :, :].rearrange("p a q o -> p (a q o)"), 0.2,
                                                   zz[:, h, :, :, :].rearrange("p a q o -> p (a q o)"),
                                                   ALU.mult, ALU.max).then_inc(s["z"], 1)
                            v.wait_ge(s["z"], 3 * k + 2)
                            v.tensor_tensor(zz[:, h, 0, :, :], zl[:, h, 0, :, :], zl[:, h, 1, :, :], ALU.min).then_inc(s["z"], 1)
                            v.wait_ge(s["z"], 3 * k + 3)
                            wait(v, s["prob"], k - 1)
                            v.tensor_tensor(dz[:, h, :, :], zz[:, h, 0, :, :], zl[:, h, 1, :, :], ALU.subtract).then_inc(s["dz"], 1)

                        def select(k, slot, turn):
                            wait(v, s["used"], k - 1)
                            a, b = self.onehot(k)
                            v.tensor_tensor(sel[:, slot % 2, :, :], a, b, ALU.is_equal).then_inc(s["sel"], 1)

                        def weigh(k, slot, turn):
                            h = slot % 2
                            v.wait_ge(s["prob"], k + 1)
                            v.wait_ge(s["sel"], k + 1)
                            for q in range(VQ):
                                last = v.tensor_tensor(psel[:, h, q, :, :], sel[:, h, q, :].unsqueeze(1).to_broadcast([P, HEADS, W]),
                                                       prob[:, h, q, :].unsqueeze(2).to_broadcast([P, HEADS, W]), ALU.mult)
                            last.then_inc(s["psel_v"], 1)

                        def add(k, slot, turn):
                            base = self.window(v, k)
                            v.wait_ge(s["used"], k + 1)
                            wait(v, s["added"], k)
                            at = bass.ds(base, W)
                            p = p_s[slot % 2]
                            v.tensor_tensor(self.den[:, at], self.den[:, at], p[0:HEADS, HEADS * W:(HEADS + 1) * W], ALU.add)
                            v.tensor_tensor(acc[0:dim, :, at], acc[0:dim, :, at],
                                            p[0:dim, 0:HEADS * W].rearrange("p (h n) -> p h n", h=HEADS), ALU.add).then_inc(s["added"], 1)
                        pipeline(v, U, [(0, hot), (1, largest), (2, merge), (3, take_top), (4, select), (4, scores), (4, weigh),
                                        (5, add)])
                        self.advance(v, s["added"], NG)
            with nc.Fori(0, self.is_general + 1):
                self.clear(n, [(self.acc[0:dim, :], 0.0), (self.den[:, :], 0.0)])
                self.rounds([x for k, x in s.items() if k != "rows"] + dst_in + ed_in, body)

    def norm(self, v, a_sem, then, x, width, tmp, st, root):
        nb = x.shape[0]
        full = [nb, JB, width]
        then(v.tensor_reduce(st[0:nb, 0, :], x, AX.X, ALU.add))
        then(v.tensor_scalar(st[0:nb, 0, :], st[0:nb, 0, :], 1.0 / width, None, ALU.mult))
        then(v.tensor_tensor(x, x, st[0:nb, 0, :].unsqueeze(2).to_broadcast(full), ALU.subtract))
        then(v.tensor_tensor(tmp, x, x, ALU.mult))
        then(v.tensor_reduce(st[0:nb, 1, :], tmp, AX.X, ALU.add))
        v.tensor_scalar(st[0:nb, 1, :], st[0:nb, 1, :], 1.0 / width, LN_EPS, ALU.mult, ALU.add).then_inc(a_sem, 1)
        root()
        then(v.reciprocal(st[0:nb, 1, :], st[0:nb, 1, :]))
        then(v.tensor_tensor(x, x, st[0:nb, 1, :].unsqueeze(2).to_broadcast(full), ALU.mult))

    def node_rows(self, dram, t, width):
        return dram.rearrange("(t j p) f -> t p j f", j=JB, p=NB)[bass.ds(t, 1), :, :, :].rearrange("a p j f -> (a p) j f")

    def node_layer(self, n, kind, x_in):
        nc = self.nc
        with ExitStack() as ctx:
            sb, ps, sem = self.sb, self.ps, self.sem
            xs = sb(n + "xs", [NB, JB, D], F32, ctx)
            y = sb(n + "y", [NB, JB, D], F32, ctx)
            tmp = sb(n + "tmp", [NB, JB, D], F32, ctx)
            st = sb(n + "st", [P, 2, JB], F32, ctx)
            parts = 2 if kind == "product" else 1
            sums = sb(n + "sums", [P, parts, NS], F32, ctx)
            xt = sb(n + "xt", [P, JB, P], F32, ctx)
            tab = sb(n + "tab", [NB, JB, D + HEADS], F32, ctx)
            edt = sb(n + "edt", [NB, JB, HEADS], F32, ctx)
            p_x = ps(n + "px", [P, 8, P], ctx)
            p_y = ps(n + "py", [P, 8, P], ctx)
            p_z = ps(n + "pz", [P, 8, P], ctx)
            names = ("xin", "sumd", "turned", "xt", "lin", "var", "rooted", "step", "turned2", "xt2", "tabbed",
                     "tabd", "sent")
            s = {k: sem(n + k, ctx) for k in names}
            SENT = 2 if kind == "sum" else 3
            LINKS = 8
            with nc.Block() as block:
                @block.sync
                def _(e):
                    def step(t):
                        wait(e, s["sent"], t * (16 * SENT))
                        e.dma_start(xs[:, :, :], self.node_rows(x_in, t, D)).then_inc(s["xin"], 16)
                        e.wait_ge(s["step"], (t + 1) * LINKS)
                        if kind == "sum":
                            e.dma_start(self.node_rows(self.x1_d, t, D), y[:, :, :]).then_inc(s["sent"], 16)
                            e.wait_ge(s["tabd"], t + 1)
                            e.dma_start(self.node_rows(self.up_d, t, D), tab[:, :, 0:D]).then_inc(s["sent"], 16)
                        else:
                            e.dma_start(self.node_rows(self.x2_d, t, D), y[:, :, :]).then_inc(s["sent"], 16)
                            e.wait_ge(s["tabd"], t + 1)
                            e.dma_start(self.node_rows(self.t1_d, t, D + HEADS), tab[:, :, :]).then_inc(s["sent"], 16)
                            e.dma_start(self.node_rows(self.ed_d[0][0:N, :], t, HEADS), edt[:, :, :]).then_inc(s["sent"], 16)
                    each(e, step)
                    e.wait_ge(s["sent"], NT * 16 * SENT)

                @block.scalar
                def _(a):
                    def step(t):
                        wait(a, s["sent"], t * (16 * SENT))
                        nc.scalar.activation(sums[:, :, :], self.acc[:, 0:parts * NP].rearrange("p (h n) -> p h n", h=parts)
                                             [:, :, bass.ds(t * NS, NS)], ACT.Copy).then_inc(s["sumd"], 1)
                        if kind == "sum":
                            a.wait_ge(s["turned"], t + 1)
                            nc.scalar.activation(xt[:, :, 0:NB], p_x[:, 0:JB, 0:NB], ACT.Copy).then_inc(s["xt"], 1)
                        a.wait_ge(s["var"], t + 1)
                        nc.scalar.activation(st[0:NB, 1, :], st[0:NB, 1, :], ACT.Sqrt).then_inc(s["rooted"], 1)
                        a.wait_ge(s["turned2"], t + 1)
                        nc.scalar.activation(xt[:, :, 0:NB], p_z[:, 0:JB, 0:NB], ACT.Copy).then_inc(s["xt2"], 1)
                        a.wait_ge(s["tabbed"], t + 1)
                        if kind == "sum":
                            nc.scalar.activation(tab[:, :, 0:D], p_x[0:NB, 0:JB, :], ACT.Copy).then_inc(s["tabd"], 1)
                        else:
                            nc.scalar.activation(tab[:, :, 0:D], y[:, :, :], ACT.Copy)
                            nc.scalar.activation(tab[:, :, D:D + HEADS], p_x[0:NB, 0:JB, 0:HEADS], ACT.Copy)
                            for hh, p in enumerate((p_y, p_z)):
                                nc.scalar.activation(self.top[:, hh, bass.ds(t * NS, NS)].rearrange("b (j p) -> b j p", j=JB),
                                                     p[0:2, 0:JB, 0:NB], ACT.Copy)
                            nc.scalar.activation(edt[:, :, :], p_x[0:NB, 0:JB, HEADS:2 * HEADS], ACT.Copy).then_inc(s["tabd"], 1)
                    each(a, step)

                @block.tensor
                def _(te):
                    def step(t):
                        te.wait_ge(s["xin"], (t + 1) * 16)
                        wait(te, s["tabd"], t)
                        if kind == "sum":
                            for j in range(JB):
                                last = nc.tensor.transpose(p_x[:, j, 0:NB], xs[:, j, :], self.ident[0:NB, 0:NB])
                            last.then_inc(s["turned"], 1)
                        te.wait_ge(s["sumd"], t + 1)
                        if kind == "sum":
                            te.wait_ge(s["xt"], t + 1)
                        for j in range(JB):
                            if kind == "sum":
                                nc.tensor.matmul(p_y[0:NB, j, :], xt[:, j, 0:NB], self.l0_w[:, 0, :], start=True, stop=False)
                                nc.tensor.matmul(p_y[0:NB, j, :], sums[:, 0, j * NB:(j + 1) * NB], self.l0_w[:, 1, :], start=False, stop=False)
                                last = nc.tensor.matmul(p_y[0:NB, j, :], self.ones[0:1, 0:NB], self.l0_b[:, :], start=False, stop=True)
                            else:
                                for h in range(2):
                                    last = nc.tensor.matmul(p_y[0:NB, j, :], sums[:, h, j * NB:(j + 1) * NB], self.outw[:, h, :],
                                                            start=(h == 0), stop=(h == 1))
                        last.then_inc(s["lin"], 1)
                        te.wait_ge(s["step"], (t + 1) * LINKS)
                        for j in range(JB):
                            last = nc.tensor.transpose(p_z[:, j, 0:NB], y[:, j, :], self.ident[0:NB, 0:NB])
                        last.then_inc(s["turned2"], 1)
                        te.wait_ge(s["xt2"], t + 1)
                        for j in range(JB):
                            w = self.up[:, :] if kind == "sum" else self.g_a[0][:, :]
                            last = nc.tensor.matmul(p_x[0:NB, j, 0:w.shape[1]], xt[:, j, 0:NB], w, start=True, stop=True)
                        if kind == "product":
                            for hh, p in enumerate((p_y, p_z)):
                                for j in range(JB):
                                    last = nc.tensor.matmul(p[0:2, j, 0:NB], self.g_a[0][:, 2 * hh:2 * hh + 2], xt[:, j, 0:NB],
                                                            start=True, stop=True)
                        last.then_inc(s["tabbed"], 1)
                    each(te, step)

                @block.vector
                def _(v):
                    def step(t):
                        then = Chain(v, s["step"], t * LINKS)
                        wait(v, s["sent"], t * (16 * SENT))
                        v.wait_ge(s["lin"], t + 1)
                        v.wait_ge(s["xin"], (t + 1) * 16)
                        if kind == "sum":
                            then(v.scalar_tensor_tensor(y[:, :, :].rearrange("p j f -> p (j f)"),
                                                        p_y[0:NB, 0:JB, :].rearrange("p j f -> p (j f)"), 0.0,
                                                        xs[:, :, :].rearrange("p j f -> p (j f)"), ALU.max, ALU.add))
                        else:
                            then(v.tensor_tensor(y[:, :, :], p_y[0:NB, 0:JB, :], xs[:, :, :], ALU.add))
                        self.norm(v, s["var"], then, y[:, :, :], D, tmp[:, :, :], st,
                                  lambda: v.wait_ge(s["rooted"], t + 1))
                        assert then.n == LINKS, then.n
                    each(v, step)
            self.zero(s.values())

    def node_attention(self, l):
        nc = self.nc
        dim, table = (D, self.t1_d) if l == 0 else (HID, self.t2_d)
        n = f"na{l}_"
        with ExitStack() as ctx:
            sb, ps, sem = self.sb, self.ps, self.sem
            own = sb(n + "own", [NB, JB, dim + HEADS], F32, ctx)
            own_ed = sb(n + "own_ed", [NB, JB, HEADS], F32, ctx)
            sums = sb(n + "sums", [P, HEADS, NS], F32, ctx)
            den = sb(n + "den", [HEADS, NS], F32, ctx)
            top = sb(n + "top", [2, 2, NS], F32, ctx)
            dt_s = sb(n + "dt", [NB, JB, 8], F32, ctx)
            zz = sb(n + "zz", [NB, 2, JB, HEADS], F32, ctx)
            zl = sb(n + "zl", [NB, 2, JB, HEADS], F32, ctx)
            pown = sb(n + "pown", [NB, JB, HEADS], F32, ctx)
            rd = sb(n + "rd", [NB, 2, JB, HEADS], F32, ctx)
            prod = sb(n + "prod", [NB, 2, JB, HEADS, HID], F32, ctx)
            h = sb(n + "h", [NB, JB, HID], F32, ctx)
            tmp = sb(n + "tmp", [NB, JB, D], F32, ctx)
            st = sb(n + "st", [P, 2, JB], F32, ctx)
            xt = sb(n + "xt", [P, JB, P], F32, ctx)
            ht = sb(n + "ht", [HID, JB, P], F32, ctx)
            xs = sb(n + "xs", [NB, JB, D], F32, ctx)
            y = sb(n + "y", [NB, JB, D], F32, ctx)
            tab = sb(n + "tab", [NB, JB, HID + HEADS], F32, ctx)
            edt = sb(n + "edt", [NB, JB, HEADS], F32, ctx)
            p_a = ps(n + "pa", [P, 6, HEADS * HID], ctx)
            p_b = ps(n + "pb", [P, 6, HEADS * HID], ctx)
            p_t = ps(n + "pt", [P, 8, P], ctx)
            p_dt = p_b[0:NB, 5, 0:JB * 8].rearrange("p (j o) -> p j o", o=8)
            p_es = p_b[:, :, :].rearrange("p a (b n) -> p (a b) n", n=P)
            names = ("ownin", "xin", "sumd", "turned0", "xt", "lin", "dt", "own", "exped", "var", "rooted", "step", "turned",
                     "ht", "out", "tabd", "sent", "go_t", "go_s")
            s = {k: sem(n + k, ctx) for k in names}
            SENT = 2 if l == 0 else 1
            LINKS = 25 if l == 0 else 33
            FIRST = 25
            VARS = 1 if l == 0 else 2
            with nc.Block() as block:
                @block.sync
                def _(e):
                    def step(t):
                        wait(e, s["sent"], t * (16 * SENT))
                        e.sem_inc(s["go_s"], 1)
                        e.dma_start(own[:, :, :], self.node_rows(table, t, dim + HEADS)).then_inc(s["ownin"], 16)
                        e.dma_start(own_ed[:, :, :], self.node_rows(self.ed_d[l][0:N, :], t, HEADS)).then_inc(s["ownin"], 16)
                        if l == 0:
                            e.wait_ge(s["tabd"], t + 1)
                            e.dma_start(self.node_rows(self.t2_d, t, HID + HEADS), tab[:, :, :]).then_inc(s["sent"], 16)
                            e.dma_start(self.node_rows(self.ed_d[1][0:N, :], t, HEADS), edt[:, :, :]).then_inc(s["sent"], 16)
                        else:
                            e.dma_start(xs[:, :, :], self.node_rows(self.x2_d, t, D)).then_inc(s["xin"], 16)
                            e.wait_ge(s["step"], (t + 1) * LINKS)
                            e.dma_start(self.node_rows(self.x3_d, t, D), y[:, :, :]).then_inc(s["sent"], 16)
                    each(e, step)
                    e.wait_ge(s["sent"], NT * 16 * SENT)

                @block.scalar
                def _(a):
                    def step(t):
                        at = bass.ds(t * NS, NS)
                        wait(a, s["sent"], t * (16 * SENT))
                        nc.scalar.activation(den[:, :], self.den[:, at], ACT.Copy)
                        nc.scalar.activation(top[:, :, :], self.top[:, :, at], ACT.Copy)
                        nc.scalar.activation(sums[0:dim, :, :], self.acc[0:dim, :].rearrange("p (h n) -> p h n", h=HEADS)
                                             [:, :, at], ACT.Copy).then_inc(s["sumd"], 1)
                        a.wait_ge(s["turned0"], t + 1)
                        nc.scalar.activation(xt[0:dim, :, 0:NB], p_t[0:dim, 0:JB, 0:NB], ACT.Copy).then_inc(s["xt"], 1)
                        a.wait_ge(s["own"], t + 1)
                        nc.scalar.activation(pown[:, :, :], zl[:, 0, :, :], ACT.Exp).then_inc(s["exped"], 1)
                        a.wait_ge(s["var"], t * VARS + 1)
                        nc.scalar.activation(st[0:NB, 1, :], st[0:NB, 1, :], ACT.Sqrt).then_inc(s["rooted"], 1)
                        a.wait_ge(s["turned"], t + 1)
                        nc.scalar.activation(ht[:, :, 0:NB], p_t[0:HID, 0:JB, 0:NB], ACT.Copy).then_inc(s["ht"], 1)
                        if l == 0:
                            a.wait_ge(s["out"], t + 1)
                            nc.scalar.activation(tab[:, :, 0:HID], h[:, :, :], ACT.Copy)
                            nc.scalar.activation(tab[:, :, HID:HID + HEADS], p_a[0:NB, 0:JB, 0:HEADS], ACT.Copy)
                            for hh in range(2):
                                nc.scalar.activation(self.top[:, hh, at].rearrange("b (j p) -> b j p", j=JB),
                                                     p_es[0:2, hh * JB:(hh + 1) * JB, 0:NB], ACT.Copy)
                            nc.scalar.activation(edt[:, :, :], p_a[0:NB, 0:JB, HEADS:2 * HEADS], ACT.Copy).then_inc(s["tabd"], 1)
                        else:
                            a.wait_ge(s["var"], t * VARS + 2)
                            nc.scalar.activation(st[0:NB, 1, :], st[0:NB, 1, :], ACT.Sqrt).then_inc(s["rooted"], 1)
                    each(a, step)

                @block.tensor
                def _(te):
                    def step(t):
                        te.wait_ge(s["ownin"], (t + 1) * 32)
                        wait(te, s["step"], t * LINKS)
                        if l == 0:
                            wait(te, s["tabd"], t)
                        te.sem_inc(s["go_t"], 1)
                        for j in range(JB):
                            last = nc.tensor.transpose(p_t[0:dim, j, 0:NB], own[:, j, 0:dim], self.ident[0:NB, 0:NB])
                        last.then_inc(s["turned0"], 1)
                        te.wait_ge(s["sumd"], t + 1)
                        te.sem_inc(s["go_t"], 1)
                        for j in range(JB):
                            nc.tensor.transpose(p_dt[:, j, 0:HEADS], den[:, j * NB:(j + 1) * NB], self.ident[0:HEADS, 0:HEADS])
                            for hh in range(2):
                                last = nc.tensor.transpose(p_dt[:, j, 4 + 2 * hh:6 + 2 * hh], top[:, hh, j * NB:(j + 1) * NB],
                                                           self.ident[0:2, 0:2])
                        last.then_inc(s["dt"], 1)
                        for j in range(JB):
                            for o, hd in enumerate(HEAD_OF):
                                nc.tensor.matmul(p_a[0:NB, j, o * HID:(o + 1) * HID], sums[0:dim, o, j * NB:(j + 1) * NB],
                                                 self.g_w[l][:, hd * HID:(hd + 1) * HID], start=True, stop=True)
                        te.wait_ge(s["xt"], t + 1)
                        te.wait_ge(s["step"], t * LINKS + 1)
                        for j in range(JB):
                            for o, hd in enumerate(HEAD_OF):
                                last = nc.tensor.matmul(p_b[0:NB, j, o * HID:(o + 1) * HID], xt[0:dim, j, 0:NB],
                                                        self.g_w[l][:, hd * HID:(hd + 1) * HID], start=True, stop=True)
                        last.then_inc(s["lin"], 1)
                        te.wait_ge(s["step"], t * LINKS + FIRST)
                        te.sem_inc(s["go_t"], 1)
                        for j in range(JB):
                            last = nc.tensor.transpose(p_t[0:HID, j, 0:NB], h[:, j, :], self.ident[0:NB, 0:NB])
                        last.then_inc(s["turned"], 1)
                        te.wait_ge(s["ht"], t + 1)
                        if l == 0:
                            for j in range(JB):
                                nc.tensor.matmul(p_a[0:NB, j, 0:8], ht[:, j, 0:NB], self.g_a[1][:, :], start=True, stop=True)
                            for hh in range(2):
                                for j in range(JB):
                                    last = nc.tensor.matmul(p_es[0:2, hh * JB + j, 0:NB], self.g_a[1][:, 2 * hh:2 * hh + 2],
                                                            ht[:, j, 0:NB], start=True, stop=True)
                        else:
                            for j in range(JB):
                                nc.tensor.matmul(p_a[0:NB, j, 0:D], ht[:, j, 0:NB], self.wo[:, :], start=True, stop=False)
                                last = nc.tensor.matmul(p_a[0:NB, j, 0:D], self.ones[0:1, 0:NB], self.bo[:, :], start=False, stop=True)
                        last.then_inc(s["out"], 1)
                    each(te, step)

                @block.vector
                def _(v):
                    wide = [NB, JB, HID]
                    def step(t):
                        then = Chain(v, s["step"], t * LINKS)
                        wait(v, s["sent"], t * (16 * SENT))
                        v.wait_ge(s["dt"], t + 1)
                        then(v.tensor_copy(dt_s[:, :, :], p_dt))
                        v.wait_ge(s["ownin"], (t + 1) * 32)
                        then(v.tensor_tensor(zz[:, 0, :, :], own[:, :, dim:dim + HEADS], own_ed[:, :, :], ALU.add))
                        then(v.tensor_tensor(zz[:, 1, :, :], dt_s[:, :, 4:8], own_ed[:, :, :], ALU.add))
                        then(v.tensor_scalar(zl[:, :, :, :], zz[:, :, :, :], 0.2, None, ALU.mult))
                        then(v.tensor_tensor(zz[:, :, :, :], zl[:, :, :, :], zz[:, :, :, :], ALU.max))
                        then(v.tensor_tensor(zz[:, 0, :, :], zz[:, 0, :, :], zz[:, 1, :, :], ALU.min))
                        v.tensor_tensor(zl[:, 0, :, :], zz[:, 0, :, :], zz[:, 1, :, :], ALU.subtract).then_inc(s["own"], 1)
                        v.wait_ge(s["exped"], t + 1)
                        then(v.tensor_tensor(rd[:, 0, :, :], dt_s[:, :, 0:4], pown[:, :, :], ALU.add))
                        then(v.reciprocal(rd[:, 0, :, :], rd[:, 0, :, :]))
                        then(v.tensor_scalar(rd[:, 0, :, :], rd[:, 0, :, :], 1.0 / HEADS, None, ALU.mult))
                        then(v.tensor_tensor(rd[:, 1, :, :], rd[:, 0, :, :], pown[:, :, :], ALU.mult))
                        v.wait_ge(s["lin"], t + 1)
                        for k, p in enumerate((p_a, p_b)):
                            then(v.tensor_tensor(prod[:, k, :, :, :].rearrange("p j o k -> p (j o) k"),
                                                 p[0:NB, 0:JB, :].rearrange("p j (o k) -> p (j o) k", k=HID),
                                                 rd[:, k, :, :].rearrange("p j o -> p (j o)").unsqueeze(2)
                                                 .to_broadcast([NB, JB * HEADS, HID]), ALU.mult))
                        then(v.tensor_tensor(prod[:, 0, :, :, :], prod[:, 0, :, :, :], prod[:, 1, :, :, :], ALU.add))
                        then(v.tensor_reduce(h[:, :, :], prod[:, 0, :, :, :].rearrange("p j o k -> p j k o"), AX.X, ALU.add))

                        def row(k):
                            return self.g_row[l][0:NB, k, :].unsqueeze(1).to_broadcast(wide)
                        then(v.tensor_tensor(h[:, :, :], h[:, :, :], row(0), ALU.add))
                        self.norm(v, s["var"], then, h[:, :, :], HID, tmp[:, :, 0:HID], st,
                                  lambda: v.wait_ge(s["rooted"], t * VARS + 1))
                        then(v.tensor_tensor(h[:, :, :], h[:, :, :], row(1), ALU.mult))
                        then(v.tensor_tensor(h[:, :, :], h[:, :, :], row(2), ALU.add))
                        then(v.tensor_scalar(h[:, :, :], h[:, :, :], 0.0, None, ALU.max))
                        assert then.n == FIRST, then.n
                        if l == 1:
                            v.wait_ge(s["out"], t + 1)
                            v.wait_ge(s["xin"], (t + 1) * 16)
                            then(v.tensor_tensor(y[:, :, :], p_a[0:NB, 0:JB, 0:D], xs[:, :, :], ALU.add))
                            self.norm(v, s["var"], then, y[:, :, :], D, tmp[:, :, :], st,
                                      lambda: v.wait_ge(s["rooted"], t * VARS + 2))
                        assert then.n == LINKS, then.n
                    each(v, step)
            self.zero(s.values())

    def node_last(self):
        nc = self.nc
        with ExitStack() as ctx:
            sb, ps, sem = self.sb, self.ps, self.sem
            n = "nl_"
            sums = sb(n + "sums", [P, NS], F32, ctx)
            den = sb(n + "den", [1, NS], F32, ctx)
            xs = sb(n + "xs", [NB, JB, D], F32, ctx)
            y = sb(n + "y", [NB, JB, D], F32, ctx)
            tmp = sb(n + "tmp", [NB, JB, D], F32, ctx)
            c = sb(n + "c", [NB, 4, JB], F32, ctx)
            st = sb(n + "st", [P, 2, JB], F32, ctx)
            p_d = ps(n + "pd", [P, 8, 64], ctx)
            p_y = ps(n + "py", [P, 8, P], ctx)
            s = {k: sem(n + k, ctx) for k in ("xin", "sumd", "lin", "var", "rooted", "step", "sent", "go_t")}
            LINKS = 16
            with nc.Block() as block:
                @block.sync
                def _(e):
                    def step(t):
                        wait(e, s["sent"], t * 16)
                        e.dma_start(xs[:, :, :], self.node_rows(self.x3_d, t, D)).then_inc(s["xin"], 16)
                        e.wait_ge(s["step"], (t + 1) * LINKS)
                        e.dma_start(self.node_rows(self.out, t, D), y[:, :, :]).then_inc(s["sent"], 16)
                    each(e, step)
                    e.wait_ge(s["sent"], NT * 16)

                @block.scalar
                def _(a):
                    def step(t):
                        wait(a, s["lin"], t)
                        nc.scalar.activation(den[:, :], self.den[0:1, bass.ds(t * NS, NS)], ACT.Copy)
                        nc.scalar.activation(sums[:, :], self.acc[:, bass.ds(t * NS, NS)], ACT.Copy).then_inc(s["sumd"], 1)
                        a.wait_ge(s["var"], t + 1)
                        nc.scalar.activation(st[0:NB, 1, :], st[0:NB, 1, :], ACT.Sqrt).then_inc(s["rooted"], 1)
                    each(a, step)

                @block.tensor
                def _(te):
                    def step(t):
                        te.wait_ge(s["sumd"], t + 1)
                        wait(te, s["step"], t * LINKS)
                        te.sem_inc(s["go_t"], 1)
                        for j in range(JB):
                            nc.tensor.transpose(p_d[0:NB, j, 0:1], den[:, j * NB:(j + 1) * NB], self.ident[0:1, 0:1])
                        for j in range(JB):
                            last = nc.tensor.transpose(p_y[0:NB, j, :], sums[:, j * NB:(j + 1) * NB], self.ident[:, :])
                        last.then_inc(s["lin"], 1)
                    each(te, step)

                @block.vector
                def _(v):
                    def step(t):
                        then = Chain(v, s["step"], t * LINKS)
                        v.wait_ge(s["lin"], t + 1)
                        wait(v, s["sent"], t * 16)
                        full = [NB, JB, D]

                        def col(k):
                            return c[:, k, :].unsqueeze(2).to_broadcast(full)
                        then(v.tensor_scalar(c[:, 0, :], p_d[0:NB, 0:JB, 0], 1e-8, None, ALU.max))
                        then(v.reciprocal(c[:, 1, :], c[:, 0, :]))
                        then(v.tensor_scalar(c[:, 2, :], c[:, 0, :], 1e-8, 0.3, ALU.is_gt, ALU.mult))
                        then(v.tensor_scalar(c[:, 3, :], c[:, 2, :], -1.0, 1.0, ALU.mult, ALU.add))
                        then(v.tensor_tensor(c[:, 1, :], c[:, 1, :], c[:, 2, :], ALU.mult))
                        v.wait_ge(s["xin"], (t + 1) * 16)
                        then(v.tensor_tensor(y[:, :, :], p_y[0:NB, 0:JB, :], col(1), ALU.mult))
                        then(v.tensor_tensor(tmp[:, :, :], xs[:, :, :], col(3), ALU.mult))
                        then(v.tensor_tensor(y[:, :, :], y[:, :, :], tmp[:, :, :], ALU.add))
                        then(v.tensor_tensor(y[:, :, :], y[:, :, :], xs[:, :, :], ALU.add))
                        self.norm(v, s["var"], then, y[:, :, :], D, tmp[:, :, :], st,
                                  lambda: v.wait_ge(s["rooted"], t + 1))
                        assert then.n == LINKS, then.n
                    each(v, step)
            self.zero(s.values())

    def build(self):
        nc = self.nc
        with self.ctx:
            self.allocate()
            self.x2_d = self.dram("x2_rows", [N, D])
            self.setup()
            self.is_general = nc.values_load(self.general[0:1, 0:1], min_val=0, max_val=1)
            self.sum_edges("e0_", self.i["x"], False)
            self.node_layer("n0_", "sum", self.i["x"])
            self.product_edges()
            self.node_layer("n1_", "product", self.x1_d)
            self.attend_edges(0, self.t1_d, D)
            self.node_attention(0)
            self.attend_edges(1, self.t2_d, HID)
            self.node_attention(1)
            self.sum_edges("e3_", self.x3_d, True)
            self.node_last()


def graph_layers(nc, names, aps, out):
    Program(nc, dict(zip(names, aps)), out).build()


_INS = ["x", "src", "dst", "edge_attr_3", "edge_weight", "L0_gnn_W", "L0_gnn_b", "L1_gnn_W_up0", "L1_gnn_W_up1",
        "L1_gnn_mlp_w0", "L1_gnn_mlp_b0", "L1_gnn_mlp_w1", "L1_gnn_mlp_b1", "L1_gnn_mlp_w2", "L1_gnn_mlp_b2",
        "L1_gnn_W_out0", "L1_gnn_W_out1", "L2_gnn_W1", "L2_gnn_asrc1", "L2_gnn_adst1", "L2_gnn_b1", "L2_gnn_g1",
        "L2_gnn_be1", "L2_gnn_W2", "L2_gnn_asrc2", "L2_gnn_adst2", "L2_gnn_b2", "L2_gnn_g2", "L2_gnn_be2",
        "L2_gnn_Wo", "L2_gnn_bo"]


def kernel(**inputs):
    import numpy as _np
    import concourse.bacc as _bacc
    from concourse import mybir as _mybir
    from concourse.bass_utils import run_bass_kernel_spmd as _run

    nc = _bacc.Bacc("TRN2", target_bir_lowering=False, num_devices=1)
    arrays, args = {}, []
    for name in _INS:
        a = _np.ascontiguousarray(inputs[name])
        arrays[f"in_{name}_dram"] = a
        args.append(nc.dram_tensor(f"in_{name}_dram", a.shape, _mybir.dt.from_np(a.dtype), kind="ExternalInput").ap())
    out = nc.dram_tensor("out_0_dram", (3125, 128), _mybir.dt.float32, kind="ExternalOutput").ap()
    graph_layers(nc, _INS, args, out)
    r = _run(nc, [arrays], core_ids=[0])
    return r.results[0]["out_0_dram"]
```

```python
import concourse.bass as bass
from concourse import mybir
from contextlib import ExitStack

F32 = mybir.dt.float32
I32 = mybir.dt.int32
BF16 = mybir.dt.bfloat16
ALU = mybir.AluOpType
ACT = mybir.ActivationFunctionType
AX = mybir.AxisListType

N = 3125
E = 53125
D = 128
P = 128
CH = 4
GE = CH * P
NG = -(-E // GE)
LAST = E - (NG - 1) * GE
W = 48
HW = 64
ROUNDS = -(-N // W)
NP = N + W + (-(N + W)) % P
NB = 125
JB = 5
NS = JB * NB
NT = N // NS
HEADS = 4
HID = 64
MUL = 32
NBAS = 8
BIG = 1e30
NOWHERE = float(1 << 20)
LN_EPS = 1e-5
MIN_NORM2 = 1.3e-35
HEAD_OF = [0, 2, 1, 3]
PARTS = 3
MEET = [(0, 0), (0, 1), (0, 2), (1, 0), (1, 1), (2, 0)]
TERMS = len(MEET)
SC = 2 * HEADS
SCP = PARTS * SC
SCW = SC + SCP // 2
SPLIT = 2 * PARTS - 1


def wait(eng, sem, value):
    if not isinstance(value, int) or value > 0:
        eng.wait_ge(sem, value)


def pipeline(eng, unroll, stages):
    def at(turn, s):
        for lag, step in stages:
            slot, t = (s - lag) % unroll, turn + (s - lag) // unroll
            k = t * unroll + slot
            if not isinstance(k, int) or 0 <= k < NG:
                step(k, slot, t)

    for s in range(unroll):
        at(0, s)
    with eng.Fori(1, NG // unroll) as turn:
        for s in range(unroll):
            at(turn, s)
    for s in range(max(lag for lag, _ in stages)):
        at(NG // unroll, s)


def each(eng, step):
    step(0)
    with eng.Fori(1, NT) as t:
        step(t)


class Chain:

    def __init__(self, eng, sem, start=0):
        self.eng, self.sem, self.start, self.n = eng, sem, start, 0

    def __call__(self, ins):
        self.n += 1
        ins.then_inc(self.sem, 1)
        self.eng.wait_ge(self.sem, self.start + self.n)


class Program:
    def __init__(self, nc, ins, out):
        self.nc, self.i, self.out = nc, ins, out
        self.ctx = ExitStack()

    def sb(self, name, shape, dt=F32, ctx=None):
        return (ctx or self.ctx).enter_context(self.nc.sbuf_tensor(name, shape, dt))

    def ps(self, name, shape, ctx, dt=F32):
        return ctx.enter_context(self.nc.psum_tensor(name, shape, dt))

    def sem(self, name, ctx=None):
        return (ctx or self.ctx).enter_context(self.nc.semaphore(name))

    def dram(self, name, shape, dt=F32):
        return self.nc.dram_tensor(name, shape, dt, kind="Internal").ap()

    def allocate(self):
        sb = self.sb
        self.ident = sb("ident", [P, P])
        self.ones = sb("ones", [P, P])
        self.ident_h = sb("ident_h", [P, P], BF16)
        self.pick = sb("pick", [P, 2, P], BF16)
        self.iota = sb("iota", [P, W])
        self.node_of_row = sb("node_of_row", [P, 1])
        self.iota_now = sb("iota_now", [P, W])
        self.node_now = sb("node_now", [P, 1])
        self.base_first = sb("base_first", [1, NG], I32)
        self.base_now = sb("base_now", [1, NG], I32)
        self.shift = sb("shift", [P, 1])
        self.general = sb("general", [1, 1], I32)
        self.src_t = sb("src_t", [P, NG, CH], I32)
        self.dst_t = sb("dst_t", [P, NG, CH])
        self.w_t = sb("w_t", [P, NG, CH])
        self.dir_t = sb("dir_t", [P, NG, CH, 3])
        self.l0_w = sb("l0_w", [P, 2, D])
        self.l0_b = sb("l0_b", [1, D])
        self.up = sb("up", [P, P])
        self.outw = sb("outw", [P, 2, P])
        self.m_w0 = sb("m_w0", [2 * TERMS * NBAS, P], BF16)
        self.m_b0 = sb("m_b0", [P, 1])
        self.m_w1 = sb("m_w1", [P, P])
        self.m_b1 = sb("m_b1", [P, 1])
        self.m_w2 = sb("m_w2", [P, 2, 4 * MUL])
        self.m_b2 = sb("m_b2", [PARTS, CH, 4 * MUL], BF16)
        self.ones_h = sb("ones_h", [PARTS, P], BF16)
        self.g_w = [sb("g_w1", [D, HEADS * HID]), sb("g_w2", [HID, HEADS * HID])]
        self.g_a = [sb("g_a1", [D, 8]), sb("g_a2", [HID, 8])]
        self.g_row = [sb(f"g_row{n}", [P, 3, HID]) for n in (1, 2)]
        self.wo = sb("wo", [HID, D])
        self.bo = sb("bo", [1, D])
        self.acc = sb("acc", [P, HEADS * NP])
        self.den = sb("den", [HEADS, NP])
        self.top = sb("top", [2, 2, NP])
        self.landed = [self.sem(f"rows_landed{n}") for n in range(8)]
        dram = self.dram
        self.dst_d = dram("dst_rows", [NG, GE])
        self.emb_d = dram("emb_rows", [NG, PARTS, NBAS, GE], BF16)
        self.x1_d = dram("x1_rows", [N, D])
        self.up_d = dram("up_rows", [N, D])
        self.t_d = [dram("gat1_rows", [NP, D + SCW]), dram("gat2_rows", [NP, HID + SCW])]
        self.x3_d = dram("x3_rows", [N, D])

    def setup(self):
        nc, i, sb, ps, sem = self.nc, self.i, self.sb, self.ps, self.sem
        with ExitStack() as ctx:
            src_i = sb("src_i", [NG, GE], I32, ctx)
            dst_i = sb("dst_i", [NG, GE], I32, ctx)
            w_r = sb("w_r", [NG, GE], F32, ctx)
            vec_r = sb("vec_r", [NG, GE * 3], F32, ctx)
            src_f = sb("src_f", [NG, GE], F32, ctx)
            dst_f = sb("dst_f", [NG, GE], F32, ctx)
            dst_l = sb("dst_l", [NG, GE], F32, ctx)
            fl_i = sb("fl_i", [1, 2, NG], I32, ctx)
            fl = sb("fl", [1, 2, NG], F32, ctx)
            bad = sb("bad", [NG, GE], F32, ctx)
            bad_n = sb("bad_n", [NG, 1], F32, ctx)
            bad_r = sb("bad_r", [1, 3, NG], F32, ctx)
            bad_s = sb("bad_s", [1, 4], F32, ctx)
            row = sb("row", [1, NG + 1], F32, ctx)
            fcol = sb("fcol", [NG, 1], F32, ctx)
            row_b = sb("row_b", [P, NG + 1], F32, ctx)
            l0_n = sb("l0_n", [P, 2 * D], F32, ctx)
            a_m = sb("a_m", [P, 2, 2, 8], F32, ctx)
            wt = sb("wt", [P, 2, 2, P], F32, ctx)
            m0r = sb("m0r", [NBAS, 64], F32, ctx)
            m0s = sb("m0s", [NBAS, 64], F32, ctx)
            m0p = sb("m0p", [NBAS, PARTS, 64], BF16, ctx)
            m2r = sb("m2r", [1, 4 * MUL], F32, ctx)
            m2p = sb("m2p", [1, PARTS, 4 * MUL], BF16, ctx)
            m0l = sb("m0l", [NBAS, PARTS, 64], F32, ctx)
            m2l = sb("m2l", [1, PARTS, 4 * MUL], F32, ctx)
            upr = sb("upr", [P, P], F32, ctx)
            outr = sb("outr", [P, 2, P], F32, ctx)
            zero = sb("zero", [P, SCW], F32, ctx)
            pickf = sb("pickf", [P, 2, P], F32, ctx)
            cleared = sem("cleared", ctx)
            consts = sem("consts", ctx)
            loaded = sem("loaded", ctx)
            with nc.Block() as block:
                @block.vector
                def _(v):
                    v.memset(src_i[:, :], 0).then_inc(cleared, 1)
                    v.memset(dst_i[:, :], int(NOWHERE)).then_inc(cleared, 1)
                    v.memset(w_r[:, :], 0.0).then_inc(cleared, 1)
                    v.memset(vec_r[:, :], 0.0).then_inc(cleared, 1)
                    v.memset(upr[:, :], 0.0).then_inc(cleared, 1)
                    v.memset(outr[:, :, :], 0.0).then_inc(cleared, 1)
                    v.memset(a_m[:, :, :, :], 0.0).then_inc(cleared, 1)
                    v.memset(zero[:, :], 0.0).then_inc(cleared, 1)
                    v.memset(self.m_w0[:, :], 0.0).then_inc(cleared, 1)
                    v.memset(self.m_w1[:, :], 0.0).then_inc(cleared, 1)
                    v.memset(self.m_w2[:, :, :], 0.0).then_inc(cleared, 1)
                    v.memset(self.ones[:, :], 1.0)
                    v.memset(self.top[:, :, N:], -BIG)
                    v.memset(self.ones_h[:, :], 1.0)

                @block.gpsimd
                def _(g):
                    g.memset(self.ident[:, :], 0.0).then_inc(consts, 1)
                    g.iota(self.iota[:, :], [[1, W]], base=0, channel_multiplier=0,
                           allow_small_or_imprecise_dtypes=True).then_inc(consts, 1)
                    for q in range(P // HW):
                        g.wait_ge(consts, 2 + q)
                        g.iota(self.node_of_row[q * HW:(q + 1) * HW, :], [[0, 1]], base=0, channel_multiplier=1,
                               allow_small_or_imprecise_dtypes=True).then_inc(consts, 1)
                    g.wait_ge(consts, 4)
                    g.affine_select(out=self.ident[:, :], in_=self.ident[:, :], compare_op=ALU.not_equal,
                                    fill=1.0, base=0, pattern=[[-1, P]], channel_multiplier=1).then_inc(consts, 1)
                    g.memset(pickf[:, :, :], 0.0).then_inc(consts, 1)
                    for part in range(PARTS):
                        g.wait_ge(consts, 6 + part)
                        view = pickf[:, :, :].rearrange("o b (h n) -> o b h n", h=2)
                        g.affine_select(out=view, in_=view, compare_op=ALU.not_equal, fill=1.0, base=-SC * part,
                                        pattern=[[-1, 2], [-2, 2], [0, HW]], channel_multiplier=1).then_inc(consts, 1)
                    g.wait_ge(consts, 6 + PARTS)
                    g.tensor_copy(self.ident_h[:, :], self.ident[:, :])
                    g.tensor_copy(self.pick[:, :, :], pickf[:, :, :])

                @block.sync
                def _(s):
                    n = 0

                    def load(dst, src):
                        nonlocal n
                        n += 16
                        with nc.allow_non_contiguous_dma(reason="columns of small weights"):
                            s.dma_start(dst, src).then_inc(loaded, 16)
                    s.wait_ge(cleared, 11)
                    full = (NG - 1) * GE
                    for tile, name, k in ((src_i, "src", 1), (dst_i, "dst", 1), (w_r, "edge_weight", 1)):
                        load(tile[0:NG - 1, :], i[name][0:full].rearrange("(g e) -> g e", e=GE))
                        load(tile[NG - 1:NG, 0:LAST], i[name][full:E].rearrange("(g e) -> g e", g=1))
                    load(vec_r[0:NG - 1, :], i["edge_attr_3"][0:full, :].rearrange("(g e) c -> g (e c)", e=GE))
                    load(vec_r[NG - 1:NG, 0:3 * LAST], i["edge_attr_3"][full:E, :].rearrange("(g e) c -> g (e c)", g=1))
                    firsts = i["dst"][0:full].rearrange("(g e) -> e g", e=GE)
                    load(fl_i[:, 0, 0:NG - 1], firsts[0:1, :])
                    load(fl_i[:, 1, 0:NG - 1], firsts[GE - 1:GE, :])
                    load(fl_i[:, 0, NG - 1:NG], i["dst"][full:full + 1].rearrange("(g e) -> g e", g=1))
                    load(fl_i[:, 1, NG - 1:NG], i["dst"][E - 1:E].rearrange("(g e) -> g e", g=1))
                    load(l0_n[:, :], i["L0_gnn_W"])
                    load(self.l0_b[:, :], i["L0_gnn_b"].rearrange("(a n) -> a n", a=1))
                    load(upr[0:MUL, 0:MUL], i["L1_gnn_W_up0"])
                    for c in range(3):
                        load(upr[MUL + c:P:3, MUL * (1 + c):MUL * (2 + c)], i["L1_gnn_W_up1"])
                    load(outr[0:2 * MUL, 0, 0:MUL], i["L1_gnn_W_out0"])
                    for c, (r, h) in enumerate(((64, 0), (0, 1), (64, 1))):
                        load(outr[r:r + 2 * MUL, h, MUL + c:P:3], i["L1_gnn_W_out1"])
                    load(m0r[:, :], i["L1_gnn_mlp_w0"])
                    load(m2r[:, :], i["L1_gnn_mlp_b2"].rearrange("(a n) -> a n", a=1))
                    for g in range(2):
                        at = slice(g * 64, g * 64 + 64)
                        load(self.m_b0[at, :], i["L1_gnn_mlp_b0"].rearrange("(n a) -> n a", a=1))
                        load(self.m_w1[at, at], i["L1_gnn_mlp_w1"])
                        load(self.m_b1[at, :], i["L1_gnn_mlp_b1"].rearrange("(n a) -> n a", a=1))
                        load(self.m_w2[at, g, :], i["L1_gnn_mlp_w2"])
                    for l, n_ in ((0, "1"), (1, "2")):
                        load(self.g_w[l][:, :], i["L2_gnn_W" + n_])
                        for o, h in enumerate(HEAD_OF):
                            r = HID * (h % 2)
                            for k, name in ((0, "asrc"), (HEADS, "adst")):
                                load(a_m[r:r + HID, l, h // 2, k + o:k + o + 1],
                                     i[f"L2_gnn_{name}{n_}"][h, :].rearrange("(n a) -> n a", a=1))
                        for k, name in enumerate(("b", "g", "be")):
                            load(self.g_row[l][:, k, :],
                                 i[f"L2_gnn_{name}{n_}"].rearrange("(a n) -> a n", a=1).to_broadcast([P, HID]))
                        load(self.t_d[l][N:NP, (D, HID)[l]:], zero[0:NP - N, :])
                    load(self.wo[:, :], i["L2_gnn_Wo"])
                    load(self.bo[:, :], i["L2_gnn_bo"].rearrange("(a n) -> a n", a=1))
                    s.wait_ge(loaded, n)

            step = sem("setup_step", ctx)
            counted = sem("counted", ctx)
            rowed = sem("rowed", ctx)
            spread = sem("spread", ctx)
            stored = sem("dst_stored", ctx)
            with ExitStack() as pctx:
                p_n = ps("p_n", [1, 1], pctx)
                p_row = ps("p_row", [P, NG + 1], pctx)
                p_col = ps("p_col", [NG, 1], pctx)
                with nc.Block() as block:
                    @block.vector
                    def _(v):
                        then = Chain(v, step)
                        v.tensor_copy(src_f[:, :], src_i[:, :])
                        v.tensor_copy(fl[:, :, :], fl_i[:, :, :]).then_inc(spread, 1)
                        then(v.tensor_copy(dst_f[:, :], dst_i[:, :]))
                        then(v.tensor_tensor(bad[:, 0:GE - 1], dst_f[:, 0:GE - 1], dst_f[:, 1:GE], ALU.is_gt))
                        then(v.tensor_reduce(bad_n[:, :], bad[:, 0:GE - 1], AX.X, ALU.add))
                        then(v.memset(bad_r[:, :, :], 0.0))
                        v.wait_ge(spread, 1)
                        first, last = fl[:, 0, :], fl[:, 1, :]
                        then(v.tensor_tensor(bad_r[:, 0, :], last, first, ALU.subtract))
                        then(v.tensor_scalar(bad_r[:, 0, :], bad_r[:, 0, :], float(W - 1), None, ALU.is_gt))
                        v.tensor_tensor(bad_r[:, 1, 0:NG - 1], last[:, 0:NG - 1], first[:, 1:NG], ALU.is_gt)
                        then(v.tensor_tensor(bad_r[:, 2, 0:NG - 2], last[:, 0:NG - 2], first[:, 2:NG], ALU.is_ge))
                        then(v.tensor_reduce(bad_s[:, 0:1], bad_r[:, :, :], AX.XY, ALU.add))
                        v.wait_ge(counted, 1)
                        then(v.tensor_tensor(bad_s[:, 1:2], bad_s[:, 0:1], p_n[:, :], ALU.add))
                        then(v.tensor_scalar(row[:, NG:NG + 1], bad_s[:, 1:2], 0.0, None, ALU.is_gt))
                        then(v.tensor_copy(self.general[:, :], row[:, NG:NG + 1]))
                        then(v.tensor_scalar(bad_s[:, 2:3], row[:, NG:NG + 1], -1.0, 1.0, ALU.mult, ALU.add))
                        then(v.tensor_scalar(row[:, 0:NG], first, bad_s[:, 2:3], None, ALU.mult))
                        v.tensor_copy(self.base_first[:, :], row[:, 0:NG]).then_inc(rowed, 1)
                        v.wait_ge(counted, 3)
                        v.tensor_copy(row_b[:, :], p_row[:, :])
                        then(v.tensor_copy(fcol[:, :], p_col[:, :]))
                        then(v.tensor_scalar(self.shift[:, :], row_b[:, NG:NG + 1], float(W), None, ALU.mult))
                        v.tensor_scalar(dst_l[:, :], dst_f[:, :], fcol[:, 0:1], None, ALU.subtract).then_inc(spread, 1)

                    @block.tensor
                    def _(t):
                        t.wait_ge(step, 3)
                        nc.tensor.matmul(p_n[:, :], bad_n[:, :], self.ones[0:NG, 0:1], start=True, stop=True).then_inc(counted, 1)
                        t.wait_ge(rowed, 1)
                        nc.tensor.matmul(p_row[:, :], self.ones[0:1, :], row[:, :], start=True, stop=True).then_inc(counted, 1)
                        nc.tensor.matmul(p_col[:, :], row[:, 0:NG], self.ones[0:1, 0:1], start=True, stop=True).then_inc(counted, 1)

                    @block.sync
                    def _(s):
                        s.wait_ge(spread, 2)
                        s.dma_start(self.dst_d, dst_l[:, :]).then_inc(stored, 16)
                        s.wait_ge(stored, 16)

            turned = sem("turned", ctx)
            taken = sem("taken", ctx)
            vstep = sem("dir_step", ctx)
            rooted = sem("rooted", ctx)
            with ExitStack() as pctx:
                p_t = [ps(f"p_t{n}", [P, CH, P], pctx) for n in range(4)]
                nrm = sb("nrm", [P, NG, CH], F32, pctx)
                sqv = sb("sqv", [P, NG, CH, 3], F32, pctx)
                vec_t = sb("vec_t", [P, NG, CH, 3], F32, pctx)
                vec_v = vec_r[:, :].rearrange("g (e c) -> g c e", c=3)
                jobs = [("src", lambda q: src_f[:, q * P:(q + 1) * P]), ("dst", lambda q: dst_f[:, q * P:(q + 1) * P]),
                        ("w", lambda q: w_r[:, q * P:(q + 1) * P])]
                jobs += [(c, lambda q, c=c: vec_v[:, c, q * P:(q + 1) * P]) for c in range(3)]
                with nc.Block() as block:
                    @block.tensor
                    def _(t):
                        for n, (_, part) in enumerate(jobs):
                            wait(t, taken, n - 3)
                            for q in range(CH):
                                last = nc.tensor.transpose(p_t[n % 4][:, q, 0:NG], part(q), self.ident[0:NG, 0:NG])
                            last.then_inc(turned, 1)
                        t.wait_ge(taken, 3)
                        for h in range(2):
                            last = nc.tensor.transpose(p_t[2][:, h, :], l0_n[:, h * P:(h + 1) * P], self.ident[:, :])
                        last.then_inc(turned, 1)
                        t.wait_ge(taken, 4)
                        for h in range(2):
                            nc.tensor.transpose(p_t[3][:, h, :], self.g_w[0][:, h * P:(h + 1) * P], self.ident[:, :])
                            last = nc.tensor.transpose(p_t[3][:, 2 + h, 0:HID], self.g_w[1][:, h * P:(h + 1) * P],
                                                       self.ident[0:HID, 0:HID])
                        last.then_inc(turned, 1)
                        t.wait_ge(taken, 9)
                        for l, k in ((0, D), (1, HID)):
                            for h in range(2):
                                last = nc.tensor.matmul(p_t[l][0:k, 0, 0:8], wt[:, l, h, 0:k], a_m[:, l, h, :],
                                                        start=(h == 0), stop=(h == 1))
                        last.then_inc(turned, 1)

                    @block.vector
                    def _(v):
                        view = [p[:, :, 0:NG].rearrange("p q g -> p g q") for p in p_t]
                        v.wait_ge(turned, 1)
                        v.tensor_copy(self.src_t[:, :, :], view[0]).then_inc(taken, 1)
                        v.wait_ge(turned, 2)
                        v.tensor_tensor(self.dst_t[:, :, :], view[1],
                                        row_b[:, 0:NG].unsqueeze(2).to_broadcast([P, NG, CH]), ALU.subtract).then_inc(taken, 1)
                        v.wait_ge(turned, 3)
                        v.tensor_copy(self.w_t[:, :, :], view[2]).then_inc(taken, 1)
                        for c in range(3):
                            v.wait_ge(turned, 4 + c)
                            v.tensor_copy(vec_t[:, :, :, c], view[(3 + c) % 4]).then_inc(taken, 1)
                        v.wait_ge(turned, 7)
                        v.tensor_copy(self.l0_w[:, :, :], p_t[2][:, 0:2, :]).then_inc(taken, 1)
                        v.wait_ge(turned, 8)
                        v.tensor_copy(wt[:, 0, :, :], p_t[3][:, 0:2, :]).then_inc(taken, 1)
                        v.tensor_copy(wt[:, 1, :, 0:HID], p_t[3][:, 2:4, 0:HID]).then_inc(taken, 1)
                        then = Chain(v, vstep)
                        v.wait_ge(taken, 9)
                        then(v.tensor_tensor(sqv[:, :, :, :], vec_t[:, :, :, :], vec_t[:, :, :, :], ALU.mult))
                        then(v.tensor_reduce(nrm[:, :, :], sqv[:, :, :, :], AX.X, ALU.add))
                        then(v.tensor_scalar(nrm[:, :, :], nrm[:, :, :], MIN_NORM2, None, ALU.max))
                        v.wait_ge(rooted, 1)
                        then(v.tensor_scalar(nrm[:, :, :], nrm[:, :, :], 1e-12, None, ALU.add))
                        then(v.reciprocal(nrm[:, :, :], nrm[:, :, :]))
                        v.tensor_tensor(self.dir_t[:, :, :, :], vec_t[:, :, :, :],
                                        nrm[:, :, :].unsqueeze(3).to_broadcast([P, NG, CH, 3]), ALU.mult)
                        v.wait_ge(turned, 9)
                        v.tensor_copy(self.g_a[0][:, :], p_t[0][:, 0, 0:8])
                        v.tensor_copy(self.g_a[1][:, :], p_t[1][0:HID, 0, 0:8])
                        v.tensor_scalar(m0s[:, :], m0r[:, :], float(NBAS) ** 0.5, None, ALU.mult)
                        v.tensor_scalar(self.up[:, :], upr[:, :], float(MUL) ** -0.5, None, ALU.mult)
                        out_scale = float(2 * MUL) ** -0.5 / 16.0
                        v.tensor_scalar(self.outw[:, :, :], outr[:, :, :], out_scale, None, ALU.mult)

                    @block.scalar
                    def _(a):
                        a.wait_ge(vstep, 3)
                        nc.scalar.activation(nrm[:, :, :], nrm[:, :, :], ACT.Sqrt).then_inc(rooted, 1)

            clipped = sem("clipped", ctx)
            squared = sem("squared", ctx)
            bumped = sem("bumped", ctx)
            masked = sem("masked", ctx)
            emb_out = sem("emb_out", ctx)
            parted = sem("parted", ctx)
            left = sem("left", ctx)
            wparts = sem("weight_parts", ctx)
            with ExitStack() as pctx:
                w_c = sb("w_c", [NG, GE], F32, pctx)
                centre = sb("centre", [NG, NBAS], F32, pctx)
                emb = sb("emb", [NG, NBAS, GE], F32, pctx)
                parts = sb("emb_parts", [NG, PARTS, NBAS, GE], BF16, pctx)
                with nc.Block() as block:
                    @block.vector
                    def _(v):
                        for k in range(NBAS):
                            v.memset(centre[:, k:k + 1], -float(k))
                        v.tensor_scalar(w_c[:, :], w_r[:, :], 0.0, 1.0, ALU.max, ALU.min).then_inc(clipped, 1)
                        for lo, h in ((64, 0), (0, 1), (64, 1)):
                            v.tensor_scalar(self.outw[lo:lo + MUL, h, :], self.outw[lo:lo + MUL, h, :],
                                            3.0 ** 0.5, None, ALU.mult)
                        then = Chain(v, wparts)
                        for whole, part, rest in ((m0s, m0p, m0l), (m2r, m2p, m2l)):
                            now = whole[:, :]
                            for k in range(PARTS):
                                then(v.tensor_copy(part[:, k, :], now))
                                if k < PARTS - 1:
                                    then(v.tensor_tensor(rest[:, k, :], now, part[:, k, :], ALU.subtract))
                                    now = rest[:, k, :]
                        for k in range(NBAS + 1):
                            if k < NBAS:
                                v.wait_ge(bumped, k + 1)
                                v.scalar_tensor_tensor(emb[:, k, :], w_r[:, :], 1.0, emb[:, k, :],
                                                       ALU.is_le, ALU.mult).then_inc(masked, 1)
                            for n in range(2 if k else 0):
                                v.wait_ge(parted, 2 * (k - 1) + n + 1)
                                if n == 0:
                                    v.tensor_tensor(emb[:, k - 1, :], emb[:, k - 1, :], parts[:, 0, k - 1, :],
                                                    ALU.subtract).then_inc(left, 1)
                                else:
                                    v.tensor_tensor(parts[:, 2, k - 1, :], emb[:, k - 1, :], parts[:, 1, k - 1, :],
                                                    ALU.subtract).then_inc(left, 1)

                    @block.scalar
                    def _(a):
                        a.wait_ge(clipped, 1)
                        for k in range(NBAS):
                            nc.scalar.activation(emb[:, k, :], w_c[:, :], ACT.Square, scale=float(NBAS - 1),
                                                 bias=centre[:, k:k + 1]).then_inc(squared, 1)
                        for k in range(NBAS):
                            a.wait_ge(squared, k + 1)
                            nc.scalar.activation(emb[:, k, :], emb[:, k, :], ACT.Exp, scale=-0.5).then_inc(bumped, 1)
                        for k in range(NBAS):
                            a.wait_ge(masked, k + 1)
                            nc.scalar.activation(parts[:, 0, k, :], emb[:, k, :], ACT.Copy).then_inc(parted, 1)
                            a.wait_ge(left, 2 * k + 1)
                            nc.scalar.activation(parts[:, 1, k, :], emb[:, k, :], ACT.Copy).then_inc(parted, 1)

                    @block.sync
                    def _(s):
                        n = 0
                        s.wait_ge(wparts, 2 * SPLIT)
                        for g in range(2):
                            for t, (_, part) in enumerate(MEET):
                                r = (g * TERMS + t) * NBAS
                                n += 16
                                s.dma_start(self.m_w0[r:r + NBAS, g * 64:g * 64 + 64], m0p[:, part, :]).then_inc(emb_out, 16)
                        for part in range(PARTS):
                            for q in range(CH):
                                n += 16
                                s.dma_start(self.m_b2[part:part + 1, q, :], m2p[:, part, :]).then_inc(emb_out, 16)
                        s.wait_ge(left, 2 * NBAS)
                        s.dma_start(self.emb_d, parts[:, :, :, :]).then_inc(emb_out, 16)
                        s.wait_ge(emb_out, n + 16)
            self.zero([cleared, consts, loaded, step, counted, rowed, spread, stored, turned, taken, vstep, rooted,
                       clipped, squared, bumped, masked, emb_out, parted, left, wparts])

    def clear(self, name, cells):
        nc = self.nc
        with nc.Block() as block:
            @block.vector
            def _(v):
                v.tensor_copy(self.iota_now[:, :], self.iota[:, :])
                v.tensor_copy(self.node_now[:, :], self.node_of_row[:, :])
                v.tensor_copy(self.base_now[:, :], self.base_first[:, :])
                for ap, value in cells:
                    v.memset(ap, value)

    def advance(self, v, done, n):
        v.wait_ge(done, n)
        v.tensor_scalar(self.iota_now[:, :], self.iota_now[:, :], self.shift[:, 0:1], None, ALU.add)
        v.tensor_scalar(self.node_now[:, :], self.node_now[:, :], self.shift[:, 0:1], None, ALU.add)
        v.tensor_scalar(self.base_now[:, :], self.base_now[:, :], self.shift[0:1, 0:1], None, ALU.add)

    def zero(self, sems):
        nc = self.nc
        ids = sorted(s.num for s in sems)
        while ids:
            n = 1
            while n < len(ids) and ids[n] == ids[0] + n:
                n += 1
            nc.gpsimd.sem_clear(range(ids[0], ids[0] + n))
            ids = ids[n:]
        nc.all_engine_barrier()

    def rounds(self, sems, body):
        with self.nc.Fori(0, self.is_general * (ROUNDS - 1) + 1):
            body()
            self.nc.gpsimd.dma_reset(range(self.landed[0].num, self.landed[-1].num + 1))
            self.zero(sems + self.landed)

    def gather(self, g, slots, table, width, rows, idx, s):
        def step(k, slot, turn):
            wait(g, s["used"], k - slots + 1)
            g.tensor_copy(idx[:, slot, :], self.src_t[:, bass.ds(k, 1), :].rearrange("p a q -> p (a q)")).then_inc(s["idx"], 1)
            g.wait_ge(s["idx"], k + 1)
            g.sem_inc(s["turn"], 1)
            for q in range(CH):
                g.indirect_dma_start(rows[:, slot, q, 0:width], None, table,
                                     bass.IndirectOffsetOnAxis(ap=idx[:, slot, q:q + 1], axis=0)).then_inc(s["rows"][slot], 16)
        return step

    def window(self, v, k):
        return v.value_load(self.base_now[0:1, bass.ds(k, 1)], min_val=0, max_val=NP - W)

    def onehot(self, k):
        a = self.iota_now[:, :].unsqueeze(1).to_broadcast([P, CH, W])
        b = self.dst_t[:, bass.ds(k, 1), :].rearrange("p a q -> p (a q)").unsqueeze(2).to_broadcast([P, CH, W])
        return a, b

    def sum_edges(self, name, table, weighted):
        nc = self.nc
        U = 4
        with ExitStack() as ctx:
            rows = self.sb(name + "rows", [P, U, CH, D], F32, ctx)
            idx = self.sb(name + "idx", [P, U, CH], I32, ctx)
            sel = self.sb(name + "sel", [P, U, CH, W], F32, ctx)
            p_s = [self.ps(f"{name}p{n}", [P, 512], ctx) for n in range(2)]
            s = {k: self.sem(name + k, ctx) for k in ("idx", "turn", "sel0", "sel", "used", "added")}
            landed = self.landed[0:U]
            s["rows"] = landed
            acc = self.acc[:, 0:NP]
            cells = [(acc, 0.0)] + ([(self.den[0:1, :], 0.0)] if weighted else [])
            self.clear(name, cells)

            def body():
                with nc.Block() as block:
                    @block.gpsimd
                    def _(g):
                        pipeline(g, U, [(0, self.gather(g, U, table, D, rows, idx, s))])

                    @block.tensor
                    def _(t):
                        def step(k, slot, turn):
                            t.wait_ge(s["sel"], k + 1)
                            wait(t, s["added"], k - 1)
                            t.wait_ge(landed[slot], (turn + 1) * 16 * CH)
                            p = p_s[slot % 2]
                            for q in range(CH):
                                last = nc.tensor.matmul(p[:, 0:W], rows[:, slot, q, :], sel[:, slot, q, :],
                                                        start=(q == 0), stop=(q == CH - 1))
                            if weighted:
                                for q in range(CH):
                                    last = nc.tensor.matmul(p[0:1, W:2 * W], self.ones[:, 0:1], sel[:, slot, q, :],
                                                            start=(q == 0), stop=(q == CH - 1))
                            last.then_inc(s["used"], 1)
                        pipeline(t, U, [(0, step)])

                    @block.vector
                    def _(v):
                        def select(k, slot, turn):
                            wait(v, s["used"], k - U + 1)
                            a, b = self.onehot(k)
                            if not weighted:
                                v.tensor_tensor(sel[:, slot, :, :], a, b, ALU.is_equal).then_inc(s["sel"], 1)
                                return
                            v.tensor_tensor(sel[:, slot, :, :], a, b, ALU.is_equal).then_inc(s["sel0"], 1)
                            v.wait_ge(s["sel0"], k + 1)
                            w = self.w_t[:, bass.ds(k, 1), :].rearrange("p a q -> p (a q)").unsqueeze(2).to_broadcast([P, CH, W])
                            v.tensor_tensor(sel[:, slot, :, :], sel[:, slot, :, :], w, ALU.mult).then_inc(s["sel"], 1)

                        def add(k, slot, turn):
                            base = self.window(v, k)
                            v.wait_ge(s["used"], k + 1)
                            wait(v, s["added"], k)
                            at = bass.ds(base, W)
                            if weighted:
                                v.tensor_tensor(self.den[0:1, at], self.den[0:1, at], p_s[slot % 2][0:1, W:2 * W], ALU.add)
                            v.tensor_tensor(acc[:, at], acc[:, at], p_s[slot % 2][:, 0:W], ALU.add).then_inc(s["added"], 1)
                        pipeline(v, U, [(0, select), (1, add)])
                        self.advance(v, s["added"], NG)
            self.rounds([x for k, x in s.items() if k != "rows"], body)

    def product_edges(self):
        nc = self.nc
        U = 8
        with ExitStack() as ctx:
            sb, ps, sem = self.sb, self.ps, self.sem
            rows = sb("tp_rows", [P, U, CH, D], F32, ctx)
            idx = sb("tp_idx", [P, U, CH], I32, ctx)
            sel = sb("tp_sel", [P, U, CH, W], F32, ctx)
            emb = sb("tp_emb", [2 * TERMS * NBAS, U // 2, GE], BF16, ctx)
            h0 = sb("tp_h0", [P, 2, GE], F32, ctx)
            h1 = sb("tp_h1", [P, 2, GE], F32, ctx)
            msg = sb("tp_msg", [P, 2, CH, 2 * P], F32, ctx)
            u = sb("tp_u", [P, 2, CH, MUL], F32, ctx)
            vy = sb("tp_vy", [P, 2, CH, 3, MUL], F32, ctx)
            dot = sb("tp_dot", [P, 2, CH, MUL], F32, ctx)
            p_h0 = ps("tp_p0", [P, GE], ctx)
            p_h1 = ps("tp_p1", [P, GE], ctx)
            p_w = [ps(f"tp_pw{n}", [P, CH, 2, 4 * MUL], ctx) for n in range(2)]
            p_s = [ps(f"tp_ps{n}", [P, 512], ctx) for n in range(2)]
            names = ("idx", "turn", "hid0", "hid1", "act0", "act1", "coef", "sel", "parts", "msgs", "used", "added", "summed")
            s = {k: sem("tp_" + k, ctx) for k in names}
            landed = self.landed[0:U]
            emb_in = [sem(f"tp_emb{n}", ctx) for n in range(U // 2)]
            s["rows"] = landed
            acc = self.acc[:, 0:2 * NP].rearrange("p (h n) -> p h n", h=2)
            self.clear("tp", [(acc, 0.0)])

            def pairs(step):
                def at(k, slot, turn):
                    if slot % 2 == 0:
                        step(turn * (U // 2) + slot // 2, k, slot // 2, turn)
                return at

            def body():
                with nc.Block() as block:
                    @block.gpsimd
                    def _(g):
                        g_s = dict(s, used=s["msgs"])
                        pipeline(g, U, [(0, self.gather(g, U, self.up_d, D, rows, idx, g_s))])

                    @block.sync
                    def _(e):
                        def load(pair, k, slot, turn):
                            wait(e, s["hid0"], pair - U // 2 + 1)
                            for g in range(2):
                                row = g * TERMS * NBAS
                                for part in range(PARTS):
                                    m = sum(p == part for p, _ in MEET)
                                    e.dma_start(emb[row:row + m * NBAS, slot, :], self.emb_d[bass.ds(k + g, 1), part, :, :]
                                                .to_broadcast([m, NBAS, GE]) if m > 1 else
                                                self.emb_d[bass.ds(k + g, 1), part, :, :].rearrange("a b e -> (a b) e"))\
                                        .then_inc(emb_in[slot], 16)
                                    row += m * NBAS
                        pipeline(e, U, [(0, pairs(load))])

                    @block.tensor
                    def _(t):
                        def hidden0(pair, k, slot, turn):
                            t.wait_ge(emb_in[slot], (turn + 1) * (16 * 2 * PARTS))
                            wait(t, s["act0"], pair)
                            nc.tensor.matmul(p_h0[:, :], self.m_w0[:, :], emb[:, slot, :], start=True, stop=True).then_inc(s["hid0"], 1)

                        def hidden1(pair, k, slot, turn):
                            t.wait_ge(s["act0"], pair + 1)
                            wait(t, s["act1"], pair)
                            nc.tensor.matmul(p_h1[:, :], self.m_w1[:, :], h0[:, slot % 2, :], start=True, stop=True).then_inc(s["hid1"], 1)

                        def coefs(pair, k, slot, turn):
                            t.wait_ge(s["act1"], pair + 1)
                            wait(t, s["msgs"], k - 2)
                            p = p_w[slot % 2]
                            for q in range(0, CH, 2):
                                nc.tensor.matmul(p[:, q:q + 2, :, :].rearrange("p q g n -> p (q g n)"), self.ones_h[:, :],
                                                 self.m_b2[:, :, :].rearrange("p q n -> p (q n)"), start=True, stop=False)
                            for q in range(CH):
                                last = nc.tensor.matmul(p[:, q, :, :].rearrange("p g n -> p (g n)"),
                                                        h1[:, slot % 2, q * P:(q + 1) * P],
                                                        self.m_w2[:, :, :].rearrange("p g n -> p (g n)"), start=False, stop=(q % 2 == 1))
                            last.then_inc(s["coef"], 1)

                        def total(k, slot, turn):
                            t.wait_ge(s["msgs"], k + 1)
                            wait(t, s["added"], k - 1)
                            for h in range(2):
                                for q in range(CH):
                                    last = nc.tensor.matmul(p_s[slot % 2][:, h * W:(h + 1) * W],
                                                            msg[:, slot % 2, q, h * P:(h + 1) * P], sel[:, slot, q, :],
                                                            start=(q == 0), stop=(q == CH - 1))
                            last.then_inc(s["summed"], 1)
                        pipeline(t, U, [(0, pairs(hidden0)), (1, pairs(hidden1)), (2, pairs(coefs)), (4, total)])

                    @block.scalar
                    def _(a):
                        def silu0(pair, k, slot, turn):
                            a.wait_ge(s["hid0"], pair + 1)
                            wait(a, s["hid1"], pair - 1)
                            nc.scalar.activation(h0[:, slot % 2, :], p_h0[:, :], ACT.Silu, bias=self.m_b0[:, 0:1]).then_inc(s["act0"], 1)

                        def silu1(pair, k, slot, turn):
                            a.wait_ge(s["hid1"], pair + 1)
                            wait(a, s["coef"], pair - 1)
                            nc.scalar.activation(h1[:, slot % 2, :], p_h1[:, :], ACT.Silu, bias=self.m_b1[:, 0:1]).then_inc(s["act1"], 1)
                        pipeline(a, U, [(0, pairs(silu0)), (1, pairs(silu1))])

                    @block.vector
                    def _(v):
                        def select(k, slot, turn):
                            wait(v, s["summed"], k - U + 1)
                            a, b = self.onehot(k)
                            v.tensor_tensor(sel[:, slot, :, :], a, b, ALU.is_equal).then_inc(s["sel"], 1)

                        def messages(k, slot, turn):
                            h = slot % 2
                            v.wait_ge(landed[slot], (turn + 1) * 16 * CH)
                            v.wait_ge(s["coef"], turn * (U // 2) + slot // 2 + 1)
                            wait(v, s["summed"], k - 1)
                            v.wait_ge(s["sel"], k + 1)
                            p = p_w[slot // 2 % 2][:, :, h, :]
                            ss, vv = rows[:, slot, :, 0:MUL], rows[:, slot, :, MUL:].rearrange("p q (c m) -> p q c m", c=3)
                            y = self.dir_t[:, bass.ds(k, 1), :, :].rearrange("p a q c -> p (a q) c").unsqueeze(3)\
                                .to_broadcast([P, CH, 3, MUL])
                            v.tensor_tensor(msg[:, h, :, 0:MUL], p[:, :, 0:MUL], ss, ALU.mult)
                            v.tensor_tensor(u[:, h, :, :], p[:, :, MUL:2 * MUL], ss, ALU.mult).then_inc(s["parts"], 1)
                            v.tensor_tensor(vy[:, h, :, :, :], vv, y, ALU.mult).then_inc(s["parts"], 1)
                            cols = {0: 3 * MUL, 1: 5 * MUL, 2: 7 * MUL}
                            for c in range(3):
                                v.tensor_tensor(msg[:, h, :, cols[c]:cols[c] + MUL], p[:, :, 2 * MUL:3 * MUL],
                                                vv[:, :, c, :], ALU.mult)
                            v.wait_ge(s["parts"], 4 * k + 2)
                            v.tensor_tensor(dot[:, h, :, :], vy[:, h, :, 0, :], vy[:, h, :, 1, :], ALU.add).then_inc(s["parts"], 1)
                            for c in range(3):
                                v.tensor_tensor(msg[:, h, :, cols[c] - MUL:cols[c]], u[:, h, :, :], y[:, :, c, :], ALU.mult)
                            v.wait_ge(s["parts"], 4 * k + 3)
                            v.tensor_tensor(dot[:, h, :, :], dot[:, h, :, :], vy[:, h, :, 2, :], ALU.add).then_inc(s["parts"], 1)
                            v.wait_ge(s["parts"], 4 * k + 4)
                            v.tensor_tensor(msg[:, h, :, MUL:2 * MUL], p[:, :, 3 * MUL:4 * MUL], dot[:, h, :, :], ALU.mult).then_inc(s["msgs"], 1)

                        def add(k, slot, turn):
                            base = self.window(v, k)
                            v.wait_ge(s["summed"], k + 1)
                            wait(v, s["added"], k)
                            at = bass.ds(base, W)
                            v.tensor_tensor(acc[:, :, at], acc[:, :, at],
                                            p_s[slot % 2][:, 0:2 * W].rearrange("p (h n) -> p h n", h=2), ALU.add).then_inc(s["added"], 1)
                        pipeline(v, U, [(0, select), (0, messages), (1, add)])
                        self.advance(v, s["added"], NG)
            self.rounds([x for k, x in s.items() if k != "rows"] + emb_in, body)

    def attend_edges(self, l, table, dim):
        nc = self.nc
        U = 8
        width = dim + SCW
        sc = dim + SC
        with ExitStack() as ctx:
            sb, ps, sem = self.sb, self.ps, self.sem
            n = f"at{l}_"
            rows = sb(n + "rows", [P, U, CH, width], F32, ctx)
            idx = sb(n + "idx", [P, U, CH], I32, ctx)
            dst_b = sb(n + "dst_b", [P, 4, GE], F32, ctx)
            node_w = sb(n + "node_w", [W, 4, SCP // 2], F32, ctx)
            hot_t = sb(n + "hot_t", [P, U, GE], BF16, ctx)
            mask = sb(n + "mask", [P, 2, GE], F32, ctx)
            cand = sb(n + "cand", [P, 2, GE], F32, ctx)
            best = sb(n + "best", [P, 2, 2], F32, ctx)
            top_w = sb(n + "top_w", [2, 2, 2, W], F32, ctx)
            rest = sb(n + "rest", [W, 2, HEADS], F32, ctx)
            look = sb(n + "look", [P, 2, CH, SC], F32, ctx)
            zz = sb(n + "zz", [P, 2, 2, CH, HEADS], F32, ctx)
            zl = sb(n + "zl", [P, 2, 2, CH, HEADS], F32, ctx)
            dz = sb(n + "dz", [P, 2, CH, HEADS], F32, ctx)
            prob = sb(n + "prob", [P, 4, CH, HEADS], F32, ctx)
            sel = sb(n + "sel", [P, 4, CH, W], F32, ctx)
            psel = sb(n + "psel", [P, 2, CH, HEADS, W], F32, ctx)
            p_b = [ps(f"{n}pb{b}", [P, GE], ctx) for b in range(2)]
            p_e = ps(n + "pe", [SCP, GE], ctx, BF16)
            esr = sb(n + "esr", [P, 2, GE], BF16, ctx)
            p_m = ps(n + "pm", [2, P], ctx)
            p_l = ps(n + "pl", [P, CH, PARTS, SC], ctx)
            p_s = [ps(f"{n}ps{a}", [P, 512], ctx) for a in range(2)]
            turned_best = p_m[:, :]
            p_w = ps(n + "pw", [W, 4], ctx)
            names = ("idx", "turn", "spread", "hot", "mask", "cand", "bestt", "merged", "topw", "topt",
                     "part", "nodew", "looked", "look", "z", "dz", "prob", "sel", "psel_v", "psel_a", "used", "added", "est", "esr", "go_v", "go_t")
            s = {k: sem(n + k, ctx) for k in names}
            landed = self.landed[0:U]
            dst_in = [sem(f"{n}dst{a}", ctx) for a in range(4)]
            sc_in = [sem(f"{n}sc{a}", ctx) for a in range(4)]
            s["rows"] = landed
            acc = self.acc[:, :].rearrange("p (h n) -> p h n", h=HEADS)
            VQ = 2

            def body():
                with nc.Block() as block:
                    @block.gpsimd
                    def _(g):
                        pipeline(g, U, [(0, self.gather(g, U, table[0:N, :], width, rows, idx, s))])

                    @block.sync
                    def _(e):
                        def load(k, slot, turn):
                            b = slot % 4
                            wait(e, s["hot"], k - 3)
                            wait(e, s["looked"], k - 3)
                            e.dma_start(dst_b[:, b, :], self.dst_d[bass.ds(k, 1), :].to_broadcast([P, GE])).then_inc(dst_in[b], 16)
                            base = e.value_load(self.base_now[0:1, bass.ds(k, 1)], min_val=0, max_val=NP - W)
                            e.dma_start(node_w[:, b, :], table[bass.ds(base, W), sc:width]).then_inc(sc_in[b], 16)
                        pipeline(e, U, [(0, load)])

                    @block.tensor
                    def _(t):
                        def turn_es(k, slot, turn):
                            t.wait_ge(landed[slot], (turn + 1) * 16 * CH)
                            wait(t, s["esr"], k)
                            for q in range(CH):
                                last = nc.tensor.transpose(p_e[:, q * P:(q + 1) * P],
                                                           rows[:, slot, q, sc:width].bitcast(BF16), self.ident_h[:, :])
                            last.then_inc(s["est"], 1)

                        def spread(k, slot, turn):
                            t.wait_ge(s["esr"], k + 1)
                            wait(t, s["cand"], 2 * k)
                            for b in range(2):
                                last = nc.tensor.matmul(p_b[b][:, :], self.pick[:, b, :], esr[:, slot % 2, :], start=True, stop=True)
                            last.then_inc(s["spread"], 1)

                        def turn_best(k, slot, turn):
                            t.wait_ge(s["cand"], 2 * k + 2)
                            wait(t, s["merged"], k)
                            nc.tensor.transpose(turned_best, best[:, slot % 2, :], self.ident[:, :]).then_inc(s["bestt"], 1)

                        def turn_top(k, slot, turn):
                            t.wait_ge(s["topw"], k + 1)
                            wait(t, s["nodew"], k)
                            t.sem_inc(s["go_t"], 1)
                            for h in range(2):
                                last = nc.tensor.transpose(p_w[:, 2 * h:2 * h + 2], top_w[:, slot % 2, h, :], self.ident[0:2, 0:2])
                            last.then_inc(s["topt"], 1)

                        def lookup(k, slot, turn):
                            t.wait_ge(s["nodew"], k + 1)
                            wait(t, s["look"], k)
                            for q in range(CH):
                                last = nc.tensor.matmul(p_l[:, q, :, :].rearrange("p a o -> p (a o)"),
                                                        hot_t[0:W, slot, q * P:(q + 1) * P],
                                                        node_w[:, slot % 4, :].bitcast(BF16), start=True, stop=True)
                            last.then_inc(s["looked"], 1)

                        def total(k, slot, turn):
                            t.wait_ge(s["psel_v"], k + 1)
                            t.wait_ge(s["psel_a"], k + 1)
                            wait(t, s["added"], k - 1)
                            p = p_s[slot % 2]
                            for q in range(CH):
                                nc.tensor.matmul(p[0:dim, 0:HEADS * W], rows[:, slot, q, 0:dim],
                                                 psel[:, slot % 2, q, :, :].rearrange("p h n -> p (h n)"),
                                                 start=(q == 0), stop=(q == CH - 1))
                            for q in range(CH):
                                last = nc.tensor.matmul(p[0:HEADS, HEADS * W:(HEADS + 1) * W], prob[:, slot % 4, q, :],
                                                        sel[:, slot % 4, q, :], start=(q == 0), stop=(q == CH - 1))
                            last.then_inc(s["used"], 1)
                        pipeline(t, U, [(1, spread), (3, turn_top), (6, total), (0, turn_es), (3, lookup), (1, turn_best)])

                    @block.scalar
                    def _(a):
                        def es_rows(k, slot, turn):
                            a.wait_ge(s["est"], k + 1)
                            wait(a, s["spread"], k - 1)
                            nc.scalar.activation(esr[0:SCP, slot % 2, :], p_e[:, :], ACT.Copy).then_inc(s["esr"], 1)

                        def masks(k, slot, turn):
                            a.wait_ge(s["hot"], k + 1)
                            wait(a, s["cand"], 2 * (k - 1))
                            nc.scalar.activation(mask[:, slot % 2, :], hot_t[:, slot, :], ACT.Copy,
                                                 scale=BIG, bias=-BIG).then_inc(s["mask"], 1)

                        def weigh(k, slot, turn):
                            a.wait_ge(s["dz"], k + 1)
                            wait(a, s["used"], k - 3)
                            nc.scalar.activation(prob[:, slot % 4, :, :], dz[:, slot % 2, :, :], ACT.Exp).then_inc(s["prob"], 1)

                        def weigh_rest(k, slot, turn):
                            a.wait_ge(s["prob"], k + 1)
                            a.wait_ge(s["sel"], k + 1)
                            wait(a, s["used"], k - 1)
                            for q in range(VQ, CH):
                                for o in range(HEADS):
                                    last = nc.scalar.activation(psel[:, slot % 2, q, o, :], sel[:, slot % 4, q, :], ACT.Copy,
                                                                scale=prob[:, slot % 4, q, o:o + 1])
                            last.then_inc(s["psel_a"], 1)
                        pipeline(a, U, [(5, weigh_rest), (0, masks), (4, weigh), (0, es_rows)])

                    @block.vector
                    def _(v):
                        def hot(k, slot, turn):
                            b = slot % 4
                            v.wait_ge(dst_in[b], (2 * turn + slot // 4 + 1) * 16)
                            wait(v, s["looked"], k - U + 1)
                            wait(v, s["mask"], k - U + 1)
                            v.tensor_scalar(hot_t[:, slot, :], dst_b[:, b, :], self.node_now[:, 0:1], None, ALU.is_equal).then_inc(s["hot"], 1)

                        def largest(b):
                            def step(k, slot, turn):
                                if b == 0:
                                    v.wait_ge(s["mask"], k + 1)
                                    v.wait_ge(s["spread"], k + 1)
                                    wait(v, s["bestt"], k - 1)
                                    wait(v, s["cand"], 2 * k)
                                v.sem_inc(s["go_v"], 1)
                                v.tensor_tensor_reduce(out=cand[:, b, :], in0=p_b[b][:, :], in1=mask[:, slot % 2, :],
                                                       scale=1.0, scalar=-BIG, op0=ALU.add, op1=ALU.max,
                                                       accum_out=best[:, slot % 2, b:b + 1]).then_inc(s["cand"], 1)
                            return step

                        first = [v.alloc_register(f"{n}first{a}") for a in range(U)]

                        def place(k, slot, turn):
                            v.reg_load(first[slot], self.base_now[0:1, bass.ds(k, 1)])

                        def merge(k, slot, turn):
                            base = v.snap(first[slot], min_val=0, max_val=NP - W)
                            v.wait_ge(s["bestt"], k + 1)
                            wait(v, s["merged"], k)
                            at = bass.ds(base, W)
                            v.tensor_tensor(self.top[:, :, at], self.top[:, :, at],
                                            turned_best.rearrange("b (h n) -> b h n", h=2)[:, :, 0:W], ALU.max).then_inc(s["merged"], 1)

                        def take_top(k, slot, turn):
                            base = v.snap(first[slot], min_val=0, max_val=NP - W)
                            if isinstance(k, int) and k == NG - 1:
                                v.wait_ge(s["merged"], NG)
                            else:
                                v.wait_ge(s["merged"], k + 2)
                            wait(v, s["topt"], k - 1)
                            v.tensor_copy(top_w[:, slot % 2, :, :], self.top[:, :, bass.ds(base, W)]).then_inc(s["topw"], 1)

                        def part(n):
                            def step(k, slot, turn):
                                b, left = slot % 4, rest[:, slot % 2, :]
                                parts = node_w[:, b, :].bitcast(BF16)
                                if n == 0:
                                    v.wait_ge(sc_in[b], (2 * turn + slot // 4 + 1) * 16)
                                    v.wait_ge(s["topt"], k + 1)
                                    v.tensor_copy(parts[:, 0:HEADS], p_w[:, :]).then_inc(s["part"], 1)
                                    return
                                v.wait_ge(s["part"], 3 * k + n)
                                if n == 1:
                                    v.tensor_tensor(left, p_w[:, :], parts[:, 0:HEADS], ALU.subtract).then_inc(s["part"], 1)
                                elif n == 2:
                                    v.tensor_copy(parts[:, SC:SC + HEADS], left).then_inc(s["part"], 1)
                                else:
                                    v.tensor_tensor(parts[:, 2 * SC:2 * SC + HEADS], left, parts[:, SC:SC + HEADS],
                                                    ALU.subtract).then_inc(s["nodew"], 1)
                            return step

                        def score(n):
                            def step(k, slot, turn):
                                h = slot % 2
                                e, e_top, ed = zz[:, h, 0, :, :], zz[:, h, 1, :, :], look[:, h, :, HEADS:SC]
                                flat = [x[:, h, :, :, :].rearrange("p a q o -> p (a q o)") for x in (zz, zl)]
                                if n == 0:
                                    v.wait_ge(s["looked"], k + 1)
                                    v.tensor_reduce(look[:, h, :, :], p_l[:, :, :, :].rearrange("p q a o -> p q o a"),
                                                    AX.X, ALU.add).then_inc(s["look"], 1)
                                elif n == 1:
                                    v.wait_ge(s["look"], k + 1)
                                    wait(v, s["dz"], k)
                                    v.tensor_tensor(e, ed, rows[:, slot, :, dim:dim + HEADS], ALU.add)
                                    v.tensor_tensor(e_top, ed, look[:, h, :, 0:HEADS], ALU.add).then_inc(s["z"], 1)
                                elif n == 2:
                                    v.wait_ge(s["z"], 3 * k + 1)
                                    v.scalar_tensor_tensor(flat[1], flat[0], 0.2, flat[0], ALU.mult, ALU.max).then_inc(s["z"], 1)
                                elif n == 3:
                                    v.wait_ge(s["z"], 3 * k + 2)
                                    v.tensor_tensor(e, zl[:, h, 0, :, :], zl[:, h, 1, :, :], ALU.min).then_inc(s["z"], 1)
                                else:
                                    v.wait_ge(s["z"], 3 * k + 3)
                                    wait(v, s["prob"], k - 1)
                                    v.tensor_tensor(dz[:, h, :, :], e, zl[:, h, 1, :, :], ALU.subtract).then_inc(s["dz"], 1)
                            return step

                        def select(k, slot, turn):
                            wait(v, s["used"], k - 3)
                            a, b = self.onehot(k)
                            v.tensor_tensor(sel[:, slot % 4, :, :], a, b, ALU.is_equal).then_inc(s["sel"], 1)

                        def weigh(q):
                            def step(k, slot, turn):
                                if q == 0:
                                    v.wait_ge(s["prob"], k + 1)
                                    v.wait_ge(s["sel"], k + 1)
                                    wait(v, s["used"], k - 1)
                                last = v.tensor_tensor(psel[:, slot % 2, q, :, :],
                                                       sel[:, slot % 4, q, :].unsqueeze(1).to_broadcast([P, HEADS, W]),
                                                       prob[:, slot % 4, q, :].unsqueeze(2).to_broadcast([P, HEADS, W]), ALU.mult)
                                if q == VQ - 1:
                                    last.then_inc(s["psel_v"], 1)
                            return step

                        def add(k, slot, turn):
                            base = v.snap(first[slot], min_val=0, max_val=NP - W)
                            v.wait_ge(s["used"], k + 1)
                            wait(v, s["added"], k)
                            at = bass.ds(base, W)
                            p = p_s[slot % 2]
                            v.tensor_tensor(self.den[:, at], self.den[:, at], p[0:HEADS, HEADS * W:(HEADS + 1) * W], ALU.add)
                            v.tensor_tensor(acc[0:dim, :, at], acc[0:dim, :, at],
                                            p[0:dim, 0:HEADS * W].rearrange("p (h n) -> p h n", h=HEADS), ALU.add).then_inc(s["added"], 1)
                        pipeline(v, U, [(2, merge), (3, take_top), (5, weigh(0)), (4, score(0)), (3, part(0)), (5, weigh(1)),
                                        (4, score(1)), (3, part(1)), (0, hot), (4, score(2)), (3, part(2)), (4, select),
                                        (4, score(3)), (3, part(3)), (1, largest(0)), (4, score(4)), (1, largest(1)),
                                        (0, place), (7, add)])
                        self.advance(v, s["added"], NG)
            with nc.Fori(0, self.is_general + 1):
                self.clear(n, [(self.acc[0:dim, :], 0.0), (self.den[:, :], 0.0), (esr[:, :, :], 0.0)])
                self.rounds([x for k, x in s.items() if k != "rows"] + dst_in + sc_in, body)

    def norm(self, v, a_sem, then, x, width, tmp, st, root):
        nb = x.shape[0]
        full = [nb, JB, width]
        then(v.tensor_reduce(st[0:nb, 0, :], x, AX.X, ALU.add))
        then(v.tensor_scalar(st[0:nb, 0, :], st[0:nb, 0, :], 1.0 / width, None, ALU.mult))
        then(v.tensor_tensor(x, x, st[0:nb, 0, :].unsqueeze(2).to_broadcast(full), ALU.subtract))
        then(v.tensor_tensor(tmp, x, x, ALU.mult))
        then(v.tensor_reduce(st[0:nb, 1, :], tmp, AX.X, ALU.add))
        v.tensor_scalar(st[0:nb, 1, :], st[0:nb, 1, :], 1.0 / width, LN_EPS, ALU.mult, ALU.add).then_inc(a_sem, 1)
        root()
        then(v.reciprocal(st[0:nb, 1, :], st[0:nb, 1, :]))
        then(v.tensor_tensor(x, x, st[0:nb, 1, :].unsqueeze(2).to_broadcast(full), ALU.mult))

    def split(self, v, sem, start, tab, at, rest):
        then = Chain(v, sem, start)
        parts = tab[:, :, at + SC:at + SCW].bitcast(BF16)
        left = tab[:, :, at:at + SC]
        for k in range(PARTS):
            part = parts[:, :, k * SC:(k + 1) * SC]
            then(v.tensor_copy(part, left))
            if k < PARTS - 1:
                then(v.tensor_tensor(rest[:, k, :, :], left, part, ALU.subtract))
                left = rest[:, k, :, :]

    def node_rows(self, dram, t, width):
        return dram.rearrange("(t j p) f -> t p j f", j=JB, p=NB)[bass.ds(t, 1), :, :, :].rearrange("a p j f -> (a p) j f")

    def node_layer(self, n, kind, x_in):
        nc = self.nc
        with ExitStack() as ctx:
            sb, ps, sem = self.sb, self.ps, self.sem
            xs = sb(n + "xs", [NB, JB, D], F32, ctx)
            y = sb(n + "y", [NB, JB, D], F32, ctx)
            tmp = sb(n + "tmp", [NB, JB, D], F32, ctx)
            st = sb(n + "st", [P, 2, JB], F32, ctx)
            parts = 2 if kind == "product" else 1
            sums = sb(n + "sums", [P, parts, NS], F32, ctx)
            xt = sb(n + "xt", [P, JB, P], F32, ctx)
            tab = sb(n + "tab", [NB, JB, D + SCW], F32, ctx)
            rest = sb(n + "rest", [NB, 2, JB, SC], F32, ctx)
            p_x = ps(n + "px", [P, 8, P], ctx)
            p_y = ps(n + "py", [P, 8, P], ctx)
            p_z = ps(n + "pz", [P, 8, P], ctx)
            names = ("xin", "sumd", "turned", "xt", "lin", "var", "rooted", "step", "turned2", "xt2", "tabbed",
                     "tabd", "split", "sent")
            s = {k: sem(n + k, ctx) for k in names}
            SENT = 2
            LINKS = 8
            with nc.Block() as block:
                @block.sync
                def _(e):
                    def step(t):
                        wait(e, s["sent"], t * (16 * SENT))
                        e.dma_start(xs[:, :, :], self.node_rows(x_in, t, D)).then_inc(s["xin"], 16)
                        e.wait_ge(s["step"], (t + 1) * LINKS)
                        if kind == "sum":
                            e.dma_start(self.node_rows(self.x1_d, t, D), y[:, :, :]).then_inc(s["sent"], 16)
                            e.wait_ge(s["tabd"], t + 1)
                            e.dma_start(self.node_rows(self.up_d, t, D), tab[:, :, 0:D]).then_inc(s["sent"], 16)
                        else:
                            e.dma_start(self.node_rows(self.x2_d, t, D), y[:, :, :]).then_inc(s["sent"], 16)
                            e.wait_ge(s["split"], (t + 1) * SPLIT)
                            e.dma_start(self.node_rows(self.t_d[0][0:N, :], t, D + SCW), tab[:, :, :]).then_inc(s["sent"], 16)
                    each(e, step)
                    e.wait_ge(s["sent"], NT * 16 * SENT)

                @block.scalar
                def _(a):
                    def step(t):
                        wait(a, s["sent"], t * (16 * SENT))
                        nc.scalar.activation(sums[:, :, :], self.acc[:, 0:parts * NP].rearrange("p (h n) -> p h n", h=parts)
                                             [:, :, bass.ds(t * NS, NS)], ACT.Copy).then_inc(s["sumd"], 1)
                        if kind == "sum":
                            a.wait_ge(s["turned"], t + 1)
                            nc.scalar.activation(xt[:, :, 0:NB], p_x[:, 0:JB, 0:NB], ACT.Copy).then_inc(s["xt"], 1)
                        a.wait_ge(s["var"], t + 1)
                        nc.scalar.activation(st[0:NB, 1, :], st[0:NB, 1, :], ACT.Sqrt).then_inc(s["rooted"], 1)
                        a.wait_ge(s["turned2"], t + 1)
                        nc.scalar.activation(xt[:, :, 0:NB], p_z[:, 0:JB, 0:NB], ACT.Copy).then_inc(s["xt2"], 1)
                        a.wait_ge(s["tabbed"], t + 1)
                        if kind == "sum":
                            nc.scalar.activation(tab[:, :, 0:D], p_x[0:NB, 0:JB, :], ACT.Copy).then_inc(s["tabd"], 1)
                        else:
                            nc.scalar.activation(tab[:, :, 0:D], y[:, :, :], ACT.Copy)
                            nc.scalar.activation(tab[:, :, D:D + SC], p_x[0:NB, 0:JB, 0:SC], ACT.Copy)
                            for hh, p in enumerate((p_y, p_z)):
                                last = nc.scalar.activation(self.top[:, hh, bass.ds(t * NS, NS)].rearrange("b (j p) -> b j p", j=JB),
                                                            p[0:2, 0:JB, 0:NB], ACT.Copy)
                            last.then_inc(s["tabd"], 1)
                    each(a, step)

                @block.tensor
                def _(te):
                    def step(t):
                        te.wait_ge(s["xin"], (t + 1) * 16)
                        wait(te, s["tabd"], t)
                        if kind == "sum":
                            for j in range(JB):
                                last = nc.tensor.transpose(p_x[:, j, 0:NB], xs[:, j, :], self.ident[0:NB, 0:NB])
                            last.then_inc(s["turned"], 1)
                        te.wait_ge(s["sumd"], t + 1)
                        if kind == "sum":
                            te.wait_ge(s["xt"], t + 1)
                        for j in range(JB):
                            if kind == "sum":
                                nc.tensor.matmul(p_y[0:NB, j, :], xt[:, j, 0:NB], self.l0_w[:, 0, :], start=True, stop=False)
                                nc.tensor.matmul(p_y[0:NB, j, :], sums[:, 0, j * NB:(j + 1) * NB], self.l0_w[:, 1, :], start=False, stop=False)
                                last = nc.tensor.matmul(p_y[0:NB, j, :], self.ones[0:1, 0:NB], self.l0_b[:, :], start=False, stop=True)
                            else:
                                for h in range(2):
                                    last = nc.tensor.matmul(p_y[0:NB, j, :], sums[:, h, j * NB:(j + 1) * NB], self.outw[:, h, :],
                                                            start=(h == 0), stop=(h == 1))
                        last.then_inc(s["lin"], 1)
                        te.wait_ge(s["step"], (t + 1) * LINKS)
                        for j in range(JB):
                            last = nc.tensor.transpose(p_z[:, j, 0:NB], y[:, j, :], self.ident[0:NB, 0:NB])
                        last.then_inc(s["turned2"], 1)
                        te.wait_ge(s["xt2"], t + 1)
                        for j in range(JB):
                            w = self.up[:, :] if kind == "sum" else self.g_a[0][:, :]
                            last = nc.tensor.matmul(p_x[0:NB, j, 0:w.shape[1]], xt[:, j, 0:NB], w, start=True, stop=True)
                        if kind == "product":
                            for hh, p in enumerate((p_y, p_z)):
                                for j in range(JB):
                                    last = nc.tensor.matmul(p[0:2, j, 0:NB], self.g_a[0][:, 2 * hh:2 * hh + 2], xt[:, j, 0:NB],
                                                            start=True, stop=True)
                        last.then_inc(s["tabbed"], 1)
                    each(te, step)

                @block.vector
                def _(v):
                    def step(t):
                        then = Chain(v, s["step"], t * LINKS)
                        wait(v, s["sent"], t * (16 * SENT))
                        v.wait_ge(s["lin"], t + 1)
                        v.wait_ge(s["xin"], (t + 1) * 16)
                        if kind == "sum":
                            then(v.scalar_tensor_tensor(y[:, :, :].rearrange("p j f -> p (j f)"),
                                                        p_y[0:NB, 0:JB, :].rearrange("p j f -> p (j f)"), 0.0,
                                                        xs[:, :, :].rearrange("p j f -> p (j f)"), ALU.max, ALU.add))
                        else:
                            then(v.tensor_tensor(y[:, :, :], p_y[0:NB, 0:JB, :], xs[:, :, :], ALU.add))
                        self.norm(v, s["var"], then, y[:, :, :], D, tmp[:, :, :], st,
                                  lambda: v.wait_ge(s["rooted"], t + 1))
                        assert then.n == LINKS, then.n
                        if kind == "product":
                            v.wait_ge(s["tabd"], t + 1)
                            self.split(v, s["split"], t * SPLIT, tab, D, rest)
                    each(v, step)
            self.zero(s.values())

    def node_attention(self, l):
        nc = self.nc
        dim, table = (D, HID)[l], self.t_d[l][0:N, :]
        n = f"na{l}_"
        with ExitStack() as ctx:
            sb, ps, sem = self.sb, self.ps, self.sem
            own = sb(n + "own", [NB, JB, dim + SC], F32, ctx)
            sums = sb(n + "sums", [P, HEADS, NS], F32, ctx)
            den = sb(n + "den", [HEADS, NS], F32, ctx)
            top = sb(n + "top", [2, 2, NS], F32, ctx)
            dt_s = sb(n + "dt", [NB, JB, 8], F32, ctx)
            zz = sb(n + "zz", [NB, 2, JB, HEADS], F32, ctx)
            zl = sb(n + "zl", [NB, 2, JB, HEADS], F32, ctx)
            pown = sb(n + "pown", [NB, JB, HEADS], F32, ctx)
            rd = sb(n + "rd", [NB, 2, JB, HEADS], F32, ctx)
            prod = sb(n + "prod", [NB, 2, JB, HEADS, HID], F32, ctx)
            h = sb(n + "h", [NB, JB, HID], F32, ctx)
            tmp = sb(n + "tmp", [NB, JB, D], F32, ctx)
            st = sb(n + "st", [P, 2, JB], F32, ctx)
            xt = sb(n + "xt", [P, JB, P], F32, ctx)
            ht = sb(n + "ht", [HID, JB, P], F32, ctx)
            xs = sb(n + "xs", [NB, JB, D], F32, ctx)
            y = sb(n + "y", [NB, JB, D], F32, ctx)
            tab = sb(n + "tab", [NB, JB, HID + SCW], F32, ctx)
            rest = sb(n + "rest", [NB, 2, JB, SC], F32, ctx)
            p_a = ps(n + "pa", [P, 6, HEADS * HID], ctx)
            p_b = ps(n + "pb", [P, 6, HEADS * HID], ctx)
            p_t = ps(n + "pt", [P, 8, P], ctx)
            p_dt = p_b[0:NB, 5, 0:JB * 8].rearrange("p (j o) -> p j o", o=8)
            p_es = p_b[:, :, :].rearrange("p a (b n) -> p (a b) n", n=P)
            names = ("ownin", "xin", "sumd", "turned0", "xt", "lin", "dt", "own", "exped", "var", "rooted", "step", "turned",
                     "ht", "out", "tabd", "split", "sent", "go_t", "go_s")
            s = {k: sem(n + k, ctx) for k in names}
            SENT = 1
            LINKS = 25 if l == 0 else 33
            FIRST = 25
            VARS = 1 if l == 0 else 2
            with nc.Block() as block:
                @block.sync
                def _(e):
                    def step(t):
                        wait(e, s["sent"], t * (16 * SENT))
                        e.sem_inc(s["go_s"], 1)
                        e.dma_start(own[:, :, :], self.node_rows(table, t, dim + SCW)[:, :, 0:dim + SC]).then_inc(s["ownin"], 16)
                        if l == 0:
                            e.wait_ge(s["split"], (t + 1) * SPLIT)
                            e.dma_start(self.node_rows(self.t_d[1][0:N, :], t, HID + SCW), tab[:, :, :]).then_inc(s["sent"], 16)
                        else:
                            e.dma_start(xs[:, :, :], self.node_rows(self.x2_d, t, D)).then_inc(s["xin"], 16)
                            e.wait_ge(s["step"], (t + 1) * LINKS)
                            e.dma_start(self.node_rows(self.x3_d, t, D), y[:, :, :]).then_inc(s["sent"], 16)
                    each(e, step)
                    e.wait_ge(s["sent"], NT * 16 * SENT)

                @block.scalar
                def _(a):
                    def step(t):
                        at = bass.ds(t * NS, NS)
                        wait(a, s["sent"], t * (16 * SENT))
                        nc.scalar.activation(den[:, :], self.den[:, at], ACT.Copy)
                        nc.scalar.activation(top[:, :, :], self.top[:, :, at], ACT.Copy)
                        nc.scalar.activation(sums[0:dim, :, :], self.acc[0:dim, :].rearrange("p (h n) -> p h n", h=HEADS)
                                             [:, :, at], ACT.Copy).then_inc(s["sumd"], 1)
                        a.wait_ge(s["turned0"], t + 1)
                        nc.scalar.activation(xt[0:dim, :, 0:NB], p_t[0:dim, 0:JB, 0:NB], ACT.Copy).then_inc(s["xt"], 1)
                        a.wait_ge(s["own"], t + 1)
                        nc.scalar.activation(pown[:, :, :], zl[:, 0, :, :], ACT.Exp).then_inc(s["exped"], 1)
                        a.wait_ge(s["var"], t * VARS + 1)
                        nc.scalar.activation(st[0:NB, 1, :], st[0:NB, 1, :], ACT.Sqrt).then_inc(s["rooted"], 1)
                        a.wait_ge(s["turned"], t + 1)
                        nc.scalar.activation(ht[:, :, 0:NB], p_t[0:HID, 0:JB, 0:NB], ACT.Copy).then_inc(s["ht"], 1)
                        if l == 0:
                            a.wait_ge(s["out"], t + 1)
                            nc.scalar.activation(tab[:, :, 0:HID], h[:, :, :], ACT.Copy)
                            nc.scalar.activation(tab[:, :, HID:HID + SC], p_a[0:NB, 0:JB, 0:SC], ACT.Copy)
                            for hh in range(2):
                                last = nc.scalar.activation(self.top[:, hh, at].rearrange("b (j p) -> b j p", j=JB),
                                                     p_es[0:2, hh * JB:(hh + 1) * JB, 0:NB], ACT.Copy)
                            last.then_inc(s["tabd"], 1)
                        else:
                            a.wait_ge(s["var"], t * VARS + 2)
                            nc.scalar.activation(st[0:NB, 1, :], st[0:NB, 1, :], ACT.Sqrt).then_inc(s["rooted"], 1)
                    each(a, step)

                @block.tensor
                def _(te):
                    def step(t):
                        te.wait_ge(s["ownin"], (t + 1) * 16)
                        wait(te, s["step"], t * LINKS)
                        if l == 0:
                            wait(te, s["tabd"], t)
                        te.sem_inc(s["go_t"], 1)
                        for j in range(JB):
                            last = nc.tensor.transpose(p_t[0:dim, j, 0:NB], own[:, j, 0:dim], self.ident[0:NB, 0:NB])
                        last.then_inc(s["turned0"], 1)
                        te.wait_ge(s["sumd"], t + 1)
                        te.sem_inc(s["go_t"], 1)
                        for j in range(JB):
                            nc.tensor.transpose(p_dt[:, j, 0:HEADS], den[:, j * NB:(j + 1) * NB], self.ident[0:HEADS, 0:HEADS])
                            for hh in range(2):
                                last = nc.tensor.transpose(p_dt[:, j, 4 + 2 * hh:6 + 2 * hh], top[:, hh, j * NB:(j + 1) * NB],
                                                           self.ident[0:2, 0:2])
                        last.then_inc(s["dt"], 1)
                        for j in range(JB):
                            for o, hd in enumerate(HEAD_OF):
                                nc.tensor.matmul(p_a[0:NB, j, o * HID:(o + 1) * HID], sums[0:dim, o, j * NB:(j + 1) * NB],
                                                 self.g_w[l][:, hd * HID:(hd + 1) * HID], start=True, stop=True)
                        te.wait_ge(s["xt"], t + 1)
                        te.wait_ge(s["step"], t * LINKS + 1)
                        for j in range(JB):
                            for o, hd in enumerate(HEAD_OF):
                                last = nc.tensor.matmul(p_b[0:NB, j, o * HID:(o + 1) * HID], xt[0:dim, j, 0:NB],
                                                        self.g_w[l][:, hd * HID:(hd + 1) * HID], start=True, stop=True)
                        last.then_inc(s["lin"], 1)
                        te.wait_ge(s["step"], t * LINKS + FIRST)
                        te.sem_inc(s["go_t"], 1)
                        for j in range(JB):
                            last = nc.tensor.transpose(p_t[0:HID, j, 0:NB], h[:, j, :], self.ident[0:NB, 0:NB])
                        last.then_inc(s["turned"], 1)
                        te.wait_ge(s["ht"], t + 1)
                        if l == 0:
                            for j in range(JB):
                                nc.tensor.matmul(p_a[0:NB, j, 0:8], ht[:, j, 0:NB], self.g_a[1][:, :], start=True, stop=True)
                            for hh in range(2):
                                for j in range(JB):
                                    last = nc.tensor.matmul(p_es[0:2, hh * JB + j, 0:NB], self.g_a[1][:, 2 * hh:2 * hh + 2],
                                                            ht[:, j, 0:NB], start=True, stop=True)
                        else:
                            for j in range(JB):
                                nc.tensor.matmul(p_a[0:NB, j, 0:D], ht[:, j, 0:NB], self.wo[:, :], start=True, stop=False)
                                last = nc.tensor.matmul(p_a[0:NB, j, 0:D], self.ones[0:1, 0:NB], self.bo[:, :], start=False, stop=True)
                        last.then_inc(s["out"], 1)
                    each(te, step)

                @block.vector
                def _(v):
                    wide = [NB, JB, HID]
                    def step(t):
                        then = Chain(v, s["step"], t * LINKS)
                        wait(v, s["sent"], t * (16 * SENT))
                        v.wait_ge(s["dt"], t + 1)
                        then(v.tensor_copy(dt_s[:, :, :], p_dt))
                        v.wait_ge(s["ownin"], (t + 1) * 16)
                        then(v.tensor_tensor(zz[:, 0, :, :], own[:, :, dim:dim + HEADS], own[:, :, dim + HEADS:dim + SC], ALU.add))
                        then(v.tensor_tensor(zz[:, 1, :, :], dt_s[:, :, 4:8], own[:, :, dim + HEADS:dim + SC], ALU.add))
                        then(v.tensor_scalar(zl[:, :, :, :], zz[:, :, :, :], 0.2, None, ALU.mult))
                        then(v.tensor_tensor(zz[:, :, :, :], zl[:, :, :, :], zz[:, :, :, :], ALU.max))
                        then(v.tensor_tensor(zz[:, 0, :, :], zz[:, 0, :, :], zz[:, 1, :, :], ALU.min))
                        v.tensor_tensor(zl[:, 0, :, :], zz[:, 0, :, :], zz[:, 1, :, :], ALU.subtract).then_inc(s["own"], 1)
                        v.wait_ge(s["exped"], t + 1)
                        then(v.tensor_tensor(rd[:, 0, :, :], dt_s[:, :, 0:4], pown[:, :, :], ALU.add))
                        then(v.reciprocal(rd[:, 0, :, :], rd[:, 0, :, :]))
                        then(v.tensor_scalar(rd[:, 0, :, :], rd[:, 0, :, :], 1.0 / HEADS, None, ALU.mult))
                        then(v.tensor_tensor(rd[:, 1, :, :], rd[:, 0, :, :], pown[:, :, :], ALU.mult))
                        v.wait_ge(s["lin"], t + 1)
                        for k, p in enumerate((p_a, p_b)):
                            then(v.tensor_tensor(prod[:, k, :, :, :].rearrange("p j o k -> p (j o) k"),
                                                 p[0:NB, 0:JB, :].rearrange("p j (o k) -> p (j o) k", k=HID),
                                                 rd[:, k, :, :].rearrange("p j o -> p (j o)").unsqueeze(2)
                                                 .to_broadcast([NB, JB * HEADS, HID]), ALU.mult))
                        then(v.tensor_tensor(prod[:, 0, :, :, :], prod[:, 0, :, :, :], prod[:, 1, :, :, :], ALU.add))
                        then(v.tensor_reduce(h[:, :, :], prod[:, 0, :, :, :].rearrange("p j o k -> p j k o"), AX.X, ALU.add))

                        def row(k):
                            return self.g_row[l][0:NB, k, :].unsqueeze(1).to_broadcast(wide)
                        then(v.tensor_tensor(h[:, :, :], h[:, :, :], row(0), ALU.add))
                        self.norm(v, s["var"], then, h[:, :, :], HID, tmp[:, :, 0:HID], st,
                                  lambda: v.wait_ge(s["rooted"], t * VARS + 1))
                        then(v.tensor_tensor(h[:, :, :], h[:, :, :], row(1), ALU.mult))
                        then(v.tensor_tensor(h[:, :, :], h[:, :, :], row(2), ALU.add))
                        then(v.tensor_scalar(h[:, :, :], h[:, :, :], 0.0, None, ALU.max))
                        assert then.n == FIRST, then.n
                        if l == 1:
                            v.wait_ge(s["out"], t + 1)
                            v.wait_ge(s["xin"], (t + 1) * 16)
                            then(v.tensor_tensor(y[:, :, :], p_a[0:NB, 0:JB, 0:D], xs[:, :, :], ALU.add))
                            self.norm(v, s["var"], then, y[:, :, :], D, tmp[:, :, :], st,
                                      lambda: v.wait_ge(s["rooted"], t * VARS + 2))
                        assert then.n == LINKS, then.n
                        if l == 0:
                            v.wait_ge(s["tabd"], t + 1)
                            self.split(v, s["split"], t * SPLIT, tab, HID, rest)
                    each(v, step)
            self.zero(s.values())

    def node_last(self):
        nc = self.nc
        with ExitStack() as ctx:
            sb, ps, sem = self.sb, self.ps, self.sem
            n = "nl_"
            sums = sb(n + "sums", [P, NS], F32, ctx)
            den = sb(n + "den", [1, NS], F32, ctx)
            xs = sb(n + "xs", [NB, JB, D], F32, ctx)
            y = sb(n + "y", [NB, JB, D], F32, ctx)
            tmp = sb(n + "tmp", [NB, JB, D], F32, ctx)
            c = sb(n + "c", [NB, 4, JB], F32, ctx)
            st = sb(n + "st", [P, 2, JB], F32, ctx)
            p_d = ps(n + "pd", [P, 8, 64], ctx)
            p_y = ps(n + "py", [P, 8, P], ctx)
            s = {k: sem(n + k, ctx) for k in ("xin", "sumd", "lin", "var", "rooted", "step", "sent", "go_t")}
            LINKS = 16
            with nc.Block() as block:
                @block.sync
                def _(e):
                    def step(t):
                        wait(e, s["sent"], t * 16)
                        e.dma_start(xs[:, :, :], self.node_rows(self.x3_d, t, D)).then_inc(s["xin"], 16)
                        e.wait_ge(s["step"], (t + 1) * LINKS)
                        e.dma_start(self.node_rows(self.out, t, D), y[:, :, :]).then_inc(s["sent"], 16)
                    each(e, step)
                    e.wait_ge(s["sent"], NT * 16)

                @block.scalar
                def _(a):
                    def step(t):
                        wait(a, s["lin"], t)
                        nc.scalar.activation(den[:, :], self.den[0:1, bass.ds(t * NS, NS)], ACT.Copy)
                        nc.scalar.activation(sums[:, :], self.acc[:, bass.ds(t * NS, NS)], ACT.Copy).then_inc(s["sumd"], 1)
                        a.wait_ge(s["var"], t + 1)
                        nc.scalar.activation(st[0:NB, 1, :], st[0:NB, 1, :], ACT.Sqrt).then_inc(s["rooted"], 1)
                    each(a, step)

                @block.tensor
                def _(te):
                    def step(t):
                        te.wait_ge(s["sumd"], t + 1)
                        wait(te, s["step"], t * LINKS)
                        te.sem_inc(s["go_t"], 1)
                        for j in range(JB):
                            nc.tensor.transpose(p_d[0:NB, j, 0:1], den[:, j * NB:(j + 1) * NB], self.ident[0:1, 0:1])
                        for j in range(JB):
                            last = nc.tensor.transpose(p_y[0:NB, j, :], sums[:, j * NB:(j + 1) * NB], self.ident[:, :])
                        last.then_inc(s["lin"], 1)
                    each(te, step)

                @block.vector
                def _(v):
                    def step(t):
                        then = Chain(v, s["step"], t * LINKS)
                        v.wait_ge(s["lin"], t + 1)
                        wait(v, s["sent"], t * 16)
                        full = [NB, JB, D]

                        def col(k):
                            return c[:, k, :].unsqueeze(2).to_broadcast(full)
                        then(v.tensor_scalar(c[:, 0, :], p_d[0:NB, 0:JB, 0], 1e-8, None, ALU.max))
                        then(v.reciprocal(c[:, 1, :], c[:, 0, :]))
                        then(v.tensor_scalar(c[:, 2, :], c[:, 0, :], 1e-8, 0.3, ALU.is_gt, ALU.mult))
                        then(v.tensor_scalar(c[:, 3, :], c[:, 2, :], -1.0, 1.0, ALU.mult, ALU.add))
                        then(v.tensor_tensor(c[:, 1, :], c[:, 1, :], c[:, 2, :], ALU.mult))
                        v.wait_ge(s["xin"], (t + 1) * 16)
                        then(v.tensor_tensor(y[:, :, :], p_y[0:NB, 0:JB, :], col(1), ALU.mult))
                        then(v.tensor_tensor(tmp[:, :, :], xs[:, :, :], col(3), ALU.mult))
                        then(v.tensor_tensor(y[:, :, :], y[:, :, :], tmp[:, :, :], ALU.add))
                        then(v.tensor_tensor(y[:, :, :], y[:, :, :], xs[:, :, :], ALU.add))
                        self.norm(v, s["var"], then, y[:, :, :], D, tmp[:, :, :], st,
                                  lambda: v.wait_ge(s["rooted"], t + 1))
                        assert then.n == LINKS, then.n
                    each(v, step)
            self.zero(s.values())

    def build(self):
        nc = self.nc
        with self.ctx:
            self.allocate()
            self.x2_d = self.dram("x2_rows", [N, D])
            self.setup()
            self.is_general = nc.values_load(self.general[0:1, 0:1], min_val=0, max_val=1)
            self.sum_edges("e0_", self.i["x"], False)
            self.node_layer("n0_", "sum", self.i["x"])
            self.product_edges()
            self.node_layer("n1_", "product", self.x1_d)
            self.attend_edges(0, self.t_d[0], D)
            self.node_attention(0)
            self.attend_edges(1, self.t_d[1], HID)
            self.node_attention(1)
            self.sum_edges("e3_", self.x3_d, True)
            self.node_last()


def graph_layers(nc, names, aps, out):
    Program(nc, dict(zip(names, aps)), out).build()


_INS = ["x", "src", "dst", "edge_attr_3", "edge_weight", "L0_gnn_W", "L0_gnn_b", "L1_gnn_W_up0", "L1_gnn_W_up1",
        "L1_gnn_mlp_w0", "L1_gnn_mlp_b0", "L1_gnn_mlp_w1", "L1_gnn_mlp_b1", "L1_gnn_mlp_w2", "L1_gnn_mlp_b2",
        "L1_gnn_W_out0", "L1_gnn_W_out1", "L2_gnn_W1", "L2_gnn_asrc1", "L2_gnn_adst1", "L2_gnn_b1", "L2_gnn_g1",
        "L2_gnn_be1", "L2_gnn_W2", "L2_gnn_asrc2", "L2_gnn_adst2", "L2_gnn_b2", "L2_gnn_g2", "L2_gnn_be2",
        "L2_gnn_Wo", "L2_gnn_bo"]


def kernel(**inputs):
    import numpy as _np
    import concourse.bacc as _bacc
    from concourse import mybir as _mybir
    from concourse.bass_utils import run_bass_kernel_spmd as _run

    nc = _bacc.Bacc("TRN2", target_bir_lowering=False, num_devices=1)
    arrays, args = {}, []
    for name in _INS:
        a = _np.ascontiguousarray(inputs[name])
        arrays[f"in_{name}_dram"] = a
        args.append(nc.dram_tensor(f"in_{name}_dram", a.shape, _mybir.dt.from_np(a.dtype), kind="ExternalInput").ap())
    out = nc.dram_tensor("out_0_dram", (3125, 128), _mybir.dt.float32, kind="ExternalOutput").ap()
    graph_layers(nc, _INS, args, out)
    r = _run(nc, [arrays], core_ids=[0])
    return r.results[0]["out_0_dram"]
```

```python
import concourse.bass as bass
from concourse import mybir
from contextlib import ExitStack

F32 = mybir.dt.float32
I32 = mybir.dt.int32
BF16 = mybir.dt.bfloat16
ALU = mybir.AluOpType
ACT = mybir.ActivationFunctionType
AX = mybir.AxisListType

N = 3125
E = 53125
D = 128
P = 128
CH = 4
GE = CH * P
NG = -(-E // GE)
LAST = E - (NG - 1) * GE
W = 40
HW = 64
ROUNDS = -(-N // W)
NP = N + W + (-(N + W)) % P
NB = 125
JB = 5
NS = JB * NB
NT = N // NS
HEADS = 4
HID = 64
MUL = 32
NBAS = 8
BIG = 1e30
NOWHERE = float(1 << 20)
LN_EPS = 1e-5
MIN_NORM2 = 1.3e-35
HEAD_OF = [0, 2, 1, 3]
PARTS = 3
MEET = [(0, 0), (0, 1), (0, 2), (1, 0), (1, 1), (2, 0)]
TERMS = len(MEET)
SC = 2 * HEADS
SCP = PARTS * SC
SCW = SC + SCP // 2
SPLIT = 2 * PARTS - 1


def wait(eng, sem, value):
    if not isinstance(value, int) or value > 0:
        eng.wait_ge(sem, value)


def pipeline(eng, unroll, stages):
    def at(turn, s):
        for lag, step in stages:
            slot, t = (s - lag) % unroll, turn + (s - lag) // unroll
            k = t * unroll + slot
            if not isinstance(k, int) or 0 <= k < NG:
                step(k, slot, t)

    for s in range(unroll):
        at(0, s)
    with eng.Fori(1, NG // unroll) as turn:
        for s in range(unroll):
            at(turn, s)
    for s in range(max(lag for lag, _ in stages)):
        at(NG // unroll, s)


def steps(stages):
    for now in range(NT + max(lag for lag, _ in stages)):
        for lag, step in stages:
            if 0 <= now - lag < NT:
                step(now - lag)


class Chain:

    def __init__(self, eng, sem, start=0):
        self.eng, self.sem, self.start, self.n = eng, sem, start, 0

    def __call__(self, ins):
        self.n += 1
        ins.then_inc(self.sem, 1)
        self.eng.wait_ge(self.sem, self.start + self.n)


class Program:
    def __init__(self, nc, ins, out):
        self.nc, self.i, self.out = nc, ins, out
        self.ctx = ExitStack()

    def sb(self, name, shape, dt=F32, ctx=None):
        return (ctx or self.ctx).enter_context(self.nc.sbuf_tensor(name, shape, dt))

    def ps(self, name, shape, ctx, dt=F32):
        return ctx.enter_context(self.nc.psum_tensor(name, shape, dt))

    def sem(self, name, ctx=None):
        return (ctx or self.ctx).enter_context(self.nc.semaphore(name))

    def dram(self, name, shape, dt=F32):
        return self.nc.dram_tensor(name, shape, dt, kind="Internal").ap()

    def allocate(self):
        sb = self.sb
        self.ident = sb("ident", [P, P])
        self.ones = sb("ones", [P, P])
        self.ident_h = sb("ident_h", [P, P], BF16)
        self.pick = sb("pick", [P, 2, P], BF16)
        self.iota = sb("iota", [P, W])
        self.node_of_row = sb("node_of_row", [P, 1])
        self.iota_now = sb("iota_now", [P, W])
        self.node_now = sb("node_now", [P, 1])
        self.base_first = sb("base_first", [1, NG], I32)
        self.base_now = sb("base_now", [1, NG], I32)
        self.shift = sb("shift", [P, 1])
        self.general = sb("general", [1, 1], I32)
        self.src_t = sb("src_t", [P, NG, CH], I32)
        self.dst_t = sb("dst_t", [P, NG, CH])
        self.w_t = sb("w_t", [P, NG, CH])
        self.dir_t = sb("dir_t", [P, NG, CH, 3])
        self.l0_w = sb("l0_w", [P, 2, D])
        self.l0_b = sb("l0_b", [PARTS, 1, D], BF16)
        self.up = sb("up", [P, P])
        self.outw = sb("outw", [P, 2, P])
        self.m_w0 = sb("m_w0", [2 * TERMS * NBAS, P], BF16)
        self.m_b0 = sb("m_b0", [P, 1])
        self.m_w1 = sb("m_w1", [P, P])
        self.m_b1 = sb("m_b1", [P, 1])
        self.m_w2 = sb("m_w2", [P, 2, 4 * MUL])
        self.m_b2 = sb("m_b2", [P, CH, 4 * MUL], BF16)
        self.ones_h = sb("ones_h", [P, P], BF16)
        self.g_w = [sb("g_w1", [D, HEADS * HID]), sb("g_w2", [HID, HEADS * HID])]
        self.g_a = [sb("g_a1", [D, 8]), sb("g_a2", [HID, 8])]
        self.g_row = [sb(f"g_row{n}", [P, 3, HID]) for n in (1, 2)]
        self.wo = sb("wo", [HID, D])
        self.bo = sb("bo", [PARTS, 1, D], BF16)
        self.acc = sb("acc", [P, HEADS * NP])
        self.den = sb("den", [HEADS, NP])
        self.top = sb("top", [2, 2, NP])
        self.landed = [self.sem(f"rows_landed{n}") for n in range(8)]
        dram = self.dram
        self.dst_d = dram("dst_rows", [NG, GE])
        self.emb_d = dram("emb_rows", [NG, PARTS, NBAS, GE], BF16)
        self.x1_d = dram("x1_rows", [N, D])
        self.x2_d = dram("x2_rows", [N, D])
        self.up_d = dram("up_rows", [N, D])
        self.t_d = [dram("gat1_rows", [NP, D + SCW]), dram("gat2_rows", [NP, HID + SCW])]
        self.x3_d = dram("x3_rows", [N, D])

    def setup(self):
        nc, i, sb, ps, sem = self.nc, self.i, self.sb, self.ps, self.sem
        with ExitStack() as ctx:
            src_i = sb("src_i", [NG, GE], I32, ctx)
            dst_i = sb("dst_i", [NG, GE], I32, ctx)
            w_r = sb("w_r", [NG, GE], F32, ctx)
            vec_r = sb("vec_r", [NG, GE * 3], F32, ctx)
            src_f = sb("src_f", [NG, GE], F32, ctx)
            dst_f = sb("dst_f", [NG, GE], F32, ctx)
            dst_l = sb("dst_l", [NG, GE], F32, ctx)
            fl_i = sb("fl_i", [1, 2, NG], I32, ctx)
            fl = sb("fl", [1, 2, NG], F32, ctx)
            bad = sb("bad", [NG, GE], F32, ctx)
            bad_n = sb("bad_n", [NG, 1], F32, ctx)
            bad_r = sb("bad_r", [1, 3, NG], F32, ctx)
            bad_s = sb("bad_s", [1, 4], F32, ctx)
            row = sb("row", [1, NG + 1], F32, ctx)
            fcol = sb("fcol", [NG, 1], F32, ctx)
            row_b = sb("row_b", [P, NG + 1], F32, ctx)
            l0_n = sb("l0_n", [P, 2 * D], F32, ctx)
            a_m = sb("a_m", [P, 2, 2, 8], F32, ctx)
            wt = sb("wt", [P, 2, 2, P], F32, ctx)
            m0r = sb("m0r", [NBAS, 64], F32, ctx)
            m0s = sb("m0s", [NBAS, 64], F32, ctx)
            m0p = sb("m0p", [NBAS, PARTS, 64], BF16, ctx)
            m2r = sb("m2r", [1, 4 * MUL], F32, ctx)
            m2p = sb("m2p", [1, PARTS, 4 * MUL], BF16, ctx)
            b0r = sb("b0r", [1, D], F32, ctx)
            b0p = sb("b0p", [1, PARTS, D], BF16, ctx)
            bor = sb("bor", [1, D], F32, ctx)
            bop = sb("bop", [1, PARTS, D], BF16, ctx)
            m0l = sb("m0l", [NBAS, PARTS, 64], F32, ctx)
            m2l = sb("m2l", [1, PARTS, 4 * MUL], F32, ctx)
            b0l = sb("b0l", [1, PARTS, D], F32, ctx)
            bol = sb("bol", [1, PARTS, D], F32, ctx)
            upr = sb("upr", [P, P], F32, ctx)
            outr = sb("outr", [P, 2, P], F32, ctx)
            zero = sb("zero", [P, SCW], F32, ctx)
            pickf = sb("pickf", [P, 2, P], F32, ctx)
            cleared = sem("cleared", ctx)
            consts = sem("consts", ctx)
            loaded = sem("loaded", ctx)
            weights_in = sem("weights_in", ctx)
            late_in = sem("late_in", ctx)
            with nc.Block() as block:
                @block.vector
                def _(v):
                    v.memset(src_i[:, :], 0).then_inc(cleared, 1)
                    v.memset(dst_i[:, :], int(NOWHERE)).then_inc(cleared, 1)
                    v.memset(w_r[:, :], 0.0).then_inc(cleared, 1)
                    v.memset(vec_r[:, :], 0.0).then_inc(cleared, 1)
                    v.memset(upr[:, :], 0.0).then_inc(cleared, 1)
                    v.memset(outr[:, :, :], 0.0).then_inc(cleared, 1)
                    v.memset(a_m[:, :, :, :], 0.0).then_inc(cleared, 1)
                    v.memset(zero[:, :], 0.0).then_inc(cleared, 1)
                    v.memset(self.m_w0[:, :], 0.0).then_inc(cleared, 1)
                    v.memset(self.m_w1[:, :], 0.0).then_inc(cleared, 1)
                    v.memset(self.m_w2[:, :, :], 0.0).then_inc(cleared, 1)
                    v.memset(self.ones[:, :], 1.0)
                    v.memset(self.top[:, :, N:], -BIG)
                    v.memset(self.ones_h[:, :], 1.0)
                    v.memset(self.m_b2[:, :, :], 0.0)

                @block.gpsimd
                def _(g):
                    g.memset(self.ident[:, :], 0.0).then_inc(consts, 1)
                    g.iota(self.iota[:, :], [[1, W]], base=0, channel_multiplier=0,
                           allow_small_or_imprecise_dtypes=True).then_inc(consts, 1)
                    for q in range(P // HW):
                        g.wait_ge(consts, 2 + q)
                        g.iota(self.node_of_row[q * HW:(q + 1) * HW, :], [[0, 1]], base=0, channel_multiplier=1,
                               allow_small_or_imprecise_dtypes=True).then_inc(consts, 1)
                    g.wait_ge(consts, 4)
                    g.affine_select(out=self.ident[:, :], in_=self.ident[:, :], compare_op=ALU.not_equal,
                                    fill=1.0, base=0, pattern=[[-1, P]], channel_multiplier=1).then_inc(consts, 1)
                    g.memset(pickf[:, :, :], 0.0).then_inc(consts, 1)
                    for part in range(PARTS):
                        g.wait_ge(consts, 6 + part)
                        view = pickf[:, :, :].rearrange("o b (h n) -> o b h n", h=2)
                        g.affine_select(out=view, in_=view, compare_op=ALU.not_equal, fill=1.0, base=-SC * part,
                                        pattern=[[-1, 2], [-2, 2], [0, HW]], channel_multiplier=1).then_inc(consts, 1)
                    g.wait_ge(consts, 6 + PARTS)
                    g.tensor_copy(self.ident_h[:, :], self.ident[:, :])
                    g.tensor_copy(self.pick[:, :, :], pickf[:, :, :])

                @block.sync
                def _(s):
                    n = 0

                    def load(dst, src):
                        nonlocal n
                        n += 16
                        with nc.allow_non_contiguous_dma(reason="first and last edges of the groups"):
                            s.dma_start(dst, src).then_inc(loaded, 16)
                    s.wait_ge(cleared, 11)
                    full = (NG - 1) * GE
                    for tile, name, k in ((src_i, "src", 1), (dst_i, "dst", 1), (w_r, "edge_weight", 1)):
                        load(tile[0:NG - 1, :], i[name][0:full].rearrange("(g e) -> g e", e=GE))
                        load(tile[NG - 1:NG, 0:LAST], i[name][full:E].rearrange("(g e) -> g e", g=1))
                    load(vec_r[0:NG - 1, :], i["edge_attr_3"][0:full, :].rearrange("(g e) c -> g (e c)", e=GE))
                    load(vec_r[NG - 1:NG, 0:3 * LAST], i["edge_attr_3"][full:E, :].rearrange("(g e) c -> g (e c)", g=1))
                    firsts = i["dst"][0:full].rearrange("(g e) -> e g", e=GE)
                    load(fl_i[:, 0, 0:NG - 1], firsts[0:1, :])
                    load(fl_i[:, 1, 0:NG - 1], firsts[GE - 1:GE, :])
                    load(fl_i[:, 0, NG - 1:NG], i["dst"][full:full + 1].rearrange("(g e) -> g e", g=1))
                    load(fl_i[:, 1, NG - 1:NG], i["dst"][E - 1:E].rearrange("(g e) -> g e", g=1))
                    s.wait_ge(loaded, n)

            weights = late = 0

            def weight_loads(eng):
                nonlocal weights

                def load(dst, src):
                    nonlocal weights
                    weights += 16
                    with nc.allow_non_contiguous_dma(reason="columns of small weights"):
                        eng.dma_start(dst, src).then_inc(weights_in, 16)
                load(l0_n[:, :], i["L0_gnn_W"])
                for l, n_ in ((0, "1"), (1, "2")):
                    load(self.g_w[l][:, :], i["L2_gnn_W" + n_])
                    for b in range(2):
                        for k, name in ((0, "asrc"), (HEADS, "adst")):
                            at = k + 2 * b
                            load(a_m[b * HID:(b + 1) * HID, l, :, :].rearrange("p h o -> p (h o)")[:, at:at + 10:9],
                                 i[f"L2_gnn_{name}{n_}"][b:HEADS:2, :].rearrange("a n -> n a"))
                load(upr[0:MUL, 0:MUL], i["L1_gnn_W_up0"])
                for c in range(3):
                    load(upr[MUL + c:P:3, MUL * (1 + c):MUL * (2 + c)], i["L1_gnn_W_up1"])
                load(outr[0:2 * MUL, 0, 0:MUL], i["L1_gnn_W_out0"])
                for c, (r, h) in enumerate(((64, 0), (0, 1), (64, 1))):
                    load(outr[r:r + 2 * MUL, h, MUL + c:P:3], i["L1_gnn_W_out1"])
                load(m0r[:, :], i["L1_gnn_mlp_w0"])
                for row_, name in ((m2r, "L1_gnn_mlp_b2"), (b0r, "L0_gnn_b"), (bor, "L2_gnn_bo")):
                    load(row_[:, :], i[name].rearrange("(a n) -> a n", a=1))

            def late_loads(eng):
                nonlocal late

                def load(dst, src):
                    nonlocal late
                    late += 16
                    with nc.allow_non_contiguous_dma(reason="columns of small weights"):
                        eng.dma_start(dst, src).then_inc(late_in, 16)
                for g in range(2):
                    at = slice(g * 64, g * 64 + 64)
                    load(self.m_b0[at, :], i["L1_gnn_mlp_b0"].rearrange("(n a) -> n a", a=1))
                    load(self.m_w1[at, at], i["L1_gnn_mlp_w1"])
                    load(self.m_b1[at, :], i["L1_gnn_mlp_b1"].rearrange("(n a) -> n a", a=1))
                    load(self.m_w2[at, g, :], i["L1_gnn_mlp_w2"])
                for l, n_ in ((0, "1"), (1, "2")):
                    for k, name in enumerate(("b", "g", "be")):
                        load(self.g_row[l][:, k, :],
                             i[f"L2_gnn_{name}{n_}"].rearrange("(a n) -> a n", a=1).to_broadcast([P, HID]))
                    load(self.t_d[l][N:NP, (D, HID)[l]:], zero[0:NP - N, :])
                load(self.wo[:, :], i["L2_gnn_Wo"])

            step = sem("setup_step", ctx)
            counted = sem("counted", ctx)
            rowed = sem("rowed", ctx)
            spread = sem("spread", ctx)
            stored = sem("dst_stored", ctx)
            with ExitStack() as pctx:
                p_n = ps("p_n", [1, 1], pctx)
                p_row = ps("p_row", [P, NG + 1], pctx)
                p_col = ps("p_col", [NG, 1], pctx)
                with nc.Block() as block:
                    @block.vector
                    def _(v):
                        then = Chain(v, step)
                        v.tensor_copy(src_f[:, :], src_i[:, :])
                        v.tensor_copy(fl[:, :, :], fl_i[:, :, :]).then_inc(spread, 1)
                        then(v.tensor_copy(dst_f[:, :], dst_i[:, :]))
                        then(v.tensor_tensor(bad[:, 0:GE - 1], dst_f[:, 0:GE - 1], dst_f[:, 1:GE], ALU.is_gt))
                        then(v.tensor_reduce(bad_n[:, :], bad[:, 0:GE - 1], AX.X, ALU.add))
                        then(v.memset(bad_r[:, :, :], 0.0))
                        v.wait_ge(spread, 1)
                        first, last = fl[:, 0, :], fl[:, 1, :]
                        then(v.tensor_tensor(bad_r[:, 0, :], last, first, ALU.subtract))
                        then(v.tensor_scalar(bad_r[:, 0, :], bad_r[:, 0, :], float(W - 1), None, ALU.is_gt))
                        v.tensor_tensor(bad_r[:, 1, 0:NG - 1], last[:, 0:NG - 1], first[:, 1:NG], ALU.is_gt)
                        then(v.tensor_tensor(bad_r[:, 2, 0:NG - 2], last[:, 0:NG - 2], first[:, 2:NG], ALU.is_ge))
                        then(v.tensor_reduce(bad_s[:, 0:1], bad_r[:, :, :], AX.XY, ALU.add))
                        v.wait_ge(counted, 1)
                        then(v.tensor_tensor(bad_s[:, 1:2], bad_s[:, 0:1], p_n[:, :], ALU.add))
                        then(v.tensor_scalar(row[:, NG:NG + 1], bad_s[:, 1:2], 0.0, None, ALU.is_gt))
                        then(v.tensor_copy(self.general[:, :], row[:, NG:NG + 1]))
                        then(v.tensor_scalar(bad_s[:, 2:3], row[:, NG:NG + 1], -1.0, 1.0, ALU.mult, ALU.add))
                        then(v.tensor_scalar(row[:, 0:NG], first, bad_s[:, 2:3], None, ALU.mult))
                        v.tensor_copy(self.base_first[:, :], row[:, 0:NG]).then_inc(rowed, 1)
                        v.wait_ge(counted, 3)
                        v.tensor_copy(row_b[:, :], p_row[:, :])
                        then(v.tensor_copy(fcol[:, :], p_col[:, :]))
                        then(v.tensor_scalar(self.shift[:, :], row_b[:, NG:NG + 1], float(W), None, ALU.mult))
                        v.tensor_scalar(dst_l[:, :], dst_f[:, :], fcol[:, 0:1], None, ALU.subtract).then_inc(spread, 1)

                    @block.tensor
                    def _(t):
                        t.wait_ge(step, 3)
                        nc.tensor.matmul(p_n[:, :], bad_n[:, :], self.ones[0:NG, 0:1], start=True, stop=True).then_inc(counted, 1)
                        t.wait_ge(rowed, 1)
                        nc.tensor.matmul(p_row[:, :], self.ones[0:1, :], row[:, :], start=True, stop=True).then_inc(counted, 1)
                        nc.tensor.matmul(p_col[:, :], row[:, 0:NG], self.ones[0:1, 0:1], start=True, stop=True).then_inc(counted, 1)

                    @block.scalar
                    def _(a):
                        weight_loads(a)

                    @block.sync
                    def _(s):
                        s.wait_ge(spread, 2)
                        s.dma_start(self.dst_d, dst_l[:, :]).then_inc(stored, 16)
                        s.wait_ge(stored, 16)

            turned = sem("turned", ctx)
            taken = sem("taken", ctx)
            vstep = sem("dir_step", ctx)
            rooted = sem("rooted", ctx)
            with ExitStack() as pctx:
                p_t = [ps(f"p_t{n}", [P, CH, P], pctx) for n in range(4)]
                nrm = sb("nrm", [P, NG, CH], F32, pctx)
                sqv = sb("sqv", [P, NG, CH, 3], F32, pctx)
                vec_t = sb("vec_t", [P, NG, CH, 3], F32, pctx)
                vec_v = vec_r[:, :].rearrange("g (e c) -> g c e", c=3)
                jobs = [("src", lambda q: src_f[:, q * P:(q + 1) * P]), ("dst", lambda q: dst_f[:, q * P:(q + 1) * P]),
                        ("w", lambda q: w_r[:, q * P:(q + 1) * P])]
                jobs += [(c, lambda q, c=c: vec_v[:, c, q * P:(q + 1) * P]) for c in range(3)]
                with nc.Block() as block:
                    @block.tensor
                    def _(t):
                        for n, (_, part) in enumerate(jobs):
                            wait(t, taken, n - 3)
                            for q in range(CH):
                                last = nc.tensor.transpose(p_t[n % 4][:, q, 0:NG], part(q), self.ident[0:NG, 0:NG])
                            last.then_inc(turned, 1)
                        t.wait_ge(weights_in, weights)
                        t.wait_ge(taken, 3)
                        for h in range(2):
                            last = nc.tensor.transpose(p_t[2][:, h, :], l0_n[:, h * P:(h + 1) * P], self.ident[:, :])
                        last.then_inc(turned, 1)
                        t.wait_ge(taken, 4)
                        for h in range(2):
                            nc.tensor.transpose(p_t[3][:, h, :], self.g_w[0][:, h * P:(h + 1) * P], self.ident[:, :])
                            last = nc.tensor.transpose(p_t[3][:, 2 + h, 0:HID], self.g_w[1][:, h * P:(h + 1) * P],
                                                       self.ident[0:HID, 0:HID])
                        last.then_inc(turned, 1)
                        t.wait_ge(taken, 9)
                        for l, k in ((0, D), (1, HID)):
                            for h in range(2):
                                last = nc.tensor.matmul(p_t[l][0:k, 0, 0:8], wt[:, l, h, 0:k], a_m[:, l, h, :],
                                                        start=(h == 0), stop=(h == 1))
                        last.then_inc(turned, 1)

                    @block.sync
                    def _(s):
                        late_loads(s)

                    @block.vector
                    def _(v):
                        view = [p[:, :, 0:NG].rearrange("p q g -> p g q") for p in p_t]
                        v.wait_ge(turned, 1)
                        v.tensor_copy(self.src_t[:, :, :], view[0]).then_inc(taken, 1)
                        v.wait_ge(turned, 2)
                        v.tensor_tensor(self.dst_t[:, :, :], view[1],
                                        row_b[:, 0:NG].unsqueeze(2).to_broadcast([P, NG, CH]), ALU.subtract).then_inc(taken, 1)
                        v.wait_ge(turned, 3)
                        v.tensor_copy(self.w_t[:, :, :], view[2]).then_inc(taken, 1)
                        for c in range(3):
                            v.wait_ge(turned, 4 + c)
                            v.tensor_copy(vec_t[:, :, :, c], view[(3 + c) % 4]).then_inc(taken, 1)
                        v.wait_ge(turned, 7)
                        v.tensor_copy(self.l0_w[:, :, :], p_t[2][:, 0:2, :]).then_inc(taken, 1)
                        v.wait_ge(turned, 8)
                        v.tensor_copy(wt[:, 0, :, :], p_t[3][:, 0:2, :]).then_inc(taken, 1)
                        v.tensor_copy(wt[:, 1, :, 0:HID], p_t[3][:, 2:4, 0:HID]).then_inc(taken, 1)
                        then = Chain(v, vstep)
                        v.wait_ge(taken, 9)
                        then(v.tensor_tensor(sqv[:, :, :, :], vec_t[:, :, :, :], vec_t[:, :, :, :], ALU.mult))
                        then(v.tensor_reduce(nrm[:, :, :], sqv[:, :, :, :], AX.X, ALU.add))
                        then(v.tensor_scalar(nrm[:, :, :], nrm[:, :, :], MIN_NORM2, None, ALU.max))
                        v.wait_ge(rooted, 1)
                        then(v.tensor_scalar(nrm[:, :, :], nrm[:, :, :], 1e-12, None, ALU.add))
                        then(v.reciprocal(nrm[:, :, :], nrm[:, :, :]))
                        v.tensor_tensor(self.dir_t[:, :, :, :], vec_t[:, :, :, :],
                                        nrm[:, :, :].unsqueeze(3).to_broadcast([P, NG, CH, 3]), ALU.mult)
                        v.wait_ge(turned, 9)
                        v.tensor_copy(self.g_a[0][:, :], p_t[0][:, 0, 0:8])
                        v.tensor_copy(self.g_a[1][:, :], p_t[1][0:HID, 0, 0:8])
                        v.tensor_scalar(m0s[:, :], m0r[:, :], float(NBAS) ** 0.5, None, ALU.mult)
                        v.tensor_scalar(self.up[:, :], upr[:, :], float(MUL) ** -0.5, None, ALU.mult)
                        out_scale = float(2 * MUL) ** -0.5 / 16.0
                        v.tensor_scalar(self.outw[:, :, :], outr[:, :, :], out_scale, None, ALU.mult)

                    @block.scalar
                    def _(a):
                        a.wait_ge(vstep, 3)
                        nc.scalar.activation(nrm[:, :, :], nrm[:, :, :], ACT.Sqrt).then_inc(rooted, 1)

            clipped = sem("clipped", ctx)
            squared = sem("squared", ctx)
            bumped = sem("bumped", ctx)
            masked = sem("masked", ctx)
            emb_out = sem("emb_out", ctx)
            parted = sem("parted", ctx)
            left = sem("left", ctx)
            wparts = sem("weight_parts", ctx)
            with ExitStack() as pctx:
                w_c = sb("w_c", [NG, GE], F32, pctx)
                centre = sb("centre", [NG, NBAS], F32, pctx)
                emb = sb("emb", [NG, NBAS, GE], F32, pctx)
                parts = sb("emb_parts", [NG, PARTS, NBAS, GE], BF16, pctx)
                with nc.Block() as block:
                    @block.vector
                    def _(v):
                        for k in range(NBAS):
                            v.memset(centre[:, k:k + 1], -float(k))
                        v.tensor_scalar(w_c[:, :], w_r[:, :], 0.0, 1.0, ALU.max, ALU.min).then_inc(clipped, 1)
                        for lo, h in ((64, 0), (0, 1), (64, 1)):
                            v.tensor_scalar(self.outw[lo:lo + MUL, h, :], self.outw[lo:lo + MUL, h, :],
                                            3.0 ** 0.5, None, ALU.mult)
                        then = Chain(v, wparts)
                        for whole, part, rest in ((m0s, m0p, m0l), (m2r, m2p, m2l), (b0r, b0p, b0l), (bor, bop, bol)):
                            now = whole[:, :]
                            for k in range(PARTS):
                                then(v.tensor_copy(part[:, k, :], now))
                                if k < PARTS - 1:
                                    then(v.tensor_tensor(rest[:, k, :], now, part[:, k, :], ALU.subtract))
                                    now = rest[:, k, :]
                        for k in range(NBAS):
                            v.wait_ge(bumped, k + 1)
                            v.scalar_tensor_tensor(emb[:, k, :], w_r[:, :], 1.0, emb[:, k, :],
                                                   ALU.is_le, ALU.mult).then_inc(masked, 1)
                        for k in range(NBAS):
                            v.wait_ge(parted, k + 1)
                            v.tensor_tensor(emb[:, k, :], emb[:, k, :], parts[:, 0, k, :], ALU.subtract).then_inc(left, 1)
                        for k in range(NBAS):
                            v.wait_ge(parted, NBAS + k + 1)
                            v.tensor_tensor(parts[:, 2, k, :], emb[:, k, :], parts[:, 1, k, :], ALU.subtract).then_inc(left, 1)

                    @block.scalar
                    def _(a):
                        a.wait_ge(clipped, 1)
                        for k in range(NBAS):
                            nc.scalar.activation(emb[:, k, :], w_c[:, :], ACT.Square, scale=float(NBAS - 1),
                                                 bias=centre[:, k:k + 1]).then_inc(squared, 1)
                        for k in range(NBAS):
                            a.wait_ge(squared, k + 1)
                            nc.scalar.activation(emb[:, k, :], emb[:, k, :], ACT.Exp, scale=-0.5).then_inc(bumped, 1)
                        for k in range(NBAS):
                            a.wait_ge(masked, k + 1)
                            nc.scalar.activation(parts[:, 0, k, :], emb[:, k, :], ACT.Copy).then_inc(parted, 1)
                        for k in range(NBAS):
                            a.wait_ge(left, k + 1)
                            nc.scalar.activation(parts[:, 1, k, :], emb[:, k, :], ACT.Copy).then_inc(parted, 1)

                    @block.sync
                    def _(s):
                        n = 0
                        s.wait_ge(wparts, 4 * SPLIT)
                        for g in range(2):
                            for t, (_, part) in enumerate(MEET):
                                r = (g * TERMS + t) * NBAS
                                n += 16
                                s.dma_start(self.m_w0[r:r + NBAS, g * 64:g * 64 + 64], m0p[:, part, :]).then_inc(emb_out, 16)
                        for part in range(PARTS):
                            for bias, parted_bias, times in ((self.m_b2, m2p, CH), (self.l0_b, b0p, 1), (self.bo, bop, 1)):
                                for q in range(times):
                                    n += 16
                                    s.dma_start(bias[part:part + 1, q, :], parted_bias[:, part, :]).then_inc(emb_out, 16)
                        for part, (made, count) in enumerate(((parted, NBAS), (parted, 2 * NBAS), (left, 2 * NBAS))):
                            s.wait_ge(made, count)
                            s.dma_start(self.emb_d[:, part, :, :], parts[:, part, :, :]).then_inc(emb_out, 16)
                        s.wait_ge(emb_out, n + 16 * PARTS)
                        s.wait_ge(late_in, late)
            self.zero([cleared, consts, loaded, weights_in, late_in, step, counted, rowed, spread, stored, turned, taken, vstep, rooted,
                       clipped, squared, bumped, masked, emb_out, parted, left, wparts])

    def clear(self, rows, columns, cells):
        nc = self.nc
        cut = [columns * k // 8 for k in (0, 4, 8)]
        with nc.Block() as block:
            @block.scalar
            def _(a):
                nc.scalar.activation(self.acc[0:rows, cut[1]:cut[2]],
                                     self.ones[0:rows, 0:1].to_broadcast([rows, cut[2] - cut[1]]), ACT.Copy, scale=0.0)

            @block.gpsimd
            def _(g):
                for ap in cells:
                    g.memset(ap, 0.0)

            @block.vector
            def _(v):
                v.tensor_copy(self.iota_now[:, :], self.iota[:, :])
                v.tensor_copy(self.node_now[:, :], self.node_of_row[:, :])
                v.tensor_copy(self.base_now[:, :], self.base_first[:, :])
                v.memset(self.acc[0:rows, 0:cut[1]], 0.0)

    def advance(self, v, done, n):
        v.wait_ge(done, n)
        v.tensor_scalar(self.iota_now[:, :], self.iota_now[:, :], self.shift[:, 0:1], None, ALU.add)
        v.tensor_scalar(self.node_now[:, :], self.node_now[:, :], self.shift[:, 0:1], None, ALU.add)
        v.tensor_scalar(self.base_now[:, :], self.base_now[:, :], self.shift[0:1, 0:1], None, ALU.add)

    def zero(self, sems):
        nc = self.nc
        ids = sorted(s.num for s in sems)
        while ids:
            n = 1
            while n < len(ids) and ids[n] == ids[0] + n:
                n += 1
            nc.gpsimd.sem_clear(range(ids[0], ids[0] + n))
            ids = ids[n:]
        nc.all_engine_barrier()

    def rounds(self, sems, body):
        with self.nc.Fori(0, self.is_general * (ROUNDS - 1) + 1):
            body()
            self.nc.gpsimd.dma_reset(range(self.landed[0].num, self.landed[-1].num + 1))
            self.zero(sems + self.landed)

    def indices(self, slots, idx, s):
        def step(k, slot, turn):
            wait(self.nc.scalar, s["used"], k - slots + 1)
            self.nc.scalar.activation(idx[:, slot, :], self.src_t[:, bass.ds(k, 1), :].rearrange("p a q -> p (a q)"),
                                      ACT.Copy).then_inc(s["idx"], 1)
        return step

    def gather(self, g, slots, table, width, rows, idx, s):
        def step(k, slot, turn):
            wait(g, s["used"], k - slots + 1)
            g.wait_ge(s["idx"], k + 1)
            g.sem_inc(s["turn"], 1)
            for q in range(CH):
                g.indirect_dma_start(rows[:, slot, q, 0:width], None, table,
                                     bass.IndirectOffsetOnAxis(ap=idx[:, slot, q:q + 1], axis=0)).then_inc(s["rows"][slot], 16)
        return step

    def window(self, v, k):
        return v.value_load(self.base_now[0:1, bass.ds(k, 1)], min_val=0, max_val=NP - W)

    def onehot(self, k):
        a = self.iota_now[:, :].unsqueeze(1).to_broadcast([P, CH, W])
        b = self.dst_t[:, bass.ds(k, 1), :].rearrange("p a q -> p (a q)").unsqueeze(2).to_broadcast([P, CH, W])
        return a, b

    def sum_edges(self, name, table, weighted):
        nc = self.nc
        U = 4
        with ExitStack() as ctx:
            rows = self.sb(name + "rows", [P, U, CH, D], F32, ctx)
            idx = self.sb(name + "idx", [P, U, CH], I32, ctx)
            sel = self.sb(name + "sel", [P, U, CH, W], F32, ctx)
            p_s = [self.ps(f"{name}p{n}", [P, 512], ctx) for n in range(2)]
            s = {k: self.sem(name + k, ctx) for k in ("idx", "turn", "sel0", "sel", "used", "added")}
            landed = self.landed[0:U]
            s["rows"] = landed
            acc = self.acc[:, 0:NP]
            self.clear(P, NP, [self.den[0:1, :]] if weighted else [])

            def body():
                with nc.Block() as block:
                    @block.gpsimd
                    def _(g):
                        pipeline(g, U, [(0, self.gather(g, U, table, D, rows, idx, s))])

                    @block.scalar
                    def _(a):
                        pipeline(a, U, [(0, self.indices(U, idx, s))])

                    @block.tensor
                    def _(t):
                        def step(k, slot, turn):
                            t.wait_ge(s["sel"], k + 1)
                            wait(t, s["added"], k - 1)
                            t.wait_ge(landed[slot], (turn + 1) * 16 * CH)
                            p = p_s[slot % 2]
                            for q in range(CH):
                                last = nc.tensor.matmul(p[:, 0:W], rows[:, slot, q, :], sel[:, slot, q, :],
                                                        start=(q == 0), stop=(q == CH - 1))
                            if weighted:
                                for q in range(CH):
                                    last = nc.tensor.matmul(p[0:1, W:2 * W], self.ones[:, 0:1], sel[:, slot, q, :],
                                                            start=(q == 0), stop=(q == CH - 1))
                            last.then_inc(s["used"], 1)
                        pipeline(t, U, [(0, step)])

                    @block.vector
                    def _(v):
                        def select(k, slot, turn):
                            wait(v, s["used"], k - U + 1)
                            a, b = self.onehot(k)
                            if not weighted:
                                v.tensor_tensor(sel[:, slot, :, :], a, b, ALU.is_equal).then_inc(s["sel"], 1)
                                return
                            v.tensor_tensor(sel[:, slot, :, :], a, b, ALU.is_equal).then_inc(s["sel0"], 1)
                            v.wait_ge(s["sel0"], k + 1)
                            w = self.w_t[:, bass.ds(k, 1), :].rearrange("p a q -> p (a q)").unsqueeze(2).to_broadcast([P, CH, W])
                            v.tensor_tensor(sel[:, slot, :, :], sel[:, slot, :, :], w, ALU.mult).then_inc(s["sel"], 1)

                        def add(k, slot, turn):
                            base = self.window(v, k)
                            v.wait_ge(s["used"], k + 1)
                            wait(v, s["added"], k)
                            at = bass.ds(base, W)
                            if weighted:
                                v.tensor_tensor(self.den[0:1, at], self.den[0:1, at], p_s[slot % 2][0:1, W:2 * W], ALU.add)
                            v.tensor_tensor(acc[:, at], acc[:, at], p_s[slot % 2][:, 0:W], ALU.add).then_inc(s["added"], 1)
                        pipeline(v, U, [(0, select), (1, add)])
                        self.advance(v, s["added"], NG)
            self.rounds([x for k, x in s.items() if k != "rows"], body)

    def product_edges(self):
        nc = self.nc
        U = 8
        with ExitStack() as ctx:
            sb, ps, sem = self.sb, self.ps, self.sem
            rows = sb("tp_rows", [P, U, CH, D], F32, ctx)
            idx = sb("tp_idx", [P, U, CH], I32, ctx)
            sel = sb("tp_sel", [P, U, CH, W], F32, ctx)
            emb = sb("tp_emb", [2 * TERMS * NBAS, U // 2, GE], BF16, ctx)
            h0 = sb("tp_h0", [P, 2, GE], F32, ctx)
            h1 = sb("tp_h1", [P, 2, GE], F32, ctx)
            msg = sb("tp_msg", [P, 2, CH, 2 * P], F32, ctx)
            u = sb("tp_u", [P, 2, CH, MUL], F32, ctx)
            vy = sb("tp_vy", [P, 2, CH, 3, MUL], F32, ctx)
            dot = sb("tp_dot", [P, 2, CH, MUL], F32, ctx)
            p_h0 = ps("tp_p0", [P, GE], ctx)
            p_h1 = ps("tp_p1", [P, GE], ctx)
            p_w = [ps(f"tp_pw{n}", [P, CH, 2, 4 * MUL], ctx) for n in range(2)]
            p_s = [ps(f"tp_ps{n}", [P, 512], ctx) for n in range(2)]
            names = ("idx", "turn", "hid0", "hid1", "act0", "act1", "coef", "sel", "parts", "msgs", "used", "added", "summed")
            s = {k: sem("tp_" + k, ctx) for k in names}
            landed = self.landed[0:U]
            emb_in = [sem(f"tp_emb{n}", ctx) for n in range(U // 2)]
            s["rows"] = landed
            acc = self.acc[:, 0:2 * NP].rearrange("p (h n) -> p h n", h=2)
            self.clear(P, 2 * NP, [])

            def pairs(step):
                def at(k, slot, turn):
                    if slot % 2 == 0:
                        step(turn * (U // 2) + slot // 2, k, slot // 2, turn)
                return at

            def body():
                with nc.Block() as block:
                    @block.gpsimd
                    def _(g):
                        g_s = dict(s, used=s["msgs"])
                        pipeline(g, U, [(0, self.gather(g, U, self.up_d, D, rows, idx, g_s))])

                    @block.sync
                    def _(e):
                        def load(pair, k, slot, turn):
                            wait(e, s["hid0"], pair - U // 2 + 1)
                            for g in range(2):
                                row = g * TERMS * NBAS
                                for part in range(PARTS):
                                    m = sum(p == part for p, _ in MEET)
                                    e.dma_start(emb[row:row + m * NBAS, slot, :], self.emb_d[bass.ds(k + g, 1), part, :, :]
                                                .to_broadcast([m, NBAS, GE]) if m > 1 else
                                                self.emb_d[bass.ds(k + g, 1), part, :, :].rearrange("a b e -> (a b) e"))\
                                        .then_inc(emb_in[slot], 16)
                                    row += m * NBAS
                        pipeline(e, U, [(0, pairs(load))])

                    @block.tensor
                    def _(t):
                        def hidden0(pair, k, slot, turn):
                            t.wait_ge(emb_in[slot], (turn + 1) * (16 * 2 * PARTS))
                            wait(t, s["act0"], pair)
                            nc.tensor.matmul(p_h0[:, :], self.m_w0[:, :], emb[:, slot, :], start=True, stop=True).then_inc(s["hid0"], 1)

                        def hidden1(pair, k, slot, turn):
                            t.wait_ge(s["act0"], pair + 1)
                            wait(t, s["act1"], pair)
                            nc.tensor.matmul(p_h1[:, :], self.m_w1[:, :], h0[:, slot % 2, :], start=True, stop=True).then_inc(s["hid1"], 1)

                        def coefs(pair, k, slot, turn):
                            t.wait_ge(s["act1"], pair + 1)
                            wait(t, s["msgs"], k - 2)
                            p = p_w[slot % 2]
                            for q in range(0, CH, 2):
                                nc.tensor.matmul(p[:, q:q + 2, :, :].rearrange("p q g n -> p (q g n)"), self.ones_h[:, :],
                                                 self.m_b2[:, :, :].rearrange("p q n -> p (q n)"), start=True, stop=False)
                            for q in range(CH):
                                last = nc.tensor.matmul(p[:, q, :, :].rearrange("p g n -> p (g n)"),
                                                        h1[:, slot % 2, q * P:(q + 1) * P],
                                                        self.m_w2[:, :, :].rearrange("p g n -> p (g n)"), start=False, stop=(q % 2 == 1))
                            last.then_inc(s["coef"], 1)

                        def total(k, slot, turn):
                            t.wait_ge(s["msgs"], k + 1)
                            wait(t, s["added"], k - 1)
                            for h in range(2):
                                for q in range(CH):
                                    last = nc.tensor.matmul(p_s[slot % 2][:, h * W:(h + 1) * W],
                                                            msg[:, slot % 2, q, h * P:(h + 1) * P], sel[:, slot, q, :],
                                                            start=(q == 0), stop=(q == CH - 1))
                            last.then_inc(s["summed"], 1)
                        pipeline(t, U, [(0, pairs(hidden0)), (1, pairs(hidden1)), (2, pairs(coefs)), (4, total)])

                    @block.scalar
                    def _(a):
                        def silu0(pair, k, slot, turn):
                            a.wait_ge(s["hid0"], pair + 1)
                            wait(a, s["hid1"], pair - 1)
                            nc.scalar.activation(h0[:, slot % 2, :], p_h0[:, :], ACT.Silu, bias=self.m_b0[:, 0:1]).then_inc(s["act0"], 1)

                        def silu1(pair, k, slot, turn):
                            a.wait_ge(s["hid1"], pair + 1)
                            wait(a, s["coef"], pair - 1)
                            nc.scalar.activation(h1[:, slot % 2, :], p_h1[:, :], ACT.Silu, bias=self.m_b1[:, 0:1]).then_inc(s["act1"], 1)
                        pipeline(a, U, [(0, self.indices(U, idx, dict(s, used=s["msgs"]))), (0, pairs(silu0)), (1, pairs(silu1))])

                    @block.vector
                    def _(v):
                        def select(k, slot, turn):
                            wait(v, s["summed"], k - U + 1)
                            a, b = self.onehot(k)
                            v.tensor_tensor(sel[:, slot, :, :], a, b, ALU.is_equal).then_inc(s["sel"], 1)

                        def messages(k, slot, turn):
                            h = slot % 2
                            v.wait_ge(landed[slot], (turn + 1) * 16 * CH)
                            v.wait_ge(s["coef"], turn * (U // 2) + slot // 2 + 1)
                            wait(v, s["summed"], k - 1)
                            v.wait_ge(s["sel"], k + 1)
                            p = p_w[slot // 2 % 2][:, :, h, :]
                            ss, vv = rows[:, slot, :, 0:MUL], rows[:, slot, :, MUL:].rearrange("p q (c m) -> p q c m", c=3)
                            y = self.dir_t[:, bass.ds(k, 1), :, :].rearrange("p a q c -> p (a q) c").unsqueeze(3)\
                                .to_broadcast([P, CH, 3, MUL])
                            v.tensor_tensor(msg[:, h, :, 0:MUL], p[:, :, 0:MUL], ss, ALU.mult)
                            v.tensor_tensor(u[:, h, :, :], p[:, :, MUL:2 * MUL], ss, ALU.mult).then_inc(s["parts"], 1)
                            v.tensor_tensor(vy[:, h, :, :, :], vv, y, ALU.mult).then_inc(s["parts"], 1)
                            cols = {0: 3 * MUL, 1: 5 * MUL, 2: 7 * MUL}
                            for c in range(3):
                                v.tensor_tensor(msg[:, h, :, cols[c]:cols[c] + MUL], p[:, :, 2 * MUL:3 * MUL],
                                                vv[:, :, c, :], ALU.mult)
                            v.wait_ge(s["parts"], 4 * k + 2)
                            v.tensor_tensor(dot[:, h, :, :], vy[:, h, :, 0, :], vy[:, h, :, 1, :], ALU.add).then_inc(s["parts"], 1)
                            for c in range(3):
                                v.tensor_tensor(msg[:, h, :, cols[c] - MUL:cols[c]], u[:, h, :, :], y[:, :, c, :], ALU.mult)
                            v.wait_ge(s["parts"], 4 * k + 3)
                            v.tensor_tensor(dot[:, h, :, :], dot[:, h, :, :], vy[:, h, :, 2, :], ALU.add).then_inc(s["parts"], 1)
                            v.wait_ge(s["parts"], 4 * k + 4)
                            v.tensor_tensor(msg[:, h, :, MUL:2 * MUL], p[:, :, 3 * MUL:4 * MUL], dot[:, h, :, :], ALU.mult).then_inc(s["msgs"], 1)

                        def add(k, slot, turn):
                            base = self.window(v, k)
                            v.wait_ge(s["summed"], k + 1)
                            wait(v, s["added"], k)
                            at = bass.ds(base, W)
                            v.tensor_tensor(acc[:, :, at], acc[:, :, at],
                                            p_s[slot % 2][:, 0:2 * W].rearrange("p (h n) -> p h n", h=2), ALU.add).then_inc(s["added"], 1)
                        pipeline(v, U, [(0, select), (1, messages), (2, add)])
                        self.advance(v, s["added"], NG)
            self.rounds([x for k, x in s.items() if k != "rows"] + emb_in, body)

    def attend_edges(self, l, table, dim):
        nc = self.nc
        U = 8
        width = dim + SCW
        sc = dim + SC
        with ExitStack() as ctx:
            sb, ps, sem = self.sb, self.ps, self.sem
            n = f"at{l}_"
            rows = sb(n + "rows", [P, U, CH, width], F32, ctx)
            idx = sb(n + "idx", [P, U, CH], I32, ctx)
            dst_b = sb(n + "dst_b", [P, 4, GE], F32, ctx)
            node_w = sb(n + "node_w", [W, U, SCP // 2], F32, ctx)
            hot_t = sb(n + "hot_t", [P, U, GE], BF16, ctx)
            mask = sb(n + "mask", [P, 2, GE], F32, ctx)
            cand = sb(n + "cand", [P, 2, GE], F32, ctx)
            best = sb(n + "best", [P, 2, 2], F32, ctx)
            top_w = sb(n + "top_w", [2, 2, 2, W], F32, ctx)
            rest = sb(n + "rest", [W, 2, HEADS], F32, ctx)
            look = sb(n + "look", [P, 2, CH, SC], F32, ctx)
            zz = sb(n + "zz", [P, 2, 2, CH, HEADS], F32, ctx)
            zl = sb(n + "zl", [P, 2, 2, CH, HEADS], F32, ctx)
            dz = sb(n + "dz", [P, 2, CH, HEADS], F32, ctx)
            prob = sb(n + "prob", [P, 4, CH, HEADS], F32, ctx)
            sel = sb(n + "sel", [P, 4, CH, W], F32, ctx)
            psel = sb(n + "psel", [P, 2, CH, HEADS, W], F32, ctx)
            p_b = [ps(f"{n}pb{b}", [P, GE], ctx) for b in range(2)]
            p_e = ps(n + "pe", [SCP, GE], ctx, BF16)
            esr = sb(n + "esr", [P, 2, GE], BF16, ctx)
            p_m = ps(n + "pm", [2, P], ctx)
            p_l = ps(n + "pl", [P, CH, PARTS, SC], ctx)
            p_s = [ps(f"{n}ps{a}", [P, 512], ctx) for a in range(2)]
            turned_best = p_m[:, :]
            p_w = ps(n + "pw", [W, 4], ctx)
            names = ("idx", "turn", "spread", "hot", "mask", "cand", "bestt", "merged", "topw", "topt",
                     "part", "nodew", "looked", "look", "z", "dz", "prob", "sel", "psel_v", "psel_a", "used", "added", "est", "esr", "go_v", "go_t")
            s = {k: sem(n + k, ctx) for k in names}
            landed = self.landed[0:U]
            dst_in = [sem(f"{n}dst{a}", ctx) for a in range(4)]
            sc_in = [sem(f"{n}sc{a}", ctx) for a in range(U)]
            s["rows"] = landed
            acc = self.acc[:, :].rearrange("p (h n) -> p h n", h=HEADS)
            VQ = 2

            def body():
                with nc.Block() as block:
                    @block.gpsimd
                    def _(g):
                        pipeline(g, U, [(0, self.gather(g, U, table[0:N, :], width, rows, idx, s))])

                    @block.sync
                    def _(e):
                        def load(k, slot, turn):
                            b = slot % 4
                            wait(e, s["hot"], k - 3)
                            e.dma_start(dst_b[:, b, :], self.dst_d[bass.ds(k, 1), :].to_broadcast([P, GE])).then_inc(dst_in[b], 16)
                            wait(e, s["looked"], k - U + 1)
                            base = e.value_load(self.base_now[0:1, bass.ds(k, 1)], min_val=0, max_val=NP - W)
                            e.dma_start(node_w[:, slot, :], table[bass.ds(base, W), sc:width]).then_inc(sc_in[slot], 16)
                        pipeline(e, U, [(0, load)])

                    @block.tensor
                    def _(t):
                        def turn_es(k, slot, turn):
                            t.wait_ge(landed[slot], (turn + 1) * 16 * CH)
                            wait(t, s["esr"], k)
                            for q in range(CH):
                                last = nc.tensor.transpose(p_e[:, q * P:(q + 1) * P],
                                                           rows[:, slot, q, sc:width].bitcast(BF16), self.ident_h[:, :])
                            last.then_inc(s["est"], 1)

                        def spread(k, slot, turn):
                            t.wait_ge(s["esr"], k + 1)
                            wait(t, s["cand"], 2 * k)
                            for b in range(2):
                                last = nc.tensor.matmul(p_b[b][:, :], self.pick[:, b, :], esr[:, slot % 2, :], start=True, stop=True)
                            last.then_inc(s["spread"], 1)

                        def turn_best(k, slot, turn):
                            t.wait_ge(s["cand"], 2 * k + 2)
                            wait(t, s["merged"], k)
                            nc.tensor.transpose(turned_best, best[:, slot % 2, :], self.ident[:, :]).then_inc(s["bestt"], 1)

                        def turn_top(k, slot, turn):
                            t.wait_ge(s["topw"], k + 1)
                            wait(t, s["nodew"], k)
                            t.sem_inc(s["go_t"], 1)
                            for h in range(2):
                                last = nc.tensor.transpose(p_w[:, 2 * h:2 * h + 2], top_w[:, slot % 2, h, :], self.ident[0:2, 0:2])
                            last.then_inc(s["topt"], 1)

                        def lookup(k, slot, turn):
                            t.wait_ge(s["nodew"], k + 1)
                            wait(t, s["look"], k)
                            for q in range(CH):
                                last = nc.tensor.matmul(p_l[:, q, :, :].rearrange("p a o -> p (a o)"),
                                                        hot_t[0:W, slot, q * P:(q + 1) * P],
                                                        node_w[:, slot, :].bitcast(BF16), start=True, stop=True)
                            last.then_inc(s["looked"], 1)

                        def total(k, slot, turn):
                            t.wait_ge(s["psel_v"], k + 1)
                            t.wait_ge(s["psel_a"], k + 1)
                            wait(t, s["added"], k - 1)
                            p = p_s[slot % 2]
                            for q in range(CH):
                                nc.tensor.matmul(p[0:dim, 0:HEADS * W], rows[:, slot, q, 0:dim],
                                                 psel[:, slot % 2, q, :, :].rearrange("p h n -> p (h n)"),
                                                 start=(q == 0), stop=(q == CH - 1))
                            for q in range(CH):
                                last = nc.tensor.matmul(p[0:HEADS, HEADS * W:(HEADS + 1) * W], prob[:, slot % 4, q, :],
                                                        sel[:, slot % 4, q, :], start=(q == 0), stop=(q == CH - 1))
                            last.then_inc(s["used"], 1)
                        pipeline(t, U, [(1, spread), (3, turn_top), (6, total), (0, turn_es), (3, lookup), (1, turn_best)])

                    @block.scalar
                    def _(a):
                        def es_rows(k, slot, turn):
                            a.wait_ge(s["est"], k + 1)
                            wait(a, s["spread"], k - 1)
                            nc.scalar.activation(esr[0:SCP, slot % 2, :], p_e[:, :], ACT.Copy).then_inc(s["esr"], 1)

                        def masks(k, slot, turn):
                            a.wait_ge(s["hot"], k + 1)
                            wait(a, s["cand"], 2 * (k - 1))
                            nc.scalar.activation(mask[:, slot % 2, :], hot_t[:, slot, :], ACT.Copy,
                                                 scale=BIG, bias=-BIG).then_inc(s["mask"], 1)

                        def weigh(k, slot, turn):
                            a.wait_ge(s["dz"], k + 1)
                            wait(a, s["used"], k - 3)
                            nc.scalar.activation(prob[:, slot % 4, :, :], dz[:, slot % 2, :, :], ACT.Exp).then_inc(s["prob"], 1)

                        def weigh_rest(k, slot, turn):
                            a.wait_ge(s["prob"], k + 1)
                            a.wait_ge(s["sel"], k + 1)
                            wait(a, s["used"], k - 1)
                            for q in range(VQ, CH):
                                for o in range(HEADS):
                                    last = nc.scalar.activation(psel[:, slot % 2, q, o, :], sel[:, slot % 4, q, :], ACT.Copy,
                                                                scale=prob[:, slot % 4, q, o:o + 1])
                            last.then_inc(s["psel_a"], 1)
                        pipeline(a, U, [(0, self.indices(U, idx, s)), (6, weigh_rest), (1, masks), (5, weigh), (1, es_rows)])

                    @block.vector
                    def _(v):
                        def hot(k, slot, turn):
                            b = slot % 4
                            v.wait_ge(dst_in[b], (2 * turn + slot // 4 + 1) * 16)
                            wait(v, s["looked"], k - U + 1)
                            wait(v, s["mask"], k - U + 1)
                            v.tensor_scalar(hot_t[:, slot, :], dst_b[:, b, :], self.node_now[:, 0:1], None, ALU.is_equal).then_inc(s["hot"], 1)

                        def largest(b):
                            def step(k, slot, turn):
                                if b == 0:
                                    v.wait_ge(s["mask"], k + 1)
                                    v.wait_ge(s["spread"], k + 1)
                                    wait(v, s["bestt"], k - 1)
                                    wait(v, s["cand"], 2 * k)
                                v.sem_inc(s["go_v"], 1)
                                v.tensor_tensor_reduce(out=cand[:, b, :], in0=p_b[b][:, :], in1=mask[:, slot % 2, :],
                                                       scale=1.0, scalar=-BIG, op0=ALU.add, op1=ALU.max,
                                                       accum_out=best[:, slot % 2, b:b + 1]).then_inc(s["cand"], 1)
                            return step

                        first = [v.alloc_register(f"{n}first{a}") for a in range(U)]

                        def place(k, slot, turn):
                            v.reg_load(first[slot], self.base_now[0:1, bass.ds(k, 1)])

                        def merge(k, slot, turn):
                            base = v.snap(first[slot], min_val=0, max_val=NP - W)
                            v.wait_ge(s["bestt"], k + 1)
                            wait(v, s["merged"], k)
                            at = bass.ds(base, W)
                            v.tensor_tensor(self.top[:, :, at], self.top[:, :, at],
                                            turned_best.rearrange("b (h n) -> b h n", h=2)[:, :, 0:W], ALU.max).then_inc(s["merged"], 1)

                        def take_top(k, slot, turn):
                            base = v.snap(first[slot], min_val=0, max_val=NP - W)
                            if isinstance(k, int) and k == NG - 1:
                                v.wait_ge(s["merged"], NG)
                            else:
                                v.wait_ge(s["merged"], k + 2)
                            wait(v, s["topt"], k - 1)
                            v.tensor_copy(top_w[:, slot % 2, :, :], self.top[:, :, bass.ds(base, W)]).then_inc(s["topw"], 1)

                        def part(n):
                            def step(k, slot, turn):
                                left = rest[:, slot % 2, :]
                                parts = node_w[:, slot, :].bitcast(BF16)
                                if n == 0:
                                    v.wait_ge(sc_in[slot], (turn + 1) * 16)
                                    v.wait_ge(s["topt"], k + 1)
                                    v.tensor_copy(parts[:, 0:HEADS], p_w[:, :]).then_inc(s["part"], 1)
                                    return
                                v.wait_ge(s["part"], 3 * k + n)
                                if n == 1:
                                    v.tensor_tensor(left, p_w[:, :], parts[:, 0:HEADS], ALU.subtract).then_inc(s["part"], 1)
                                elif n == 2:
                                    v.tensor_copy(parts[:, SC:SC + HEADS], left).then_inc(s["part"], 1)
                                else:
                                    v.tensor_tensor(parts[:, 2 * SC:2 * SC + HEADS], left, parts[:, SC:SC + HEADS],
                                                    ALU.subtract).then_inc(s["nodew"], 1)
                            return step

                        def score(n):
                            def step(k, slot, turn):
                                h = slot % 2
                                e, e_top, ed = zz[:, h, 0, :, :], zz[:, h, 1, :, :], look[:, h, :, HEADS:SC]
                                flat = [x[:, h, :, :, :].rearrange("p a q o -> p (a q o)") for x in (zz, zl)]
                                if n == 0:
                                    v.wait_ge(s["looked"], k + 1)
                                    v.tensor_reduce(look[:, h, :, :], p_l[:, :, :, :].rearrange("p q a o -> p q o a"),
                                                    AX.X, ALU.add).then_inc(s["look"], 1)
                                elif n == 1:
                                    v.wait_ge(s["look"], k + 1)
                                    wait(v, s["dz"], k)
                                    v.tensor_tensor(e, ed, rows[:, slot, :, dim:dim + HEADS], ALU.add)
                                    v.tensor_tensor(e_top, ed, look[:, h, :, 0:HEADS], ALU.add).then_inc(s["z"], 1)
                                elif n == 2:
                                    v.wait_ge(s["z"], 3 * k + 1)
                                    v.scalar_tensor_tensor(flat[1], flat[0], 0.2, flat[0], ALU.mult, ALU.max).then_inc(s["z"], 1)
                                elif n == 3:
                                    v.wait_ge(s["z"], 3 * k + 2)
                                    v.tensor_tensor(e, zl[:, h, 0, :, :], zl[:, h, 1, :, :], ALU.min).then_inc(s["z"], 1)
                                else:
                                    v.wait_ge(s["z"], 3 * k + 3)
                                    wait(v, s["prob"], k - 1)
                                    v.tensor_tensor(dz[:, h, :, :], e, zl[:, h, 1, :, :], ALU.subtract).then_inc(s["dz"], 1)
                            return step

                        def select(k, slot, turn):
                            wait(v, s["used"], k - 3)
                            a, b = self.onehot(k)
                            v.tensor_tensor(sel[:, slot % 4, :, :], a, b, ALU.is_equal).then_inc(s["sel"], 1)

                        def weigh(q):
                            def step(k, slot, turn):
                                if q == 0:
                                    v.wait_ge(s["prob"], k + 1)
                                    v.wait_ge(s["sel"], k + 1)
                                    wait(v, s["used"], k - 1)
                                last = v.tensor_tensor(psel[:, slot % 2, q, :, :],
                                                       sel[:, slot % 4, q, :].unsqueeze(1).to_broadcast([P, HEADS, W]),
                                                       prob[:, slot % 4, q, :].unsqueeze(2).to_broadcast([P, HEADS, W]), ALU.mult)
                                if q == VQ - 1:
                                    last.then_inc(s["psel_v"], 1)
                            return step

                        def add(k, slot, turn):
                            base = v.snap(first[slot], min_val=0, max_val=NP - W)
                            v.wait_ge(s["used"], k + 1)
                            wait(v, s["added"], k)
                            at = bass.ds(base, W)
                            p = p_s[slot % 2]
                            v.tensor_tensor(self.den[:, at], self.den[:, at], p[0:HEADS, HEADS * W:(HEADS + 1) * W], ALU.add)
                            v.tensor_tensor(acc[0:dim, :, at], acc[0:dim, :, at],
                                            p[0:dim, 0:HEADS * W].rearrange("p (h n) -> p h n", h=HEADS), ALU.add).then_inc(s["added"], 1)
                        pipeline(v, U, [(5, weigh(0)), (2, merge), (5, weigh(1)), (3, take_top), (4, score(0)), (0, hot),
                                        (4, score(1)), (3, part(0)), (4, select), (3, part(1)), (4, score(2)), (3, part(2)),
                                        (4, score(3)), (1, largest(0)), (3, part(3)), (4, score(4)), (1, largest(1)),
                                        (0, place), (7, add)])
                        self.advance(v, s["added"], NG)
            with nc.Fori(0, self.is_general + 1):
                self.clear(dim, HEADS * NP, [self.den[:, :], esr[:, :, :]])
                self.rounds([x for k, x in s.items() if k != "rows"] + dst_in + sc_in, body)

    def norm(self, v, a_sem, then, x, width, tmp, st, root):
        nb = x.shape[0]
        full = [nb, JB, width]
        then(v.tensor_reduce(st[0:nb, 0, :], x, AX.X, ALU.add))
        then(v.tensor_scalar(st[0:nb, 0, :], st[0:nb, 0, :], 1.0 / width, None, ALU.mult))
        then(v.tensor_tensor(x, x, st[0:nb, 0, :].unsqueeze(2).to_broadcast(full), ALU.subtract))
        then(v.tensor_tensor(tmp, x, x, ALU.mult))
        then(v.tensor_reduce(st[0:nb, 1, :], tmp, AX.X, ALU.add))
        v.tensor_scalar(st[0:nb, 1, :], st[0:nb, 1, :], 1.0 / width, LN_EPS, ALU.mult, ALU.add).then_inc(a_sem, 1)
        root()
        then(v.reciprocal(st[0:nb, 1, :], st[0:nb, 1, :]))
        then(v.tensor_tensor(x, x, st[0:nb, 1, :].unsqueeze(2).to_broadcast(full), ALU.mult))

    def split(self, v, sem, start, tab, at, rest):
        then = Chain(v, sem, start)
        parts = tab[:, :, at + SC:at + SCW].bitcast(BF16)
        left = tab[:, :, at:at + SC]
        for k in range(PARTS):
            part = parts[:, :, k * SC:(k + 1) * SC]
            then(v.tensor_copy(part, left))
            if k < PARTS - 1:
                then(v.tensor_tensor(rest[:, k, :, :], left, part, ALU.subtract))
                left = rest[:, k, :, :]

    def all_sent(self, e, sems):
        for k, sem in enumerate(sems):
            e.wait_ge(sem, 16 * len(range(k, NT, len(sems))))

    def node_rows(self, dram, t, width):
        return dram[t * NS:(t + 1) * NS, :].rearrange("(j p) f -> p j f", j=JB)

    def node_layer(self, n, kind, x_in):
        nc = self.nc
        product = kind == "product"
        with ExitStack() as ctx:
            sb, ps, sem = self.sb, self.ps, self.sem
            xs = sb(n + "xs", [NB, 3, JB, D], F32, ctx)
            y = sb(n + "y", [NB, 3, JB, D], F32, ctx)
            tmp = sb(n + "tmp", [NB, JB, D], F32, ctx)
            st = sb(n + "st", [P, 2, JB], F32, ctx)
            xt = sb(n + "xt", [P, JB, P], F32, ctx)
            yt = sb(n + "yt", [P, JB, P], F32, ctx)
            tab = sb(n + "tab", [NB, 2, JB, D + SCW], F32, ctx)
            rest = sb(n + "rest", [NB, 2, JB, SC], F32, ctx)
            p_x = ps(n + "px", [P, 8, P], ctx)
            p_y = ps(n + "py", [P, 8, P], ctx)
            p_z = ps(n + "pz", [P, 8, P], ctx)
            p_o = ps(n + "po", [P, 8, P], ctx)
            names = ("turned", "xt", "lin", "var", "rooted", "step", "turned2", "xt2", "tabbed", "scores", "along",
                     "tabd", "split")
            s = {k: sem(n + k, ctx) for k in names}
            s["xin"] = [sem(f"{n}xin{k}", ctx) for k in range(3)]
            s["ysent"] = [sem(f"{n}ysent{k}", ctx) for k in range(3)]
            s["tsent"] = [sem(f"{n}tsent{k}", ctx) for k in range(2)]
            LINKS = 8
            with nc.Block() as block:
                @block.sync
                def _(e):
                    def load(t):
                        wait(e, s["step"], (t - 3) * LINKS + 1)
                        e.dma_start(xs[:, t % 3, :, :], self.node_rows(x_in, t, D)).then_inc(s["xin"][t % 3], 16)

                    def store(t):
                        e.wait_ge(s["step"], (t + 1) * LINKS)
                        e.dma_start(self.node_rows(self.x2_d if product else self.x1_d, t, D), y[:, t % 3, :, :])\
                            .then_inc(s["ysent"][t % 3], 16)
                        if product:
                            e.wait_ge(s["split"], (t + 1) * SPLIT)
                            e.dma_start(self.node_rows(self.t_d[0][0:N, :], t, D + SCW), tab[:, t % 2, :, :]).then_inc(s["tsent"][t % 2], 16)
                        else:
                            e.wait_ge(s["tabd"], t + 1)
                            e.dma_start(self.node_rows(self.up_d, t, D), tab[:, t % 2, :, 0:D]).then_inc(s["tsent"][t % 2], 16)
                    steps([(0, load), (2, store)])
                    self.all_sent(e, s["ysent"])
                    self.all_sent(e, s["tsent"])

                @block.scalar
                def _(a):
                    def turn_x(t):
                        a.wait_ge(s["turned"], t + 1)
                        wait(a, s["lin"], t)
                        nc.scalar.activation(xt[:, :, 0:NB], p_x[:, 0:JB, 0:NB], ACT.Copy).then_inc(s["xt"], 1)

                    def root(t):
                        a.wait_ge(s["var"], t + 1)
                        nc.scalar.activation(st[0:NB, 1, :], st[0:NB, 1, :], ACT.Sqrt).then_inc(s["rooted"], 1)

                    def turn_y(t):
                        a.wait_ge(s["turned2"], t + 1)
                        wait(a, s["tabbed"], t)
                        nc.scalar.activation(yt[:, :, 0:NB], p_z[:, 0:JB, 0:NB], ACT.Copy).then_inc(s["xt2"], 1)

                    def table(t):
                        wait(a, s["tsent"][t % 2], t // 2 * 16)
                        a.wait_ge(s["tabbed"], t + 1)
                        row = tab[:, t % 2, :, :]
                        if product:
                            nc.scalar.activation(row[:, :, D:D + SC], p_o[0:NB, 0:JB, 0:SC], ACT.Copy).then_inc(s["scores"], 1)
                            nc.scalar.activation(row[:, :, 0:D], y[:, t % 3, :, :], ACT.Copy)
                            a.wait_ge(s["along"], t + 1)
                            for hh, p in enumerate((p_x, p_z)):
                                last = nc.scalar.activation(self.top[:, hh, t * NS:(t + 1) * NS].rearrange("b (j p) -> b j p", j=JB),
                                                            p[0:2, 0:JB, 0:NB], ACT.Copy)
                        else:
                            last = nc.scalar.activation(row[:, :, 0:D], p_o[0:NB, 0:JB, :], ACT.Copy)
                        last.then_inc(s["tabd"], 1)
                    steps(([] if product else [(0, turn_x)]) + [(1, turn_y), (0, root), (1, table)])

                @block.tensor
                def _(te):
                    def front(t):
                        sums = self.acc[:, 0:2 * NP].rearrange("p (h n) -> p h n", h=2)
                        te.wait_ge(s["xin"][t % 3], (t // 3 + 1) * 16)
                        if not product:
                            for j in range(JB):
                                last = nc.tensor.transpose(p_x[:, j, 0:NB], xs[:, t % 3, j, :], self.ident[0:NB, 0:NB])
                            last.then_inc(s["turned"], 1)
                            te.wait_ge(s["xt"], t + 1)
                        wait(te, s["step"], (t - 1) * LINKS + 1)
                        for j in range(JB):
                            at = slice((t * JB + j) * NB, (t * JB + j + 1) * NB)
                            if product:
                                for h in range(2):
                                    last = nc.tensor.matmul(p_y[0:NB, j, :], sums[:, h, at], self.outw[:, h, :],
                                                            start=(h == 0), stop=(h == 1))
                            else:
                                nc.tensor.matmul(p_y[0:NB, j, :], self.ones_h[0:PARTS, 0:NB], self.l0_b[:, 0, :], start=True, stop=False)
                                nc.tensor.matmul(p_y[0:NB, j, :], xt[:, j, 0:NB], self.l0_w[:, 0, :], start=False, stop=False)
                                last = nc.tensor.matmul(p_y[0:NB, j, :], sums[:, 0, at], self.l0_w[:, 1, :], start=False, stop=True)
                        last.then_inc(s["lin"], 1)

                    def back(t):
                        te.wait_ge(s["step"], (t + 1) * LINKS)
                        wait(te, s["tabd"], t)
                        for j in range(JB):
                            last = nc.tensor.transpose(p_z[:, j, 0:NB], y[:, t % 3, j, :], self.ident[0:NB, 0:NB])
                        last.then_inc(s["turned2"], 1)
                        te.wait_ge(s["xt2"], t + 1)
                        w = self.g_a[0][:, :] if product else self.up[:, :]
                        for j in range(JB):
                            last = nc.tensor.matmul(p_o[0:NB, j, 0:w.shape[1]], yt[:, j, 0:NB], w, start=True, stop=True)
                        last.then_inc(s["tabbed"], 1)
                        if product:
                            te.wait_ge(s["scores"], t + 1)
                            for hh, p in enumerate((p_x, p_z)):
                                at = D + 2 * hh
                                for j in range(JB):
                                    last = nc.tensor.transpose(p[0:2, j, 0:NB], tab[:, t % 2, j, at:at + 2], self.ident[0:NB, 0:NB])
                            last.then_inc(s["along"], 1)
                    steps([(0, front), (1, back)])

                @block.vector
                def _(v):
                    def rows(t):
                        then = Chain(v, s["step"], t * LINKS)
                        now = y[:, t % 3, :, :]
                        wait(v, s["ysent"][t % 3], t // 3 * 16)
                        wait(v, s["tabd"], t - 2)
                        v.wait_ge(s["lin"], t + 1)
                        if product:
                            then(v.tensor_tensor(now, p_y[0:NB, 0:JB, :], xs[:, t % 3, :, :], ALU.add))
                        else:
                            then(v.scalar_tensor_tensor(now.rearrange("p j f -> p (j f)"),
                                                        p_y[0:NB, 0:JB, :].rearrange("p j f -> p (j f)"), 0.0,
                                                        xs[:, t % 3, :, :].rearrange("p j f -> p (j f)"), ALU.max, ALU.add))
                        self.norm(v, s["var"], then, now, D, tmp[:, :, :], st, lambda: v.wait_ge(s["rooted"], t + 1))
                        assert then.n == LINKS, then.n

                    def parts(t):
                        v.wait_ge(s["tabd"], t + 1)
                        self.split(v, s["split"], t * SPLIT, tab[:, t % 2, :, :], D, rest)
                    steps([(0, rows)] + ([(1, parts)] if product else []))
            self.zero([x for v in s.values() for x in (v if isinstance(v, list) else [v])])

    def node_attention(self, l):
        nc = self.nc
        dim, table = (D, HID)[l], self.t_d[l][0:N, :]
        n = f"na{l}_"
        with ExitStack() as ctx:
            sb, ps, sem = self.sb, self.ps, self.sem
            own = sb(n + "own", [NB, 3, JB, dim + SC], F32, ctx)
            dt_s = sb(n + "dt", [NB, 2, JB, 8], F32, ctx)
            zz = sb(n + "zz", [NB, 2, JB, HEADS], F32, ctx)
            zl = sb(n + "zl", [NB, 2, JB, HEADS], F32, ctx)
            pown = sb(n + "pown", [NB, JB, HEADS], F32, ctx)
            rd = sb(n + "rd", [NB, 2, JB, HEADS], F32, ctx)
            prod = sb(n + "prod", [NB, 2, JB, HEADS, HID], F32, ctx)
            h = sb(n + "h", [NB, 2, JB, HID], F32, ctx)
            tmp = sb(n + "tmp", [NB, JB, D], F32, ctx)
            st = sb(n + "st", [P, 2, JB], F32, ctx)
            xt = sb(n + "xt", [P, JB, P], F32, ctx)
            ht = sb(n + "ht", [HID, JB, P], F32, ctx)
            xs = sb(n + "xs", [NB, 3, JB, D], F32, ctx) if l else None
            y = sb(n + "y", [NB, 2, JB, D], F32, ctx) if l else None
            tab = sb(n + "tab", [NB, 2, JB, HID + SCW], F32, ctx)
            rest = sb(n + "rest", [NB, 2, JB, SC], F32, ctx)
            p_a = ps(n + "pa", [P, 6, HEADS * HID], ctx)
            p_b = ps(n + "pb", [P, 6, HEADS * HID], ctx)
            p_t = ps(n + "pt", [P, 8, P], ctx)
            p_dt = p_t[0:NB, 6, 0:JB * 8].rearrange("p (j o) -> p j o", o=8)
            p_sc = p_t[0:NB, 7, 0:JB * SC].rearrange("p (j o) -> p j o", o=SC)
            names = ("turned0", "xt", "lin", "own", "exped", "var", "rooted", "step", "turned",
                     "ht", "out", "scores", "along", "top0", "vary", "rootedy", "stepy", "tabd", "split", "go_t")
            s = {k: sem(n + k, ctx) for k in names}
            s["ownin"] = [sem(f"{n}ownin{k}", ctx) for k in range(3)]
            s["xin"] = [sem(f"{n}xin{k}", ctx) for k in range(3)]
            s["sent"] = [sem(f"{n}sent{k}", ctx) for k in range(2)]
            LINKS = 24
            READ = 9
            LINKSY = 8
            with nc.Block() as block:
                @block.sync
                def _(e):
                    def load(t):
                        wait(e, s["step"], (t - 2) * LINKS)
                        e.dma_start(own[:, t % 3, :, :], self.node_rows(table, t, dim + SCW)[:, :, 0:dim + SC]).then_inc(s["ownin"][t % 3], 16)
                        if l == 1:
                            wait(e, s["stepy"], (t - 2) * LINKSY)
                            e.dma_start(xs[:, t % 3, :, :], self.node_rows(self.x2_d, t, D)).then_inc(s["xin"][t % 3], 16)

                    def store(t):
                        if l == 0:
                            e.wait_ge(s["split"], (t + 1) * SPLIT)
                            e.dma_start(self.node_rows(self.t_d[1][0:N, :], t, HID + SCW), tab[:, t % 2, :, :]).then_inc(s["sent"][t % 2], 16)
                        else:
                            e.wait_ge(s["stepy"], (t + 1) * LINKSY)
                            e.dma_start(self.node_rows(self.x3_d, t, D), y[:, t % 2, :, :]).then_inc(s["sent"][t % 2], 16)
                    steps([(0, load), (2, store)])
                    self.all_sent(e, s["sent"])

                @block.scalar
                def _(a):
                    def turn_own(t):
                        a.wait_ge(s["turned0"], t + 1)
                        wait(a, s["lin"], t)
                        wait(a, s["step"], (t - 2) * LINKS + READ)
                        nc.scalar.activation(dt_s[:, t % 2, :, :], p_dt, ACT.Copy)
                        nc.scalar.activation(xt[0:dim, :, 0:NB], p_t[0:dim, 0:JB, 0:NB], ACT.Copy).then_inc(s["xt"], 1)

                    def exps(t):
                        a.wait_ge(s["own"], t + 1)
                        nc.scalar.activation(pown[:, :, :], zl[:, 0, :, :], ACT.Exp).then_inc(s["exped"], 1)

                    def root(t):
                        a.wait_ge(s["var"], t + 1)
                        nc.scalar.activation(st[0:NB, 1, :], st[0:NB, 1, :], ACT.Sqrt).then_inc(s["rooted"], 1)

                    def turn_h(t):
                        a.wait_ge(s["turned"], t + 1)
                        nc.scalar.activation(ht[:, :, 0:NB], p_t[0:HID, 0:JB, 0:NB], ACT.Copy).then_inc(s["ht"], 1)

                    def next_table(t):
                        wait(a, s["sent"][t % 2], t // 2 * 16)
                        a.wait_ge(s["out"], t + 1)
                        row = tab[:, t % 2, :, :]
                        top = self.top[:, :, t * NS:(t + 1) * NS].rearrange("b h (j p) -> b h j p", j=JB)
                        nc.scalar.activation(row[:, :, HID:HID + SC], p_sc, ACT.Copy).then_inc(s["scores"], 1)
                        nc.scalar.activation(row[:, :, 0:HID], h[:, t % 2, :, :], ACT.Copy)
                        a.wait_ge(s["along"], 2 * t + 1)
                        nc.scalar.activation(top[:, 0, :, :], p_t[0:2, 0:JB, 0:NB], ACT.Copy).then_inc(s["top0"], 1)
                        a.wait_ge(s["along"], 2 * t + 2)
                        nc.scalar.activation(top[:, 1, :, :], p_t[0:2, 0:JB, 0:NB], ACT.Copy).then_inc(s["tabd"], 1)

                    def output(t):
                        wait(a, s["sent"][t % 2], t // 2 * 16)
                        a.wait_ge(s["out"], t + 1)
                        nc.scalar.activation(y[:, t % 2, :, :], p_t[0:NB, 0:JB, 0:D], ACT.Copy).then_inc(s["tabd"], 1)

                    def root_y(t):
                        a.wait_ge(s["vary"], t + 1)
                        nc.scalar.activation(st[0:NB, 1, :], st[0:NB, 1, :], ACT.Sqrt).then_inc(s["rootedy"], 1)
                    steps([(0, turn_own), (0, exps), (1, turn_h)] + ([(1, next_table), (0, root)] if l == 0 else [(1, output), (0, root), (1, root_y)]))

                @block.tensor
                def _(te):
                    def front(t):
                        slot = own[:, t % 3, :, :]
                        te.wait_ge(s["ownin"][t % 3], (t // 3 + 1) * 16)
                        wait(te, s["tabd"], t - 1)
                        te.sem_inc(s["go_t"], 1)
                        for j in range(JB):
                            last = nc.tensor.transpose(p_t[0:dim, j, 0:NB], slot[:, j, 0:dim], self.ident[0:NB, 0:NB])
                        for j in range(JB):
                            at = slice((t * JB + j) * NB, (t * JB + j + 1) * NB)
                            nc.tensor.transpose(p_dt[:, j, 0:HEADS], self.den[:, at], self.ident[0:HEADS, 0:HEADS])
                            for hh in range(2):
                                last = nc.tensor.transpose(p_dt[:, j, 4 + 2 * hh:6 + 2 * hh], self.top[:, hh, at],
                                                           self.ident[0:2, 0:2])
                        last.then_inc(s["turned0"], 1)
                        wait(te, s["step"], (t - 1) * LINKS + READ)
                        sums = self.acc[:, :].rearrange("p (h n) -> p h n", h=HEADS)
                        for j in range(JB):
                            at = slice((t * JB + j) * NB, (t * JB + j + 1) * NB)
                            for o, hd in enumerate(HEAD_OF):
                                nc.tensor.matmul(p_a[0:NB, j, o * HID:(o + 1) * HID], sums[0:dim, o, at],
                                                 self.g_w[l][:, hd * HID:(hd + 1) * HID], start=True, stop=True)
                        te.wait_ge(s["xt"], t + 1)
                        wait(te, s["step"], (t - 1) * LINKS + READ + 1)
                        for j in range(JB):
                            last = nc.tensor.matmul(p_b[0:NB, j, :], xt[0:dim, j, 0:NB],
                                                    self.g_w[l][:, :].rearrange("d (a b k) -> d b a k", a=2, b=2),
                                                    start=True, stop=True)
                        last.then_inc(s["lin"], 1)

                    def back(t):
                        te.wait_ge(s["step"], (t + 1) * LINKS)
                        te.wait_ge(s["xt"], min(t + 2, NT))
                        wait(te, s["tabd"], t)
                        te.sem_inc(s["go_t"], 1)
                        for j in range(JB):
                            last = nc.tensor.transpose(p_t[0:HID, j, 0:NB], h[:, t % 2, j, :], self.ident[0:NB, 0:NB])
                        last.then_inc(s["turned"], 1)
                        te.wait_ge(s["ht"], t + 1)
                        if l == 1:
                            for j in range(JB):
                                nc.tensor.matmul(p_t[0:NB, j, :], self.ones_h[0:PARTS, 0:NB], self.bo[:, 0, :], start=True, stop=False)
                                last = nc.tensor.matmul(p_t[0:NB, j, :], ht[:, j, 0:NB], self.wo[:, :], start=False, stop=True)
                            last.then_inc(s["out"], 1)
                            return
                        for j in range(JB):
                            last = nc.tensor.matmul(p_sc[:, j, :], ht[:, j, 0:NB], self.g_a[1][:, :], start=True, stop=True)
                        last.then_inc(s["out"], 1)
                        te.wait_ge(s["scores"], t + 1)
                        for hh in range(2):
                            if hh == 1:
                                te.wait_ge(s["top0"], t + 1)
                            at = HID + 2 * hh
                            for j in range(JB):
                                last = nc.tensor.transpose(p_t[0:2, j, 0:NB], tab[:, t % 2, j, at:at + 2], self.ident[0:NB, 0:NB])
                            last.then_inc(s["along"], 1)
                    steps([(0, front), (1, back)])

                @block.vector
                def _(v):
                    wide = [NB, JB, HID]

                    def mean(t):
                        then = Chain(v, s["step"], t * LINKS)
                        now, slot = h[:, t % 2, :, :], own[:, t % 3, :, :]
                        v.wait_ge(s["xt"], t + 1)
                        v.wait_ge(s["ownin"][t % 3], (t // 3 + 1) * 16)
                        v.tensor_tensor(zz[:, 0, :, :], slot[:, :, dim:dim + HEADS], slot[:, :, dim + HEADS:dim + SC], ALU.add)
                        then(v.tensor_tensor(zz[:, 1, :, :], dt_s[:, t % 2, :, 4:8], slot[:, :, dim + HEADS:dim + SC], ALU.add))
                        then(v.tensor_scalar(zl[:, :, :, :], zz[:, :, :, :], 0.2, None, ALU.mult))
                        then(v.tensor_tensor(zz[:, :, :, :], zl[:, :, :, :], zz[:, :, :, :], ALU.max))
                        then(v.tensor_tensor(zz[:, 0, :, :], zz[:, 0, :, :], zz[:, 1, :, :], ALU.min))
                        v.tensor_tensor(zl[:, 0, :, :], zz[:, 0, :, :], zz[:, 1, :, :], ALU.subtract).then_inc(s["own"], 1)
                        v.wait_ge(s["exped"], t + 1)
                        then(v.tensor_tensor(rd[:, 0, :, :], dt_s[:, t % 2, :, 0:4], pown[:, :, :], ALU.add))
                        then(v.reciprocal(rd[:, 0, :, :], rd[:, 0, :, :]))
                        then(v.tensor_scalar(rd[:, 0, :, :], rd[:, 0, :, :], 1.0 / HEADS, None, ALU.mult))
                        then(v.tensor_tensor(rd[:, 1, :, :], rd[:, 0, :, :], pown[:, :, :], ALU.mult))
                        v.wait_ge(s["lin"], t + 1)
                        for k, p in enumerate((p_a, p_b)):
                            last = v.tensor_tensor(prod[:, k, :, :, :].rearrange("p j o k -> p (j o) k"),
                                                   p[0:NB, 0:JB, :].rearrange("p j (o k) -> p (j o) k", k=HID),
                                                   rd[:, k, :, :].rearrange("p j o -> p (j o)").unsqueeze(2)
                                                   .to_broadcast([NB, JB * HEADS, HID]), ALU.mult)
                            then(last)
                        assert then.n == READ + 1, then.n
                        then(v.tensor_tensor(prod[:, 0, :, :, :], prod[:, 0, :, :, :], prod[:, 1, :, :, :], ALU.add))
                        wait(v, s["turned"], t - 1)
                        if l == 0:
                            wait(v, s["tabd"], t - 1)
                        then(v.tensor_reduce(now, prod[:, 0, :, :, :].rearrange("p j o k -> p j k o"), AX.X, ALU.add))

                        def row(k):
                            return self.g_row[l][0:NB, k, :].unsqueeze(1).to_broadcast(wide)
                        then(v.tensor_tensor(now, now, row(0), ALU.add))
                        self.norm(v, s["var"], then, now, HID, tmp[:, :, 0:HID], st, lambda: v.wait_ge(s["rooted"], t + 1))
                        then(v.tensor_tensor(now, now, row(1), ALU.mult))
                        then(v.tensor_tensor(now, now, row(2), ALU.add))
                        then(v.tensor_scalar(now, now, 0.0, None, ALU.max))
                        assert then.n == LINKS - 1, then.n
                        v.sem_inc(s["step"], 1)

                    def parts(t):
                        v.wait_ge(s["tabd"], t + 1)
                        self.split(v, s["split"], t * SPLIT, tab[:, t % 2, :, :], HID, rest)

                    def residual(t):
                        then = Chain(v, s["stepy"], t * LINKSY)
                        now = y[:, t % 2, :, :]
                        v.wait_ge(s["tabd"], t + 1)
                        v.wait_ge(s["xin"][t % 3], (t // 3 + 1) * 16)
                        then(v.tensor_tensor(now, now, xs[:, t % 3, :, :], ALU.add))
                        self.norm(v, s["vary"], then, now, D, tmp[:, :, :], st, lambda: v.wait_ge(s["rootedy"], t + 1))
                        assert then.n == LINKSY, then.n
                    steps([(0, mean), (1, parts if l == 0 else residual)])
            self.zero([x for v in s.values() for x in (v if isinstance(v, list) else [v])])

    def node_last(self):
        nc = self.nc
        with ExitStack() as ctx:
            sb, ps, sem = self.sb, self.ps, self.sem
            n = "nl_"
            xs = sb(n + "xs", [NB, 3, JB, D], F32, ctx)
            y = sb(n + "y", [NB, 2, JB, D], F32, ctx)
            tmp = sb(n + "tmp", [NB, JB, D], F32, ctx)
            c = sb(n + "c", [NB, 4, JB], F32, ctx)
            st = sb(n + "st", [P, 2, JB], F32, ctx)
            p_d = [ps(f"{n}pd{k}", [P, 8, 64], ctx) for k in range(2)]
            p_y = [ps(f"{n}py{k}", [P, 8, P], ctx) for k in range(2)]
            s = {k: sem(n + k, ctx) for k in ("lin", "var", "rooted", "step", "go_t")}
            s["xin"] = [sem(f"{n}xin{k}", ctx) for k in range(3)]
            s["sent"] = [sem(f"{n}sent{k}", ctx) for k in range(2)]
            LINKS = 15
            with nc.Block() as block:
                @block.sync
                def _(e):
                    def load(t):
                        wait(e, s["step"], (t - 2) * LINKS)
                        e.dma_start(xs[:, t % 3, :, :], self.node_rows(self.x3_d, t, D)).then_inc(s["xin"][t % 3], 16)

                    def store(t):
                        e.wait_ge(s["step"], (t + 1) * LINKS)
                        e.dma_start(self.node_rows(self.out, t, D), y[:, t % 2, :, :]).then_inc(s["sent"][t % 2], 16)
                    steps([(0, load), (2, store)])
                    self.all_sent(e, s["sent"])

                @block.scalar
                def _(a):
                    def root(t):
                        a.wait_ge(s["var"], t + 1)
                        nc.scalar.activation(st[0:NB, 1, :], st[0:NB, 1, :], ACT.Sqrt).then_inc(s["rooted"], 1)
                    steps([(0, root)])

                @block.tensor
                def _(te):
                    def turn(t):
                        wait(te, s["step"], (t - 1) * LINKS)
                        te.sem_inc(s["go_t"], 1)
                        for j in range(JB):
                            at = slice((t * JB + j) * NB, (t * JB + j + 1) * NB)
                            nc.tensor.transpose(p_d[t % 2][0:NB, j, 0:1], self.den[0:1, at], self.ident[0:1, 0:1])
                        for j in range(JB):
                            at = slice((t * JB + j) * NB, (t * JB + j + 1) * NB)
                            last = nc.tensor.transpose(p_y[t % 2][0:NB, j, :], self.acc[:, at], self.ident[:, :])
                        last.then_inc(s["lin"], 1)
                    steps([(0, turn)])

                @block.vector
                def _(v):
                    def rows(t):
                        then = Chain(v, s["step"], t * LINKS)
                        now, before = y[:, t % 2, :, :], xs[:, t % 3, :, :]
                        v.wait_ge(s["lin"], t + 1)
                        full = [NB, JB, D]

                        def col(k):
                            return c[:, k, :].unsqueeze(2).to_broadcast(full)
                        then(v.tensor_scalar(c[:, 0, :], p_d[t % 2][0:NB, 0:JB, 0], 1e-8, None, ALU.max))
                        then(v.reciprocal(c[:, 1, :], c[:, 0, :]))
                        then(v.tensor_scalar(c[:, 2, :], c[:, 0, :], 1e-8, 0.3, ALU.is_gt, ALU.mult))
                        then(v.tensor_scalar(c[:, 3, :], c[:, 2, :], -1.0, 2.0, ALU.mult, ALU.add))
                        then(v.tensor_tensor(c[:, 1, :], c[:, 1, :], c[:, 2, :], ALU.mult))
                        v.wait_ge(s["xin"][t % 3], (t // 3 + 1) * 16)
                        wait(v, s["sent"][t % 2], t // 2 * 16)
                        then(v.tensor_tensor(now, p_y[t % 2][0:NB, 0:JB, :], col(1), ALU.mult))
                        then(v.tensor_tensor(tmp[:, :, :], before, col(3), ALU.mult))
                        then(v.tensor_tensor(now, now, tmp[:, :, :], ALU.add))
                        self.norm(v, s["var"], then, now, D, tmp[:, :, :], st, lambda: v.wait_ge(s["rooted"], t + 1))
                        assert then.n == LINKS, then.n
                    steps([(0, rows)])
            self.zero([x for v in s.values() for x in (v if isinstance(v, list) else [v])])

    def build(self):
        nc = self.nc
        with self.ctx:
            self.allocate()
            self.setup()
            self.is_general = nc.values_load(self.general[0:1, 0:1], min_val=0, max_val=1)
            self.sum_edges("e0_", self.i["x"], False)
            self.node_layer("n0_", "sum", self.i["x"])
            self.product_edges()
            self.node_layer("n1_", "product", self.x1_d)
            self.attend_edges(0, self.t_d[0], D)
            self.node_attention(0)
            self.attend_edges(1, self.t_d[1], HID)
            self.node_attention(1)
            self.sum_edges("e3_", self.x3_d, True)
            self.node_last()


def graph_layers(nc, names, aps, out):
    Program(nc, dict(zip(names, aps)), out).build()


_INS = ["x", "src", "dst", "edge_attr_3", "edge_weight", "L0_gnn_W", "L0_gnn_b", "L1_gnn_W_up0", "L1_gnn_W_up1",
        "L1_gnn_mlp_w0", "L1_gnn_mlp_b0", "L1_gnn_mlp_w1", "L1_gnn_mlp_b1", "L1_gnn_mlp_w2", "L1_gnn_mlp_b2",
        "L1_gnn_W_out0", "L1_gnn_W_out1", "L2_gnn_W1", "L2_gnn_asrc1", "L2_gnn_adst1", "L2_gnn_b1", "L2_gnn_g1",
        "L2_gnn_be1", "L2_gnn_W2", "L2_gnn_asrc2", "L2_gnn_adst2", "L2_gnn_b2", "L2_gnn_g2", "L2_gnn_be2",
        "L2_gnn_Wo", "L2_gnn_bo"]


def kernel(**inputs):
    import numpy as _np
    import concourse.bacc as _bacc
    from concourse import mybir as _mybir
    from concourse.bass_utils import run_bass_kernel_spmd as _run

    nc = _bacc.Bacc("TRN2", target_bir_lowering=False, num_devices=1)
    arrays, args = {}, []
    for name in _INS:
        a = _np.ascontiguousarray(inputs[name])
        arrays[f"in_{name}_dram"] = a
        args.append(nc.dram_tensor(f"in_{name}_dram", a.shape, _mybir.dt.from_np(a.dtype), kind="ExternalInput").ap())
    out = nc.dram_tensor("out_0_dram", (3125, 128), _mybir.dt.float32, kind="ExternalOutput").ap()
    graph_layers(nc, _INS, args, out)
    r = _run(nc, [arrays], core_ids=[0])
    return r.results[0]["out_0_dram"]
```
